# Optimizing a Trainium2 kernel written in Bass

```python
import numpy as np
import jax
import jax.numpy as jnp

def _softmax(x, axis=-1):
    return jax.nn.softmax(x, axis=axis)

def _gelu(x):
    return jax.nn.gelu(x, approximate=True)

def _silu(x):
    return jax.nn.silu(x)

def _sigmoid(x):
    return jax.nn.sigmoid(x)

def _layernorm(x, axis=-1, eps=1e-05):
    m = jnp.mean(x, axis=axis, keepdims=True)
    v = jnp.var(x, axis=axis, keepdims=True)
    return (x - m) / jnp.sqrt(v + eps)

def _scatter_add(tgt, idx, src, axis=0):
    return tgt.at[idx].add(src)

def _segment_sum(src, seg, n):
    return jax.ops.segment_sum(src, seg, n)
kernel_name = 'mk_sandwich_d2_jaxref_r8_ab102d'

def setup_inputs(seed: int=0):
    np.random.seed(seed)
    _w = jnp.asarray

    def _L0_attn_setup():
        import jax, jax.numpy as jnp
        import numpy as np
        EPS = 1e-05

        def _layer_norm(x, w, b):
            mu = jnp.mean(x, axis=-1, keepdims=True)
            var = jnp.mean((x - mu) ** 2, axis=-1, keepdims=True)
            return (x - mu) * jax.lax.rsqrt(var + EPS) * w + b

        def _wkv(k, v, time_decay, curr_w):
            B, T, H = k.shape
            decay = -jnp.exp(time_decay)
            num0 = jnp.zeros((B, H), k.dtype)
            den0 = jnp.zeros((B, H), k.dtype)
            norm0 = jnp.full((B, H), -jnp.inf, k.dtype)

            def step(carry, kv):
                num, den, norm = carry
                kt, vt = kv
                ct = curr_w + kt
                cn = jnp.maximum(ct, norm)
                e_prev = jnp.exp(norm - cn)
                e_cur = jnp.exp(ct - cn)
                out = (e_prev * num + e_cur * vt) / (e_prev * den + e_cur)
                dpn = decay + norm
                new_norm = jnp.maximum(dpn, kt)
                e_d = jnp.exp(dpn - new_norm)
                e_k = jnp.exp(kt - new_norm)
                return ((e_d * num + e_k * vt, e_d * den + e_k, new_norm), out)
            kT = jnp.swapaxes(k, 0, 1)
            vT = jnp.swapaxes(v, 0, 1)
            (num, den, norm), outs = jax.lax.scan(step, (num0, den0, norm0), (kT, vT))
            return (jnp.swapaxes(outs, 0, 1), num, den, norm)

        def _reference_tuple_inner(hidden_state, ln_w, ln_b, Wk, Wv, Wr, Wo, mix_k, mix_v, mix_r, time_decay, current_token_weight):
            residual = hidden_state
            x = _layer_norm(hidden_state, ln_w, ln_b)
            B, T, H = x.shape
            sx = jnp.concatenate([jnp.zeros((B, 1, H), x.dtype), x[:, :-1, :]], axis=1)
            xk = sx + mix_k * (x - sx)
            xv = sx + mix_v * (x - sx)
            xr = sx + mix_r * (x - sx)
            r = jax.nn.sigmoid(jnp.einsum('bth,oh->bto', xr, Wr))
            k = jnp.einsum('bth,oh->bto', xk, Wk)
            v = jnp.einsum('bth,oh->bto', xv, Wv)
            wkv, num, den, norm = _wkv(k, v, time_decay, current_token_weight)
            rwkv = jnp.einsum('bth,oh->bto', r * wkv, Wo)
            out = residual + rwkv
            return (out, (x[:, -1, :], num, den, norm))
        H = 256
        B, T = (4, 256)
        key = jax.random.key(seed)
        ks = jax.random.split(key, 12)
        s = 0.02
        return {'hidden_state': jax.random.normal(ks[0], (B, T, H), dtype=jnp.float32), 'ln_w': jnp.ones((H,), jnp.float32), 'ln_b': jnp.zeros((H,), jnp.float32), 'Wk': jax.random.normal(ks[1], (H, H), jnp.float32) * s, 'Wv': jax.random.normal(ks[2], (H, H), jnp.float32) * s, 'Wr': jax.random.normal(ks[3], (H, H), jnp.float32) * s, 'Wo': jax.random.normal(ks[4], (H, H), jnp.float32) * s, 'mix_k': jax.random.uniform(ks[5], (H,), jnp.float32), 'mix_v': jax.random.uniform(ks[6], (H,), jnp.float32), 'mix_r': jax.random.uniform(ks[7], (H,), jnp.float32), 'time_decay': jax.random.normal(ks[8], (H,), jnp.float32) * 0.5, 'current_token_weight': jax.random.normal(ks[9], (H,), jnp.float32) * 0.5}
    _L0_attn_in = _L0_attn_setup()

    def _L0_ffn_setup():
        import jax, jax.numpy as jnp
        import numpy as np
        NUM_EXPERTS = 16
        C = 1.0
        key = jax.random.key(seed)
        k1, k2, k3 = jax.random.split(key, 3)
        b, s, h = (4, 256, 256)
        return {'x': jax.random.normal(k1, (b, s, h), dtype=jnp.float32), 'router_w': jax.random.normal(k2, (h, NUM_EXPERTS), dtype=jnp.float32) * 0.02, 'router_b': jnp.zeros((NUM_EXPERTS,), dtype=jnp.float32), 'expert_w': jax.random.normal(k3, (h, h), dtype=jnp.float32) * 0.02, 'expert_b': jnp.zeros((h,), dtype=jnp.float32)}
    _L0_ffn_in = _L0_ffn_setup()

    def _L1_attn_setup():
        import jax, jax.numpy as jnp
        import numpy as np
        CHUNK = 64
        L2_EPS = 1e-06
        RMS_EPS = 1e-05

        def _silu(x):
            return x * jax.nn.sigmoid(x)

        def _causal_shared_conv(x, w):
            K = w.shape[0]
            T = x.shape[1]
            xp = jnp.pad(x, ((0, 0), (K - 1, 0), (0, 0)))
            out = w[0] * xp[:, 0:T, :]
            for j in range(1, K):
                out = out + w[j] * xp[:, j:j + T, :]
            return out

        def _l2norm(x):
            return x * jax.lax.rsqrt(jnp.sum(x * x, axis=-1, keepdims=True) + L2_EPS)

        def _delta_rule_chunk(q, k, v, beta, chunk=CHUNK):
            B, H, T, dk = q.shape
            dv = v.shape[-1]
            q = q * dk ** (-0.5)
            nC = T // chunk
            q = q.reshape(B, H, nC, chunk, dk)
            k = k.reshape(B, H, nC, chunk, dk)
            v = v.reshape(B, H, nC, chunk, dv)
            beta = beta.reshape(B, H, nC, chunk)
            k_beta = k * beta[..., None]
            v_beta = v * beta[..., None]
            A = jnp.einsum('bhncd,bhnmd->bhncm', k_beta, k)
            stril = jnp.tril(jnp.ones((chunk, chunk), bool), -1)
            M = jnp.where(stril, A, 0.0) + jnp.eye(chunk, dtype=q.dtype)
            u = jax.scipy.linalg.solve_triangular(M, v_beta, lower=True)
            w = jax.scipy.linalg.solve_triangular(M, k_beta, lower=True)
            tril_incl = jnp.tril(jnp.ones((chunk, chunk), bool))

            def step(S, inp):
                q_i, k_i, u_i, w_i = inp
                u_i = u_i - jnp.einsum('bhcd,bhde->bhce', w_i, S)
                attn = jnp.where(tril_incl, jnp.einsum('bhcd,bhmd->bhcm', q_i, k_i), 0.0)
                o_i = jnp.einsum('bhcd,bhde->bhce', q_i, S) + jnp.einsum('bhcm,bhme->bhce', attn, u_i)
                S = S + jnp.einsum('bhcd,bhce->bhde', k_i, u_i)
                return (S, o_i)
            xs = tuple((jnp.moveaxis(t, 2, 0) for t in (q, k, u, w)))
            S0 = jnp.zeros((B, H, dk, dv), q.dtype)
            _, o = jax.lax.scan(step, S0, xs)
            return jnp.moveaxis(o, 0, 2).reshape(B, H, T, dv)
        key = jax.random.key(seed)
        ks = jax.random.split(key, 10)
        B, T, D, H = (2, 512, 256, 16)
        sc = 0.02
        return {'x': jax.random.normal(ks[0], (B, T, D), jnp.float32), 'Wq': jax.random.normal(ks[1], (D, D), jnp.float32) * sc, 'Wk': jax.random.normal(ks[2], (D, D), jnp.float32) * sc, 'Wv': jax.random.normal(ks[3], (D, D), jnp.float32) * sc, 'Wb': jax.random.normal(ks[4], (D, H), jnp.float32) * sc, 'Wo': jax.random.normal(ks[5], (D, D), jnp.float32) * sc, 'conv_q': jax.random.normal(ks[6], (4,), jnp.float32) * 0.5, 'conv_k': jax.random.normal(ks[7], (4,), jnp.float32) * 0.5, 'conv_v': jax.random.normal(ks[8], (4,), jnp.float32) * 0.5, 'onorm_w': jnp.ones((D // H,), jnp.float32)}
    _L1_attn_in = _L1_attn_setup()

    def _L1_ffn_setup():
        import jax, jax.numpy as jnp
        import numpy as np
        B, S, D = (2, 256, 256)
        E = 8
        TOPK = 2
        H_SHARED = 1024
        H_ROUTED = 128
        STD = 0.02
        key = jax.random.key(seed)
        ks = jax.random.split(key, 7)
        return {'x': jax.random.normal(ks[0], (B, S, D), jnp.float32), 'w12': jax.random.normal(ks[1], (E, 2 * H_ROUTED, D), jnp.float32) * STD, 'w3': jax.random.normal(ks[2], (E, D, H_ROUTED), jnp.float32) * STD, 'router_w': jax.random.normal(ks[3], (E, D), jnp.float32) * STD, 'expert_bias': jnp.zeros((E,), jnp.float32), 'sw1': jax.random.normal(ks[4], (H_SHARED, D), jnp.float32) * STD, 'sw2': jax.random.normal(ks[5], (H_SHARED, D), jnp.float32) * STD, 'sw3': jax.random.normal(ks[6], (D, H_SHARED), jnp.float32) * STD}
    _L1_ffn_in = _L1_ffn_setup()
    _d = {'L0_attn_hidden_state': _L0_attn_in['hidden_state'], 'L0_attn_ln_w': _L0_attn_in['ln_w'], 'L0_attn_ln_b': _L0_attn_in['ln_b'], 'L0_attn_Wk': _L0_attn_in['Wk'], 'L0_attn_Wv': _L0_attn_in['Wv'], 'L0_attn_Wr': _L0_attn_in['Wr'], 'L0_attn_Wo': _L0_attn_in['Wo'], 'L0_attn_mix_k': _L0_attn_in['mix_k'], 'L0_attn_mix_v': _L0_attn_in['mix_v'], 'L0_attn_mix_r': _L0_attn_in['mix_r'], 'L0_attn_time_decay': _L0_attn_in['time_decay'], 'L0_attn_current_token_weight': _L0_attn_in['current_token_weight'], 'L0_ffn_router_w': _L0_ffn_in['router_w'], 'L0_ffn_router_b': _L0_ffn_in['router_b'], 'L0_ffn_expert_w': _L0_ffn_in['expert_w'], 'L0_ffn_expert_b': _L0_ffn_in['expert_b'], 'L1_attn_Wq': _L1_attn_in['Wq'], 'L1_attn_Wk': _L1_attn_in['Wk'], 'L1_attn_Wv': _L1_attn_in['Wv'], 'L1_attn_Wb': _L1_attn_in['Wb'], 'L1_attn_Wo': _L1_attn_in['Wo'], 'L1_attn_conv_q': _L1_attn_in['conv_q'], 'L1_attn_conv_k': _L1_attn_in['conv_k'], 'L1_attn_conv_v': _L1_attn_in['conv_v'], 'L1_attn_onorm_w': _L1_attn_in['onorm_w'], 'L1_ffn_w12': _L1_ffn_in['w12'], 'L1_ffn_w3': _L1_ffn_in['w3'], 'L1_ffn_router_w': _L1_ffn_in['router_w'], 'L1_ffn_expert_bias': _L1_ffn_in['expert_bias'], 'L1_ffn_sw1': _L1_ffn_in['sw1'], 'L1_ffn_sw2': _L1_ffn_in['sw2'], 'L1_ffn_sw3': _L1_ffn_in['sw3']}
    _x0 = _d['L0_attn_hidden_state']
    _d['L0_attn_hidden_state'] = jax.random.normal(jax.random.fold_in(jax.random.key(seed), 1), (2, 512, 256), dtype=_x0.dtype)
    del _x0
    return _d

def reference(L0_attn_hidden_state, L0_attn_ln_w, L0_attn_ln_b, L0_attn_Wk, L0_attn_Wv, L0_attn_Wr, L0_attn_Wo, L0_attn_mix_k, L0_attn_mix_v, L0_attn_mix_r, L0_attn_time_decay, L0_attn_current_token_weight, L0_ffn_router_w, L0_ffn_router_b, L0_ffn_expert_w, L0_ffn_expert_b, L1_attn_Wq, L1_attn_Wk, L1_attn_Wv, L1_attn_Wb, L1_attn_Wo, L1_attn_conv_q, L1_attn_conv_k, L1_attn_conv_v, L1_attn_onorm_w, L1_ffn_w12, L1_ffn_w3, L1_ffn_router_w, L1_ffn_expert_bias, L1_ffn_sw1, L1_ffn_sw2, L1_ffn_sw3):

    def _L0_attn_ref(hidden_state, ln_w, ln_b, Wk, Wv, Wr, Wo, mix_k, mix_v, mix_r, time_decay, current_token_weight):
        import jax, jax.numpy as jnp
        import numpy as np
        EPS = 1e-05

        def _layer_norm(x, w, b):
            mu = jnp.mean(x, axis=-1, keepdims=True)
            var = jnp.mean((x - mu) ** 2, axis=-1, keepdims=True)
            return (x - mu) * jax.lax.rsqrt(var + EPS) * w + b

        def _wkv(k, v, time_decay, curr_w):
            B, T, H = k.shape
            decay = -jnp.exp(time_decay)
            num0 = jnp.zeros((B, H), k.dtype)
            den0 = jnp.zeros((B, H), k.dtype)
            norm0 = jnp.full((B, H), -jnp.inf, k.dtype)

            def step(carry, kv):
                num, den, norm = carry
                kt, vt = kv
                ct = curr_w + kt
                cn = jnp.maximum(ct, norm)
                e_prev = jnp.exp(norm - cn)
                e_cur = jnp.exp(ct - cn)
                out = (e_prev * num + e_cur * vt) / (e_prev * den + e_cur)
                dpn = decay + norm
                new_norm = jnp.maximum(dpn, kt)
                e_d = jnp.exp(dpn - new_norm)
                e_k = jnp.exp(kt - new_norm)
                return ((e_d * num + e_k * vt, e_d * den + e_k, new_norm), out)
            kT = jnp.swapaxes(k, 0, 1)
            vT = jnp.swapaxes(v, 0, 1)
            (num, den, norm), outs = jax.lax.scan(step, (num0, den0, norm0), (kT, vT))
            return (jnp.swapaxes(outs, 0, 1), num, den, norm)

        def _reference_tuple_inner(hidden_state, ln_w, ln_b, Wk, Wv, Wr, Wo, mix_k, mix_v, mix_r, time_decay, current_token_weight):
            residual = hidden_state
            x = _layer_norm(hidden_state, ln_w, ln_b)
            B, T, H = x.shape
            sx = jnp.concatenate([jnp.zeros((B, 1, H), x.dtype), x[:, :-1, :]], axis=1)
            xk = sx + mix_k * (x - sx)
            xv = sx + mix_v * (x - sx)
            xr = sx + mix_r * (x - sx)
            r = jax.nn.sigmoid(jnp.einsum('bth,oh->bto', xr, Wr))
            k = jnp.einsum('bth,oh->bto', xk, Wk)
            v = jnp.einsum('bth,oh->bto', xv, Wv)
            wkv, num, den, norm = _wkv(k, v, time_decay, current_token_weight)
            rwkv = jnp.einsum('bth,oh->bto', r * wkv, Wo)
            out = residual + rwkv
            return (out, (x[:, -1, :], num, den, norm))
        return _reference_tuple_inner(hidden_state, ln_w, ln_b, Wk, Wv, Wr, Wo, mix_k, mix_v, mix_r, time_decay, current_token_weight)[0]

    def _L0_ffn_ref(x, router_w, router_b, expert_w, expert_b):
        import jax, jax.numpy as jnp
        import numpy as np
        NUM_EXPERTS = 16
        C = 1.0
        b, s, h = x.shape
        bs = b * s
        k = min(int(bs * C / NUM_EXPERTS), bs)
        xf = x.reshape(bs, h)
        logits = xf @ router_w + router_b
        S = jax.nn.softmax(logits, axis=-1)
        G, idx = jax.lax.top_k(S.T, k)
        tokens = xf[idx]
        out = jnp.einsum('ekh,hd->ekd', tokens, expert_w) + expert_b
        weighted = G[..., None] * out
        y = jnp.zeros((bs, h), dtype=x.dtype).at[idx.reshape(-1)].add(weighted.reshape(-1, h))
        return y.reshape(b, s, h)

    def _L1_attn_ref(x, Wq, Wk, Wv, Wb, Wo, conv_q, conv_k, conv_v, onorm_w):
        import jax, jax.numpy as jnp
        import numpy as np
        CHUNK = 64
        L2_EPS = 1e-06
        RMS_EPS = 1e-05

        def _silu(x):
            return x * jax.nn.sigmoid(x)

        def _causal_shared_conv(x, w):
            K = w.shape[0]
            T = x.shape[1]
            xp = jnp.pad(x, ((0, 0), (K - 1, 0), (0, 0)))
            out = w[0] * xp[:, 0:T, :]
            for j in range(1, K):
                out = out + w[j] * xp[:, j:j + T, :]
            return out

        def _l2norm(x):
            return x * jax.lax.rsqrt(jnp.sum(x * x, axis=-1, keepdims=True) + L2_EPS)

        def _delta_rule_chunk(q, k, v, beta, chunk=CHUNK):
            B, H, T, dk = q.shape
            dv = v.shape[-1]
            q = q * dk ** (-0.5)
            nC = T // chunk
            q = q.reshape(B, H, nC, chunk, dk)
            k = k.reshape(B, H, nC, chunk, dk)
            v = v.reshape(B, H, nC, chunk, dv)
            beta = beta.reshape(B, H, nC, chunk)
            k_beta = k * beta[..., None]
            v_beta = v * beta[..., None]
            A = jnp.einsum('bhncd,bhnmd->bhncm', k_beta, k)
            stril = jnp.tril(jnp.ones((chunk, chunk), bool), -1)
            M = jnp.where(stril, A, 0.0) + jnp.eye(chunk, dtype=q.dtype)
            u = jax.scipy.linalg.solve_triangular(M, v_beta, lower=True)
            w = jax.scipy.linalg.solve_triangular(M, k_beta, lower=True)
            tril_incl = jnp.tril(jnp.ones((chunk, chunk), bool))

            def step(S, inp):
                q_i, k_i, u_i, w_i = inp
                u_i = u_i - jnp.einsum('bhcd,bhde->bhce', w_i, S)
                attn = jnp.where(tril_incl, jnp.einsum('bhcd,bhmd->bhcm', q_i, k_i), 0.0)
                o_i = jnp.einsum('bhcd,bhde->bhce', q_i, S) + jnp.einsum('bhcm,bhme->bhce', attn, u_i)
                S = S + jnp.einsum('bhcd,bhce->bhde', k_i, u_i)
                return (S, o_i)
            xs = tuple((jnp.moveaxis(t, 2, 0) for t in (q, k, u, w)))
            S0 = jnp.zeros((B, H, dk, dv), q.dtype)
            _, o = jax.lax.scan(step, S0, xs)
            return jnp.moveaxis(o, 0, 2).reshape(B, H, T, dv)
        B, T, D = x.shape
        H = Wb.shape[1]
        dk = Wq.shape[1] // H
        dv = Wv.shape[1] // H
        q = _silu(_causal_shared_conv(x @ Wq, conv_q))
        k = _silu(_causal_shared_conv(x @ Wk, conv_k))
        v = _silu(_causal_shared_conv(x @ Wv, conv_v))
        beta = jax.nn.sigmoid(x @ Wb)
        qh = _l2norm(q.reshape(B, T, H, dk)).transpose(0, 2, 1, 3)
        kh = _l2norm(k.reshape(B, T, H, dk)).transpose(0, 2, 1, 3)
        vh = v.reshape(B, T, H, dv).transpose(0, 2, 1, 3)
        o = _delta_rule_chunk(qh, kh, vh, beta.transpose(0, 2, 1))
        o = o.transpose(0, 2, 1, 3)
        o = o * jax.lax.rsqrt(jnp.mean(o * o, axis=-1, keepdims=True) + RMS_EPS) * onorm_w
        return o.reshape(B, T, H * dv) @ Wo

    def _L1_ffn_ref(x, w12, w3, router_w, expert_bias, sw1, sw2, sw3):
        import jax, jax.numpy as jnp
        import numpy as np
        B, S, D = (2, 256, 256)
        E = 8
        TOPK = 2
        H_SHARED = 1024
        H_ROUTED = 128
        STD = 0.02
        b, s, d = x.shape
        g = x @ sw1.T
        u = x @ sw2.T
        shared_out = jax.nn.silu(g) * u @ sw3.T
        scores = jax.nn.sigmoid(x @ router_w.T)
        selection_scores = scores + expert_bias
        _, top_idx = jax.lax.top_k(selection_scores, TOPK)
        top_scores = jnp.take_along_axis(scores, top_idx, axis=-1)
        top_scores = top_scores / (top_scores.sum(-1, keepdims=True) + 1e-09)
        flat_x = x.reshape(-1, d)
        T = flat_x.shape[0]
        flat_idx = top_idx.reshape(T, TOPK)
        flat_sc = top_scores.reshape(T, TOPK)
        combine = jnp.zeros((T, E), x.dtype).at[jnp.arange(T)[:, None], flat_idx].add(flat_sc)
        h12 = jnp.einsum('td,ehd->teh', flat_x, w12)
        h1, h2 = jnp.split(h12, 2, axis=-1)
        h = jax.nn.silu(h1) * h2
        out_e = jnp.einsum('teh,edh->ted', h, w3)
        routed_out = jnp.einsum('ted,te->td', out_e, combine).reshape(b, s, d)
        return shared_out + routed_out
    x = L0_attn_hidden_state
    x = x + _layernorm(_L0_attn_ref(_layernorm(x, axis=-1), L0_attn_ln_w, L0_attn_ln_b, L0_attn_Wk, L0_attn_Wv, L0_attn_Wr, L0_attn_Wo, L0_attn_mix_k, L0_attn_mix_v, L0_attn_mix_r, L0_attn_time_decay, L0_attn_current_token_weight), axis=-1)
    x = x + _layernorm(_L0_ffn_ref(_layernorm(x, axis=-1), L0_ffn_router_w, L0_ffn_router_b, L0_ffn_expert_w, L0_ffn_expert_b), axis=-1)
    x = x + _layernorm(_L1_attn_ref(_layernorm(x, axis=-1), L1_attn_Wq, L1_attn_Wk, L1_attn_Wv, L1_attn_Wb, L1_attn_Wo, L1_attn_conv_q, L1_attn_conv_k, L1_attn_conv_v, L1_attn_onorm_w), axis=-1)
    x = x + _layernorm(_L1_ffn_ref(_layernorm(x, axis=-1), L1_ffn_w12, L1_ffn_w3, L1_ffn_router_w, L1_ffn_expert_bias, L1_ffn_sw1, L1_ffn_sw2, L1_ffn_sw3), axis=-1)
    return x

_drawn_inputs = setup_inputs


def setup_inputs(seed=0):
    import zlib

    import numpy as np

    out = dict(_drawn_inputs(seed))
    spreads = {'L0_attn_ln_w': (1.0, 0.6),
     'L0_attn_ln_b': (0.0, 0.8),
     'L0_ffn_router_b': (0.0, 0.1),
     'L0_ffn_expert_b': (0.0, 0.1),
     'L1_attn_onorm_w': (1.0, 0.2),
     'L1_ffn_expert_bias': (0.0, 0.1)}
    factors = {'L0_attn_Wk': 8.0,
     'L0_attn_Wr': 4.147,
     'L0_attn_mix_k': 8.0,
     'L0_attn_mix_r': 8.0,
     'L0_attn_current_token_weight': 13.259}
    for name, (base, spread) in spreads.items():
        noise = np.random.default_rng([zlib.crc32(name.encode()), seed]).standard_normal(out[name].shape)
        drawn = base * np.exp(spread * noise) if base else spread * noise
        out[name] = jnp.asarray(drawn.astype(out[name].dtype))
    for name, factor in factors.items():
        out[name] = (out[name] * factor).astype(out[name].dtype)
    return out
```

```python
from contextlib import ExitStack

import concourse.bass as bass
from concourse import mybir

F32 = mybir.dt.float32
F32R = mybir.dt.float32r
U32 = mybir.dt.uint32
ALU = mybir.AluOpType
ACT = mybir.ActivationFunctionType
AX_X = mybir.AxisListType.X

P = 128
B, T, D = 2, 512, 256
N = B * T
NT = N // P
TB = T // P
C = D // P
LN_EPS = 1e-5


class Core:

    def __init__(self, nc, ctx):
        self.nc, self.ctx, self.named = nc, ctx, {}

    def sb(self, name, shape):
        return self.ctx.enter_context(self.nc.sbuf_tensor(name, shape, F32))

    def weights(self, ins):
        sb = self.sb
        self.w_ec = sb("w_ec", [P, C, D + 16])
        self.b_ec = sb("b_ec", [1, D + 16])
        self.w_in = self.sem("w_in")
        self.loads = [
            (self.w_ec[:, :, 0:D], ins["L0_ffn_expert_w"].rearrange("(c p) n -> p c n", p=P)),
            (self.w_ec[:, :, D:], ins["L0_ffn_router_w"].rearrange("(c p) n -> p c n", p=P)),
            (self.b_ec[:, 0:D], ins["L0_ffn_expert_b"].unsqueeze(0)),
            (self.b_ec[:, D:], ins["L0_ffn_router_b"].unsqueeze(0)),
        ]
        self.w_qkv = sb("w_qkv", [P, 3, C, D])
        self.w_beta = sb("w_beta", [P, C, 16])
        self.w_o = sb("w_o", [P, C, D])
        self.conv_w = sb("conv_w", [P, 3, 4])
        self.onorm = sb("onorm", [P, 16])
        for n, name in enumerate("qkv"):
            self.loads += [
                (self.w_qkv[:, n], ins["L1_attn_W" + name].rearrange("(c p) n -> p c n", p=P)),
                (self.conv_w[:, n], ins["L1_attn_conv_" + name].partition_broadcast(P)),
            ]
        self.loads += [
            (self.w_beta[:], ins["L1_attn_Wb"].rearrange("(c p) n -> p c n", p=P)),
            (self.w_o[:], ins["L1_attn_Wo"].rearrange("(c p) n -> p c n", p=P)),
            (self.onorm[:], ins["L1_attn_onorm_w"].partition_broadcast(P)),
        ]
        self.conv = sb("conv", [P, 4, P + 3])
        self.taps = sb("taps", [P, 4, P + 3])
        self.scratch = sb("taps_scaled", [P, 3, P + 3])
        self.above = sb("above", [P, 32])
        self.upto = sb("upto", [P, 32])
        self.same_head = sb("same_head", [P, P])
        self.numbers = sb("numbers", [P, 8])
        self.w_in_total = 16 * len(self.loads)

    def late_weights(self, ins):
        sb = self.sb
        E, self.SH = 8, 1024 // P
        self.stored = sb("stored", [P, 6 * self.SH * D])
        tile = self.SH * D

        def part(n, size, split, **sizes):
            return self.stored[:, n * tile:(n + size) * tile].rearrange(split, **sizes)

        self.sw1 = part(0, 1, "p (a d) -> p a d", d=D)
        self.sw2 = part(1, 1, "p (a d) -> p a d", d=D)
        self.w12 = part(2, 2, "p (a d) -> p a d", d=D)
        self.sw3 = part(4, 1, "p (c h) -> p c h", c=C)
        self.w3 = part(5, 1, "p (e c h) -> p e c h", e=E, c=C)
        self.router = sb("router", [E, D])
        self.expert_bias = sb("expert_bias", [P, E])
        self.f_in = self.sem("f_in")
        self.share_dram = self.nc.dram_tensor("share_dram", (E, N), F32, kind="Internal").ap()
        self.ffn_loads = [
            (self.sw1, ins["L1_ffn_sw1"].rearrange("(a p) d -> p a d", p=P)),
            (self.sw2, ins["L1_ffn_sw2"].rearrange("(a p) d -> p a d", p=P)),
            (self.w12, ins["L1_ffn_w12"].rearrange("e (a p) d -> p (e a) d", p=P)),
            (self.sw3, ins["L1_ffn_sw3"].rearrange("(c p) h -> p c h", p=P)),
            (self.w3, ins["L1_ffn_w3"].rearrange("e (c p) h -> p e c h", p=P)),
            (self.router[:], ins["L1_ffn_router_w"]),
            (self.expert_bias[:], ins["L1_ffn_expert_bias"].partition_broadcast(P)),
        ]
        self.f_in_total = 16 * len(self.ffn_loads)

    def prefetch_late(self, sp):
        for place, source in self.ffn_loads:
            sp.dma_start(place, source).then_inc(self.f_in, 16)

    def prefetch(self, sp):
        for place, source in self.loads:
            sp.dma_start(place, source).then_inc(self.w_in, 16)

    def masks(self, pool, order):
        g = self.nc.gpsimd
        count = [0]

        def link(ins):
            count[0] += 1
            ins.then_inc(order, 1)
            pool.wait_ge(order, count[0])

        def where(dst, op, fill, base, pattern, step):
            link(g.affine_select(out=dst, in_=dst, compare_op=op, fill=fill, base=base, pattern=pattern,
                                 channel_multiplier=step))

        for e in range(8):
            link(g.memset(self.numbers[:, e:e + 1], float(e)))
        for m in (self.above, self.upto, self.same_head):
            link(g.memset(m[:], 1.0))
        for r in range(4):
            rows = slice(32 * r, 32 * r + 32)
            where(self.above[rows], ALU.is_gt, 0.0, 0, [[1, 32]], -1)
            where(self.upto[rows], ALU.is_ge, 0.0, 0, [[1, 32]], -1)
        by_head = self.same_head[:].rearrange("p (h e) -> p h e", h=8)
        where(by_head, ALU.is_ge, 0.0, 0, [[-16, 8], [0, 16]], 1)
        where(by_head, ALU.is_ge, 0.0, 15, [[16, 8], [0, 16]], -1)
        link(g.memset(self.taps[:], 0.0))
        for d in range(4):
            where(self.taps[:, d], ALU.not_equal, 1.0, -d, [[1, P + 3]], -1)
        link(g.tensor_copy(self.conv[:, 0], self.taps[:, 0]))
        pool.wait_ge(self.w_in, self.w_in_total)
        for n in range(3):
            link(g.tensor_scalar(self.conv[:, 1 + n], self.taps[:, 3], self.conv_w[:, n, 0:1], 0.0, ALU.mult,
                                 ALU.add))
        for d in (2, 1, 0):
            for n in range(3):
                link(g.tensor_scalar(self.scratch[:, n], self.taps[:, d], self.conv_w[:, n, 3 - d:4 - d], 0.0,
                                     ALU.mult, ALU.add))
            for n in range(3):
                link(g.tensor_tensor(self.conv[:, 1 + n], self.conv[:, 1 + n], self.scratch[:, n], ALU.add))

    def sem(self, name):
        if name not in self.named:
            self.named[name] = self.ctx.enter_context(self.nc.semaphore(name))
        return self.named[name]


def chain(eng, sem, count):
    def link(ins):
        count[0] += 1
        ins.then_inc(sem, 1)
        eng.wait_ge(sem, count[0])
    return link


def tiles(dram):
    return dram.rearrange("(t p) d -> p t d", p=P)


class Norm:

    def __init__(self, core):
        sb = core.sb
        self.nc, self.done = core.nc, [0, 0]
        self.stats = sb("ln_stats", [P, NT, 6])
        self.mv = sb("ln_mean_var", [P, NT, 2])
        self.std = sb("ln_std_dev", [P, NT])
        self.inv = sb("ln_inverse_std", [P, NT])
        self.var_ready, self.std_ready = core.sem("ln_var"), core.sem("ln_std")

    def on_act(self, act, eps):
        self.done[1] += 1
        act.wait_ge(self.var_ready, self.done[1])
        self.nc.scalar.activation(self.std[:], self.mv[:, :, 1], ACT.Sqrt, bias=eps).then_inc(self.std_ready, 1)

    def on_dve(self, dve, link, src, dst):
        v = self.nc.vector
        self.done[0] += 1
        for t in range(NT):
            last = v.bn_stats(self.stats[:, t, :], src[:, t, :])
        link(last)
        for t in range(NT):
            last = v.bn_aggr(self.mv[:, t, :], self.stats[:, t, :])
        last.then_inc(self.var_ready, 1)
        dve.wait_ge(self.std_ready, self.done[0])
        link(v.reciprocal(self.inv[:], self.std[:]))
        for t in range(NT):
            last = v.tensor_scalar(dst[:, t, :], src[:, t, :], self.mv[:, t, 0:1], self.inv[:, t:t + 1],
                                   ALU.subtract, ALU.mult)
        return last


def time_mixing(core, ins):
    nc, sem, norm, x = core.nc, core.sem, core.norm, core.x
    KEY, VALUE, GATE, OUT = range(4)
    with ExitStack() as own:
        def sb(name, shape):
            return own.enter_context(nc.sbuf_tensor(name, shape, F32))

        w_nat = sb("w_nat", [P, 4, C, D])
        w_t = sb("w_t", [P, 4, C, D])
        vec = sb("vec", [P, 7, C])
        vec_rows = sb("vec_rows", [7 * C, P])
        decay = sb("decay", [P, C])
        xn = sb("xn", [P, NT, D])
        xl = sb("xl", [P, NT, D])
        xs = sb("xs", [P, C, B, T + 1])
        diff = sb("diff", [P, C, B, T])
        mixed = sb("mixed", [P, 3, C, B, T])
        k = sb("k", [P, C, B, T])
        v = sb("v", [P, C, B, T])
        r = sb("r", [P, C, B, T])
        top = sb("top", [P, C, B, T + 1])
        num = sb("num", [P, C, B, T + 1])
        den = sb("den", [P, C, B, T + 1])
        ea = sb("ea", [P, C, B, T])
        eb = sb("eb", [P, C, B, T])
        ec = w_nat[:].rearrange("p i c h -> p (i c h)").rearrange("p (c b t) -> p c b t", c=C, b=B)
        ed = xl[:].rearrange("p t d -> p (t d)").rearrange("p (c b t) -> p c b t", c=C, b=B)
        LN_W, LN_B, MIX_K, MIX_V, MIX_R, DECAY, BONUS = range(7)
        BEFORE = -3.0e38

        x_in, w_in, vec_in = sem("x_in"), sem("wkv_w_in"), sem("wkv_vec_in")
        vec_turned, vec_kept = sem("wkv_vec_turned"), sem("wkv_vec_kept")
        w_turned, w_kept = sem("wkv_w_turned"), sem("wkv_w_kept")
        xl_ready, xl_turned, xs_ready = sem("xl_ready"), sem("xl_turned"), sem("xs_ready")
        mix_ready, proj, kv_kept, r_kept = sem("mix_ready"), sem("wkv_proj"), sem("kv_kept"), sem("r_kept")
        decay_exp = sem("decay_exp")
        d_ready, cur_prev_exp, scaled_ready, scan_exp = (sem("bonus_diff"), sem("bonus_exp"), sem("scan_diff"),
                                                         sem("scan_exp"))
        rw_ready, rw_proj = sem("rw_ready"), sem("rw_proj")
        ps = core.ps
        hidden = ins["L0_attn_hidden_state"].rearrange("b t d -> (b t) d")

        with nc.Block() as block:

            @block.sync
            def _(sp):
                for t in range(0, NT, 2):
                    sp.dma_start(x[:, t:t + 2, :], tiles(hidden)[:, t:t + 2, :]).then_inc(x_in, 16)
                for i, name in enumerate(["ln_w", "ln_b", "mix_k", "mix_v", "mix_r", "time_decay",
                                          "current_token_weight"]):
                    sp.dma_start(vec_rows[C * i:C * i + C, :], ins["L0_attn_" + name].rearrange("(c p) -> c p", p=P)) \
                        .then_inc(vec_in, 16)
                core.prefetch(sp)

            @block.gpsimd
            def _(pool):
                for i, name in enumerate(["Wk", "Wv", "Wr", "Wo"]):
                    pool.dma_start(w_nat[:, i], ins["L0_attn_" + name].rearrange("(c p) h -> p c h", p=P)) \
                        .then_inc(w_in, 16)
                made = sem("pool_made")
                nc.gpsimd.memset(core.ident[:], 0.0).then_inc(made, 1)
                pool.wait_ge(made, 1)
                nc.gpsimd.affine_select(out=core.ident[:], in_=core.ident[:], compare_op=ALU.not_equal, fill=1.0,
                                        base=0, pattern=[[-1, P]], channel_multiplier=1).then_inc(made, 1)
                nc.gpsimd.memset(core.ones[:], 1.0).then_inc(made, 1)
                nc.gpsimd.memset(core.ln_eps[:], LN_EPS).then_inc(made, 1)
                nc.gpsimd.memset(core.l2_eps[:], 1e-6).then_inc(made, 1)
                nc.gpsimd.memset(xs[:, :, :, 0:1], 0.0).then_inc(made, 1)
                nc.gpsimd.memset(top[:, :, :, 0:1], BEFORE).then_inc(made, 1)
                nc.gpsimd.memset(num[:, :, :, 0:1], 0.0).then_inc(made, 1)
                nc.gpsimd.memset(den[:, :, :, 0:1], 0.0).then_inc(made, 1)
                core.masks(pool, sem("masks_order"))

            @block.tensor
            def _(pe):
                pe.wait_ge(sem("pool_made"), 2)
                for i in range(4):
                    pe.wait_ge(w_in, 64)
                    for h in range(C):
                        for o in range(C):
                            last = nc.tensor.transpose(ps[:, i, h * D + o * P:h * D + (o + 1) * P],
                                                       w_nat[:, i, o, h * P:(h + 1) * P], core.ident[:])
                    last.then_inc(w_turned, 1)
                pe.wait_ge(vec_in, 7 * 16)
                nc.tensor.transpose(ps[:, 4, 0:7 * C], vec_rows[:], core.ident[0:7 * C, 0:7 * C]).then_inc(vec_turned, 1)
                pe.wait_ge(vec_kept, 1)
                pe.wait_ge(xl_ready, 1)
                for b in range(B):
                    for c in range(C):
                        for t in range(TB):
                            last = nc.tensor.transpose(ps[:, 4 + 2 * b + c, t * P:(t + 1) * P],
                                                       xl[:, b * TB + t, c * P:(c + 1) * P], core.ident[:])
                    last.then_inc(xl_turned, 1)
                pe.wait_ge(w_kept, 4)
                pe.wait_ge(xs_ready, 4)
                for i in (KEY, VALUE, GATE):
                    pe.wait_ge(mix_ready, i + 1)
                    if i == GATE:
                        pe.wait_ge(kv_kept, 4)
                    for o in range(C):
                        for b in range(B):
                            bank = 4 * (i % 2) + 2 * o + b
                            for c in range(C):
                                last = nc.tensor.matmul(ps[:, bank, :], w_t[:, i, c, o * P:(o + 1) * P],
                                                        mixed[:, i, c, b, :], start=c == 0, stop=c == C - 1)
                            last.then_inc(proj, 1)
                pe.wait_ge(rw_ready, 2)
                for t in range(NT):
                    bank = 4 + t // 2
                    for c in range(C):
                        last = nc.tensor.matmul(ps[:, bank, (t % 2) * D:(t % 2 + 1) * D],
                                                r[:, c, t // TB, (t % TB) * P:(t % TB + 1) * P],
                                                w_t[:, OUT, c, :], start=c == 0, stop=c == C - 1)
                    last.then_inc(rw_proj, 1)

            @block.scalar
            def _(act):
                a = nc.scalar.activation
                act.wait_ge(sem("pool_made"), 4)
                for i in range(4):
                    act.wait_ge(w_turned, i + 1)
                    nc.scalar.copy(w_t[:, i].rearrange("p c o -> p (c o)"), ps[:, i, :]).then_inc(w_kept, 1)
                act.wait_ge(vec_turned, 1)
                nc.scalar.copy(vec[:].rearrange("p i c -> p (i c)"), ps[:, 4, 0:7 * C]).then_inc(vec_kept, 1)
                norm.on_act(act, core.ln_eps[:])
                norm.on_act(act, core.ln_eps[:])
                act.wait_ge(vec_kept, 1)
                for b in range(B):
                    act.wait_ge(xl_turned, b + 1)
                    for c in range(C):
                        a(xs[:, c, b, 1:], ps[:, 4 + 2 * b + c, :], ACT.Identity, scale=vec[:, LN_W, c:c + 1],
                          bias=vec[:, LN_B, c:c + 1]).then_inc(xs_ready, 1)
                a(decay[:], vec[:, DECAY, :], ACT.Exp).then_inc(decay_exp, 1)
                for i in (KEY, VALUE):
                    for o in range(C):
                        for b in range(B):
                            act.wait_ge(proj, 4 * i + 2 * o + b + 1)
                            nc.scalar.copy((k, v)[i][:, o, b, :], ps[:, 4 * i + 2 * o + b, :]).then_inc(kv_kept, 1)
                for c in range(C):
                    act.wait_ge(d_ready, 2 * c + 2)
                    a(ea[:, c], ea[:, c], ACT.Exp, scale=-1.0).then_inc(cur_prev_exp, 1)
                    a(eb[:, c], eb[:, c], ACT.Exp).then_inc(cur_prev_exp, 1)
                    act.wait_ge(scaled_ready, 2 * c + 2)
                    a(ec[:, c], ec[:, c], ACT.Exp).then_inc(scan_exp, 1)
                    a(ed[:, c], ed[:, c], ACT.Exp).then_inc(scan_exp, 1)
                for o in range(C):
                    for b in range(B):
                        act.wait_ge(proj, 8 + 2 * o + b + 1)
                        a(r[:, o, b, :], ps[:, 2 * o + b, :], ACT.Sigmoid).then_inc(r_kept, 1)
                norm.on_act(act, core.ln_eps[:])

            @block.vector
            def _(dve):
                V = nc.vector
                link = chain(dve, sem("dve_order"), core.dve_count)
                dve.wait_ge(x_in, 4 * 16)
                link(norm.on_dve(dve, link, x, xn))
                norm.on_dve(dve, link, xn, xl).then_inc(xl_ready, 1)
                dve.wait_ge(xs_ready, 4)
                dve.wait_ge(sem("pool_made"), 9)
                dve.wait_ge(vec_kept, 1)
                for c in range(C):
                    last = V.tensor_tensor(diff[:, c], xs[:, c, :, 1:], xs[:, c, :, :T], ALU.subtract)
                link(last)
                for i in (KEY, VALUE, GATE):
                    for c in range(C):
                        last = V.scalar_tensor_tensor(mixed[:, i, c], diff[:, c], vec[:, MIX_K + i, c:c + 1],
                                                      xs[:, c, :, :T], ALU.mult, ALU.add)
                    last.then_inc(mix_ready, 1)
                dve.wait_ge(decay_exp, 1)
                link(V.tensor_scalar(decay[:], decay[:], -1.0, None, ALU.mult))
                dve.wait_ge(w_kept, 4)
                for c in range(C):
                    dve.wait_ge(kv_kept, 2 * c + 2)
                    for b in range(B):
                        last = V.tensor_tensor_scan(top[:, c, b, 1:], decay[:, c:c + 1].to_broadcast([P, T]),
                                                    k[:, c, b, :], BEFORE, ALU.add, ALU.max)
                    link(last)
                    link(V.scalar_tensor_tensor(diff[:, c], k[:, c], vec[:, BONUS, c:c + 1], top[:, c, :, :T],
                                                ALU.add, ALU.subtract))
                    V.tensor_scalar(ea[:, c], diff[:, c], 0.0, None, ALU.max).then_inc(d_ready, 1)
                    V.tensor_scalar(eb[:, c], diff[:, c], 0.0, None, ALU.min).then_inc(d_ready, 1)
                    V.scalar_tensor_tensor(ec[:, c], top[:, c, :, :T], decay[:, c:c + 1], top[:, c, :, 1:],
                                           ALU.add, ALU.subtract).then_inc(scaled_ready, 1)
                    V.tensor_tensor(ed[:, c], k[:, c], top[:, c, :, 1:], ALU.subtract).then_inc(scaled_ready, 1)
                for c in range(C):
                    dve.wait_ge(kv_kept, 4 + 2 * c + 2)
                    dve.wait_ge(scan_exp, 2 * c + 2)
                    link(V.tensor_tensor(diff[:, c], ed[:, c], v[:, c], ALU.mult))
                    for b in range(B):
                        V.tensor_tensor_scan(num[:, c, b, 1:], ec[:, c, b, :], diff[:, c, b, :], 0.0,
                                             ALU.mult, ALU.add)
                        last = V.tensor_tensor_scan(den[:, c, b, 1:], ec[:, c, b, :], ed[:, c, b, :], 0.0,
                                                    ALU.mult, ALU.add)
                    link(last)
                    dve.wait_ge(cur_prev_exp, 2 * c + 2)
                    V.tensor_tensor(diff[:, c], ea[:, c], num[:, c, :, :T], ALU.mult)
                    V.tensor_tensor(ec[:, c], eb[:, c], v[:, c], ALU.mult)
                    link(V.tensor_tensor(ed[:, c], ea[:, c], den[:, c, :, :T], ALU.mult))
                    V.tensor_tensor(ea[:, c], ed[:, c], eb[:, c], ALU.add)
                    link(V.tensor_tensor(diff[:, c], diff[:, c], ec[:, c], ALU.add))
                    link(V.reciprocal(ea[:, c], ea[:, c]))
                    link(V.tensor_tensor(diff[:, c], diff[:, c], ea[:, c], ALU.mult))
                    dve.wait_ge(r_kept, 2 * c + 2)
                    V.tensor_tensor(r[:, c], r[:, c], diff[:, c], ALU.mult).then_inc(rw_ready, 1)
                for t in range(0, NT, 2):
                    dve.wait_ge(rw_proj, t + 2)
                    last = V.tensor_tensor(xn[:, t:t + 2, :], xn[:, t:t + 2, :],
                                           ps[:, 4 + t // 2, :].rearrange("p (t d) -> p t d", t=2), ALU.add)
                link(last)
                link(norm.on_dve(dve, link, xn, xl))
                link(V.tensor_tensor(x[:], x[:], xl[:], ALU.add))


def expert_choice(core, ins):
    nc, sem, norm, x, ps = core.nc, core.sem, core.norm, core.x, core.ps
    E = 16
    K = N // E
    W = D + E
    core.late_weights(ins)
    with ExitStack() as own:
        def sb(name, shape):
            return own.enter_context(nc.sbuf_tensor(name, shape, F32))

        xf = sb("xf", [P, NT, D])
        xf_t = sb("xf_t", [P, C, N])
        z = sb("z", [P, NT, D])
        logits = sb("logits", [P, NT, E])
        low = sb("logit_max", [P, NT])
        total = sb("exp_sum", [P, NT])
        probs = sb("probs", [P, NT, E])
        probs_t = sb("probs_t", [E, N])
        left = sb("left", [E, N])
        best = sb("best", [E, 8])
        chosen = sb("chosen", [E, N])
        g = sb("g", [P, NT])
        xf_ready, xf_turned, xf_kept = sem("xf_ready"), sem("xf_turned"), sem("xf_kept")
        z_done, z_kept, logits_kept = sem("z_done"), sem("z_kept"), sem("logits_kept")
        exp_in, exp_out, probs_ready = sem("exp_in"), sem("exp_out"), sem("probs_ready")
        probs_turned, probs_kept, chosen_ready, g_done = (sem("probs_turned"), sem("probs_kept"),
                                                          sem("chosen_ready"), sem("g_done"))
        with nc.Block() as block:

            @block.sync
            def _(sp):
                core.prefetch_late(sp)

            @block.tensor
            def _(pe):
                pe.wait_ge(core.w_in, core.w_in_total)
                pe.wait_ge(xf_ready, 1)
                for b in range(B):
                    for c in range(C):
                        for t in range(TB):
                            last = nc.tensor.transpose(ps[:, 2 * b + c, t * P:(t + 1) * P],
                                                       xf[:, b * TB + t, c * P:(c + 1) * P], core.ident[:])
                        last.then_inc(xf_turned, 1)
                for n in range(NT):
                    t = (n + 4) % NT
                    pe.wait_ge(xf_kept, 4 if n >= 4 or t >= 4 else 2)
                    for c in range(C):
                        nc.tensor.matmul(ps[:, t, 0:W], xf_t[:, c, t * P:(t + 1) * P], core.w_ec[:, c, :],
                                         start=c == 0, stop=False)
                    nc.tensor.matmul(ps[:, t, 0:W], core.ones[0:1, :], core.b_ec[:], start=False, stop=True) \
                        .then_inc(z_done, 1)
                pe.wait_ge(probs_ready, 1)
                pe.wait_ge(z_kept, NT)
                for t in range(NT):
                    last = nc.tensor.transpose(ps[0:E, t // 4, (t % 4) * P:(t % 4 + 1) * P], probs[:, t, :],
                                               core.ident[:])
                last.then_inc(probs_turned, 1)
                pe.wait_ge(chosen_ready, 1)
                for t in range(NT):
                    last = nc.tensor.matmul(ps[:, 2, t:t + 1], chosen[:, t * P:(t + 1) * P], core.ones[0:E, 0:1],
                                            start=True, stop=True)
                last.then_inc(g_done, 1)

            @block.scalar
            def _(act):
                norm.on_act(act, core.ln_eps[:])
                for b in range(B):
                    for c in range(C):
                        act.wait_ge(xf_turned, 2 * b + c + 1)
                        nc.scalar.copy(xf_t[:, c, b * T:(b + 1) * T], ps[:, 2 * b + c, :]).then_inc(xf_kept, 1)
                for n in range(NT):
                    t = (n + 4) % NT
                    act.wait_ge(logits_kept, n + 1)
                    nc.scalar.copy(z[:, t, :], ps[:, t, 0:D]).then_inc(z_kept, 1)
                act.wait_ge(exp_in, 1)
                nc.scalar.activation(probs[:], logits[:], ACT.Exp).then_inc(exp_out, 1)
                norm.on_act(act, core.ln_eps[:])

            @block.vector
            def _(dve):
                V = nc.vector
                link = chain(dve, sem("dve_order"), core.dve_count)
                norm.on_dve(dve, link, x, xf).then_inc(xf_ready, 1)
                for n in range(NT):
                    t = (n + 4) % NT
                    dve.wait_ge(z_done, n + 1)
                    V.tensor_copy(logits[:, t, :], ps[:, t, D:W]).then_inc(logits_kept, 1)
                dve.wait_ge(logits_kept, NT)
                link(V.tensor_reduce(low[:], logits[:], AX_X, ALU.max))
                V.tensor_tensor(logits[:], logits[:], low[:].unsqueeze(2).to_broadcast([P, NT, E]),
                                ALU.subtract).then_inc(exp_in, 1)
                dve.wait_ge(exp_out, 1)
                link(V.tensor_reduce(total[:], probs[:], AX_X, ALU.add))
                link(V.reciprocal(total[:], total[:]))
                V.tensor_tensor(probs[:], probs[:], total[:].unsqueeze(2).to_broadcast([P, NT, E]),
                                ALU.mult).then_inc(probs_ready, 1)
                dve.wait_ge(probs_turned, 1)
                link(V.tensor_copy(probs_t[:], ps[0:E, 0:2, :].rearrange("p a b -> p (a b)")))
                for n in range(0, K, 8):
                    src = probs_t if n == 0 else left
                    link(V.max(best[:], src[:]))
                    link(V.match_replace(left[:], best[:], src[:], 0.0))
                V.tensor_tensor(chosen[:], probs_t[:], left[:], ALU.subtract).then_inc(chosen_ready, 1)
                dve.wait_ge(g_done, 1)
                link(V.tensor_copy(g[:], ps[:, 2, 0:NT]))
                dve.wait_ge(z_kept, NT)
                for t in range(NT):
                    last = V.tensor_scalar(z[:, t, :], z[:, t, :], g[:, t:t + 1], None, ALU.mult)
                link(last)
                link(norm.on_dve(dve, link, z, xf))
                link(V.tensor_tensor(x[:], x[:], xf[:], ALU.add))


def delta_attention(core, ins):
    nc, sem, norm, x, ps, ident = core.nc, core.sem, core.norm, core.x, core.ps, core.ident
    H, DK, CH = 16, 16, 32
    G = P // CH
    HH = H // C
    NCH = T // CH
    TAPS = 4
    X_, Q_, K_, V_ = range(4)

    outer = ExitStack()

    def place(stack):
        return lambda name, shape: stack.enter_context(nc.sbuf_tensor(name, shape, F32))

    with outer:
        sb = place(outer)
        kv = sb("kv", [P, NT, 2, H, DK])
        q_t = sb("q_t", [P, C, N])
        k_t = sb("k_t", [P, C, N])
        beta = sb("beta", [P, NT, H])
        qk_t = sb("qk_t", [P, NT, H, CH])

        xa_ready, conv_done, conv_kept = sem("xa_ready"), sem("conv_done"), sem("conv_kept")
        conv_kept_dve = sem("conv_kept_dve")
        qkv_done, silu_done, beta_done = sem("qkv_done"), sem("silu_done"), sem("beta_done")
        ss_ready, ss_root, kq_ready = sem("ss_ready"), sem("ss_root"), sem("kq_ready")
        kq_turned, k_kept, q_kept = sem("kq_turned"), sem("k_kept"), sem("q_kept")
        with ExitStack() as stage:
            sb = place(stage)
            xa = sb("xa", [P, NT, D])
            xc = sb("xc", [P, C, 4, N])
            qk = sb("qk", [P, NT, 2, D])
            sq = sb("sq", [P, NT, 2, D])
            ss = sb("ss", [P, NT, 2 * H])
            with nc.Block() as block:

                @block.tensor
                def _(pe):
                    pe.wait_ge(xa_ready, 1)
                    for t in range(NT):
                        for c in range(C):
                            n = 2 * t + c
                            if n >= 8:
                                pe.wait_ge((conv_kept, conv_kept_dve)[c], t - 3)
                            lead = t % TB == 0
                            last = nc.tensor.matmul(ps[:, n % 8, :], xa[:, t, c * P:(c + 1) * P],
                                                    core.conv[:, :, 0:P], start=True, stop=lead)
                            if not lead:
                                out = ps[:, n % 8, :].rearrange("p (k t) -> p k t", k=4)[:, 1:4, 0:TAPS - 1]
                                last = nc.tensor.matmul(out, xa[:, t - 1, c * P:(c + 1) * P],
                                                        core.conv[:, 1:4, P:P + TAPS - 1], start=False, stop=True)
                            last.then_inc(conv_done, 1)
                    for t in range(NT):
                        pe.wait_ge(conv_kept, NT)
                        pe.wait_ge(conv_kept_dve, NT)
                        if t >= 4:
                            pe.wait_ge(silu_done, 3 * (t - 3))
                        bank = 2 * (t % 4)
                        tok = slice(t * P, (t + 1) * P)
                        for out, src, w in ((ps[:, bank, 0:D], Q_, core.w_qkv[:, 0]),
                                            (ps[:, bank, D:], K_, core.w_qkv[:, 1]),
                                            (ps[:, bank + 1, 0:D], V_, core.w_qkv[:, 2]),
                                            (ps[:, bank + 1, D:D + H], X_, core.w_beta[:])):
                            for c in range(C):
                                last = nc.tensor.matmul(out, xc[:, c, src, tok], w[:, c, :], start=c == 0,
                                                        stop=c == C - 1)
                        last.then_inc(qkv_done, 1)
                    pe.wait_ge(silu_done, 3 * NT)
                    for b in range(B):
                        pe.wait_ge(kq_ready, 2 * (b + 1))
                        for which in range(2):
                            for c in range(C):
                                bank = 4 * which + 2 * b + c
                                for t in range(TB):
                                    tt = b * TB + t
                                    src = (kv[:, tt, 0, c * HH:(c + 1) * HH, :].rearrange("p h d -> p (h d)"),
                                           qk[:, tt, 0, c * P:(c + 1) * P])[which]
                                    last = nc.tensor.transpose(ps[:, bank, t * P:(t + 1) * P], src, ident[:])
                                last.then_inc(kq_turned, 1)

                @block.scalar
                def _(act):
                    a = nc.scalar.activation
                    norm.on_act(act, core.ln_eps[:])
                    for t in range(NT):
                        act.wait_ge(conv_done, 2 * t + 1)
                        nc.scalar.copy(xc[:, 0, :, t * P:(t + 1) * P],
                                       ps[:, 2 * t % 8, :].rearrange("p (k t) -> p k t", k=4)).then_inc(conv_kept, 1)
                    for t in range(NT):
                        bank = 2 * (t % 4)
                        act.wait_ge(qkv_done, t + 1)
                        a(qk[:, t].rearrange("p a d -> p (a d)"), ps[:, bank, :], ACT.Silu).then_inc(silu_done, 1)
                        a(kv[:, t, 1], ps[:, bank + 1, 0:D].rearrange("p (h d) -> p h d", h=H),
                          ACT.Silu).then_inc(silu_done, 1)
                        nc.scalar.copy(beta[:, t, :], ps[:, bank + 1, D:D + H]).then_inc(silu_done, 1)
                    act.wait_ge(silu_done, 3 * NT)
                    a(beta[:], beta[:], ACT.Sigmoid).then_inc(beta_done, 1)
                    for b in range(B):
                        act.wait_ge(ss_ready, b + 1)
                        a(ss[:, b * TB:(b + 1) * TB], ss[:, b * TB:(b + 1) * TB], ACT.Sqrt,
                          bias=core.l2_eps[:]).then_inc(ss_root, 1)
                    for b in range(B):
                        for c in range(C):
                            act.wait_ge(kq_turned, 4 * b + c + 1)
                            nc.scalar.copy(k_t[:, c, b * T:(b + 1) * T], ps[:, 2 * b + c, :]).then_inc(k_kept, 1)

                @block.vector
                def _(dve):
                    V = nc.vector
                    link = chain(dve, sem("dve_order"), core.dve_count)
                    norm.on_dve(dve, link, x, xa).then_inc(xa_ready, 1)
                    for t in range(NT):
                        dve.wait_ge(conv_done, 2 * t + 2)
                        V.tensor_copy(xc[:, 1, :, t * P:(t + 1) * P],
                                      ps[:, (2 * t + 1) % 8, :].rearrange("p (k t) -> p k t", k=4)) \
                            .then_inc(conv_kept_dve, 1)
                    for b in range(B):
                        own = slice(b * TB, (b + 1) * TB)
                        for t in range(b * TB, (b + 1) * TB):
                            dve.wait_ge(silu_done, 3 * t + 1)
                            last = V.tensor_tensor(sq[:, t], qk[:, t], qk[:, t], ALU.mult)
                        link(last)
                        V.tensor_reduce(ss[:, own], sq[:, own].rearrange("p t a (h d) -> p t (a h) d", h=H), AX_X,
                                        ALU.add).then_inc(ss_ready, 1)
                        dve.wait_ge(ss_root, b + 1)
                        link(V.reciprocal(ss[:, own], ss[:, own]))
                        link(V.tensor_scalar(ss[:, own, 0:H], ss[:, own, 0:H], float(DK) ** -0.5, None, ALU.mult))
                        for t in range(b * TB, (b + 1) * TB):
                            rows = qk[:, t].rearrange("p a (h d) -> p a h d", h=H)
                            last_k = V.tensor_tensor(kv[:, t, 0], rows[:, 1],
                                                     ss[:, t, H:].unsqueeze(2).to_broadcast([P, H, DK]), ALU.mult)
                            last_q = V.tensor_tensor(rows[:, 0], rows[:, 0],
                                                     ss[:, t, 0:H].unsqueeze(2).to_broadcast([P, H, DK]), ALU.mult)
                        last_k.then_inc(kq_ready, 1)
                        last_q.then_inc(kq_ready, 1)
                    for b in range(B):
                        for c in range(C):
                            dve.wait_ge(kq_turned, 4 * b + 2 + c + 1)
                            V.tensor_copy(q_t[:, c, b * T:(b + 1) * T], ps[:, 4 + 2 * b + c, :]).then_inc(q_kept, 1)

        n_t = outer.enter_context(nc.sbuf_tensor("n_t", [P, NT, H, CH], F32))
        zeroed, spread = sem("kbd_zeroed"), sem("kbd_spread")
        pair_done, n_masked, qk_flipped = sem("pair_done"), sem("n_masked"), sem("qk_flipped")
        pool_order = sem("pool_order")
        with ExitStack() as stage:
            sb = place(stage)
            kbd = sb("kbd", [P, C, HH, N])
            with nc.Block() as block:

                @block.gpsimd
                def _(pool):
                    nc.gpsimd.memset(kbd[:, 0], 0.0).then_inc(zeroed, 1)
                    for t in range(NT):
                        for c in range(C):
                            hs = slice(c * HH, (c + 1) * HH)
                            pool.wait_ge(n_masked, C * t + c + 1)
                            nc.gpsimd.tensor_tensor(n_t[:, t, hs], n_t[:, t, hs],
                                                    beta[:, t, hs].unsqueeze(2).to_broadcast([P, HH, CH]),
                                                    ALU.mult).then_inc(pool_order, 1)

                @block.sync
                def _(sp):
                    for c in range(C):
                        sp.wait_ge(zeroed, 1)
                        sp.wait_ge(sem("kbd_zeroed_dve"), 1)
                        for h in range(HH):
                            rows = slice(h * DK, (h + 1) * DK)
                            sp.dma_start(kbd[rows, c, h, :], k_t[rows, c, :]).then_inc(spread, 16)

                @block.tensor
                def _(pe):
                    for t in range(NT):
                        for c in range(C):
                            n = C * t + c
                            pe.wait_ge(spread, 16 * C * HH)
                            if n >= 8:
                                pe.wait_ge(qk_flipped, n - 7)
                            for r in range(G):
                                tok = slice(t * P + r * CH, t * P + (r + 1) * CH)
                                for which, src in enumerate((k_t, q_t)):
                                    last = nc.tensor.matmul(
                                        ps[r * CH:(r + 1) * CH, n % 8, which * D:(which + 1) * D], src[:, c, tok],
                                        kbd[:, c, :, tok], start=True, stop=True, skip_group_check=True)
                            last.then_inc(pair_done, 1)

                @block.vector
                def _(dve):
                    V = nc.vector
                    link = chain(dve, sem("dve_order"), core.dve_count)
                    V.memset(kbd[:, 1], 0.0).then_inc(sem("kbd_zeroed_dve"), 1)
                    for t in range(NT):
                        for c in range(C):
                            n = C * t + c
                            hs = slice(c * HH, (c + 1) * HH)
                            dve.wait_ge(pair_done, n + 1)
                            V.tensor_tensor(n_t[:, t, hs],
                                            ps[:, n % 8, 0:D].rearrange("p (h i) -> p h i", h=HH),
                                            core.above[:].unsqueeze(1).to_broadcast([P, HH, CH]),
                                            ALU.mult).then_inc(n_masked, 1)
                            V.transpose(qk_t[:, t, hs].rearrange("p h i -> p (h i)"), ps[:, n % 8, D:]) \
                                .then_inc(qk_flipped, 1)
                    dve.wait_ge(qk_flipped, C * NT)
                    for t in range(NT):
                        last = V.tensor_tensor(qk_t[:, t], qk_t[:, t],
                                               core.upto[:].unsqueeze(1).to_broadcast([P, H, CH]), ALU.mult)
                    link(last)

        r_t = outer.enter_context(nc.sbuf_tensor("r_t", [P, NT * H, CH], F32))
        n_turned, n_kept, n_kept_dve = sem("n_turned"), sem("n_kept"), sem("n_kept_dve")
        eye_ready, inv_done, r_turned, r_kept = sem("eye_ready"), sem("inv_done"), sem("r_turned"), sem("r_kept")
        ROWS = 4
        with ExitStack() as stage:
            sb = place(stage)
            nm = sb("nm", [P, CH, G, CH])
            inv = sb("inv", [P, CH, G, CH])
            terms = sb("terms", [P, G, (CH - 1) * (CH - 1)])
            with nc.Block() as block:

                @block.gpsimd
                def _(pool):
                    nc.gpsimd.memset(inv[:], 0.0).then_inc(eye_ready, 1)
                    pool.wait_ge(eye_ready, 1)
                    nc.gpsimd.affine_select(out=inv[:], in_=inv[:], compare_op=ALU.not_equal, fill=1.0, base=0,
                                            pattern=[[1, CH], [0, G], [-1, CH]], channel_multiplier=0) \
                        .then_inc(eye_ready, 1)

                @block.tensor
                def _(pe):
                    cols = n_t[:].rearrange("p t h i -> p (t h) i")
                    for n in range(CH // ROWS):
                        for i in range(n * ROWS, (n + 1) * ROWS):
                            last = nc.tensor.transpose(ps[:, n, (i % ROWS) * P:(i % ROWS + 1) * P], cols[:, :, i],
                                                       ident[:])
                        last.then_inc(n_turned, 1)
                    for n in range(CH // ROWS):
                        pe.wait_ge(inv_done, n + 1)
                        if n == 0:
                            pe.wait_ge(n_kept, CH // ROWS)
                        for i in range(n * ROWS, (n + 1) * ROWS):
                            last = nc.tensor.transpose(ps[:, n, (i % ROWS) * P:(i % ROWS + 1) * P],
                                                       inv[:, i].rearrange("p g c -> p (g c)"), ident[:])
                        last.then_inc(r_turned, 1)

                @block.scalar
                def _(act):
                    for n in range(CH // ROWS):
                        act.wait_ge(n_turned, n + 1)
                        nc.scalar.copy(nm[:, n * ROWS:(n + 1) * ROWS].rearrange("p i g j -> p (i g j)"),
                                       ps[:, n, :]).then_inc(n_kept, 1)
                    for n in range(CH // ROWS):
                        act.wait_ge(r_turned, n + 1)
                        nc.scalar.copy(r_t[:, :, n * ROWS:(n + 1) * ROWS].rearrange("p h i -> p i h"),
                                       ps[:, n, :].rearrange("p (i h) -> p i h", i=ROWS)).then_inc(r_kept, 1)

                @block.vector
                def _(dve):
                    V = nc.vector
                    link = chain(dve, sem("dve_order"), core.dve_count)
                    dve.wait_ge(eye_ready, 2)
                    for i in range(1, CH):
                        dve.wait_ge(n_kept, i // ROWS + 1)
                        part = terms[:, :, 0:i * i].rearrange("p g (c j) -> p g c j", j=i)
                        link(V.tensor_tensor(part, inv[:, 0:i, :, 0:i].rearrange("p j g c -> p g c j"),
                                             nm[:, i, :, 0:i].unsqueeze(2).to_broadcast([P, G, i, i]), ALU.mult))
                        last = V.tensor_reduce(inv[:, i, :, 0:i], part, AX_X, ALU.add, negate=True)
                        if i % ROWS == ROWS - 1:
                            last.then_inc(inv_done, 1)
                            dve.wait_ge(inv_done, i // ROWS + 1)
                        else:
                            link(last)

        wu_done, wu_kept, wu_ready = sem("wu_done"), sem("wu_kept"), sem("wu_ready")
        w_turned, w_kept = sem("delta_w_turned"), sem("delta_w_kept")
        with ExitStack() as stage:
            sb = place(stage)
            wu = n_t[:].rearrange("p t h i -> p (t h i)").rearrange("p (t a h d) -> p t a h d", t=NT, a=2, h=H)
            w_t = k_t
            state = sb("state", [P, NCH, B, C, P])
            u = sb("u", [P, NT, H, DK])
            o = sb("o", [P, NT, H, DK])
            with nc.Block() as block:

                @block.tensor
                def _(pe):
                    for t in range(NT):
                        if t >= 2:
                            pe.wait_ge(wu_kept, G * (t - 1))
                        for h in range(H):
                            for r in range(G):
                                rows = slice(r * CH, (r + 1) * CH)
                                last = nc.tensor.matmul(ps[rows, G * (t % 2) + r, h * CH:(h + 1) * CH],
                                                        r_t[rows, t * H + h, :], kv[rows, t, :, h, :], start=True,
                                                        stop=True, skip_group_check=True)
                        last.then_inc(wu_done, 1)
                    for b in range(B):
                        pe.wait_ge(wu_ready, (b + 1) * TB)
                        pe.wait_ge(wu_kept, G * NT)
                        for c in range(C):
                            for t in range(TB):
                                last = nc.tensor.transpose(ps[:, 2 * b + c, t * P:(t + 1) * P],
                                                           wu[:, b * TB + t, 0, c * HH:(c + 1) * HH, :].rearrange("p h d -> p (h d)"), ident[:])
                            last.then_inc(w_turned, 1)

                @block.scalar
                def _(act):
                    for t in range(NT):
                        act.wait_ge(wu_done, t + 1)
                        for r in range(G):
                            rows = slice(r * CH, (r + 1) * CH)
                            nc.scalar.copy(wu[rows, t].rearrange("p a h d -> p h a d"),
                                           ps[rows, G * (t % 2) + r, :].rearrange("p (h a d) -> p h a d", h=H, a=2)) \
                                .then_inc(wu_kept, 1)
                    for n in range(B * C):
                        act.wait_ge(w_turned, n + 1)
                        nc.scalar.copy(w_t[:, n % C, (n // C) * T:(n // C + 1) * T], ps[:, n, :]).then_inc(w_kept, 1)

                @block.vector
                def _(dve):
                    V = nc.vector
                    V.memset(state[:, 0], 0.0).then_inc(sem("state_zeroed"), 1)
                    for t in range(NT):
                        dve.wait_ge(wu_kept, G * (t + 1))
                        V.tensor_tensor(wu[:, t], wu[:, t],
                                        beta[:, t].unsqueeze(1).unsqueeze(3).to_broadcast([P, 2, H, DK]), ALU.mult).then_inc(wu_ready, 1)

            ws_done, u_ready, ku_done, state_ready = (sem("ws_done"), sem("u_ready"), sem("ku_done"),
                                                      sem("state_ready"))
            with nc.Block() as block:
                @block.tensor
                def _(pe):
                    for n in range(NCH):
                        r = n % G
                        rows = slice(r * CH, (r + 1) * CH)
                        for phase in range(2):
                            for b in range(B):
                                t = b * TB + n // G
                                for c in range(C):
                                    q = C * b + c
                                    if phase == 0:
                                        if n:
                                            pe.wait_ge(state_ready, 4 * (n - 1) + q + 1)
                                        nc.tensor.matmul(ps[rows, q, 0:P],
                                                         w_t[:, c, b * T + n * CH:b * T + (n + 1) * CH],
                                                         state[:, n, b, c, :], start=True, stop=True,
                                                         skip_group_check=True).then_inc(ws_done, 1)
                                    elif n < NCH - 1:
                                        pe.wait_ge(u_ready, 4 * n + q + 1)
                                        nc.tensor.matmul(ps[:, 4 + q, 0:P], kv[rows, t, 0, c * HH:(c + 1) * HH, :].rearrange("p h d -> p (h d)"),
                                                         u[rows, t, c * HH:(c + 1) * HH, :], start=n == 0,
                                                         stop=n == NCH - 2, skip_group_check=True) \
                                            .then_inc(ku_done, 1)

                @block.vector
                def _(dve):
                    V = nc.vector
                    for n in range(NCH):
                        rows = slice((n % G) * CH, (n % G + 1) * CH)
                        for b in range(B):
                            t = b * TB + n // G
                            for c in range(C):
                                q = C * b + c
                                hs = slice(c * HH, (c + 1) * HH)
                                dve.wait_ge(ws_done, 4 * n + q + 1)
                                V.tensor_tensor(u[rows, t, hs], wu[rows, t, 1, hs],
                                                ps[rows, q, 0:P].rearrange("p (h e) -> p h e", h=HH),
                                                ALU.subtract).then_inc(u_ready, 1)
                        for b in range(B):
                            for c in range(C):
                                q = C * b + c
                                if n < NCH - 1:
                                    dve.wait_ge(ku_done, 4 * n + q + 1)
                                    V.tensor_tensor(state[:, n + 1, b, c, :], ps[:, 4 + q, 0:P], core.same_head[:],
                                                    ALU.mult).then_inc(state_ready, 1)

            qs_done, qs_kept, au_done, o_ready = sem("qs_done"), sem("qs_kept"), sem("au_done"), sem("o_ready")
            ms_ready, ms_root, on_ready = sem("ms_ready"), sem("ms_root"), sem("on_ready")
            o_turned, o_kept, wo_done, y_kept = sem("o_turned"), sem("o_kept"), sem("wo_done"), sem("y_kept")
            osq = wu[:, :, 0]
            ms = sb("ms", [P, NT, H])
            o_t = w_t
            y = u[:].rearrange("p t h e -> p t (h e)")
            yn = o[:].rearrange("p t h e -> p t (h e)")
            with nc.Block() as block:

                @block.tensor
                def _(pe):
                    for t in range(NT):
                        if t >= 4:
                            pe.wait_ge(qs_kept, t - 3)
                        for r in range(G):
                            for c in range(C):
                                n = (t % TB) * G + r
                                last = nc.tensor.matmul(ps[r * CH:(r + 1) * CH, t % 4, c * P:(c + 1) * P],
                                                        q_t[:, c, t * P + r * CH:t * P + (r + 1) * CH],
                                                        state[:, n, t // TB, c, :], start=True, stop=True,
                                                        skip_group_check=True)
                        last.then_inc(qs_done, 1)
                    for t in range(NT):
                        if t >= 1:
                            pe.wait_ge(o_ready, G * t)
                        for h in range(H):
                            for r in range(G):
                                rows = slice(r * CH, (r + 1) * CH)
                                last = nc.tensor.matmul(ps[rows, 4 + r, h * DK:(h + 1) * DK], qk_t[rows, t, h, :],
                                                        u[rows, t, h, :], start=True, stop=True,
                                                        skip_group_check=True)
                        last.then_inc(au_done, 1)
                    pe.wait_ge(qs_kept, NT)
                    for b in range(B):
                        pe.wait_ge(on_ready, b + 1)
                        for c in range(C):
                            for t in range(TB):
                                last = nc.tensor.transpose(ps[:, 2 * b + c, t * P:(t + 1) * P],
                                                           o[:, b * TB + t, c * HH:(c + 1) * HH, :].rearrange("p h e -> p (h e)"), ident[:])
                            last.then_inc(o_turned, 1)
                    for t in range(NT):
                        pe.wait_ge(o_kept, 2 * (t // TB) + 2)
                        for c in range(C):
                            last = nc.tensor.matmul(ps[:, 4 + t // 2, (t % 2) * D:(t % 2 + 1) * D],
                                                    o_t[:, c, t * P:(t + 1) * P], core.w_o[:, c, :], start=c == 0,
                                                    stop=c == C - 1)
                        last.then_inc(wo_done, 1)

                @block.scalar
                def _(act):
                    for t in range(NT):
                        act.wait_ge(qs_done, t + 1)
                        nc.scalar.copy(o[:, t].rearrange("p h e -> p (h e)"), ps[:, t % 4, 0:D]).then_inc(qs_kept, 1)
                    act.wait_ge(ms_ready, 1)
                    nc.scalar.activation(ms[:], ms[:], ACT.Sqrt, scale=1.0 / DK, bias=core.ln_eps[:]) \
                        .then_inc(ms_root, 1)
                    for n in range(B * C):
                        act.wait_ge(o_turned, n + 1)
                        nc.scalar.copy(o_t[:, n % C, (n // C) * T:(n // C + 1) * T], ps[:, n, :]).then_inc(o_kept, 1)
                    for t in range(0, NT, 2):
                        act.wait_ge(wo_done, t + 2)
                        nc.scalar.copy(y[:, t:t + 2].rearrange("p t d -> p (t d)"), ps[:, 4 + t // 2, :]) \
                            .then_inc(y_kept, 1)
                    norm.on_act(act, core.ln_eps[:])

                @block.vector
                def _(dve):
                    V = nc.vector
                    link = chain(dve, sem("dve_order"), core.dve_count)
                    for t in range(NT):
                        dve.wait_ge(qs_kept, t + 1)
                        dve.wait_ge(au_done, t + 1)
                        for r in range(G):
                            rows = slice(r * CH, (r + 1) * CH)
                            V.tensor_tensor(o[rows, t], o[rows, t],
                                            ps[rows, 4 + r, 0:D].rearrange("p (h e) -> p h e", h=H),
                                            ALU.add).then_inc(o_ready, 1)
                        dve.wait_ge(o_ready, G * (t + 1))
                        last = V.tensor_tensor(osq[:, t], o[:, t], o[:, t], ALU.mult)
                    link(last)
                    V.tensor_reduce(ms[:], osq, AX_X, ALU.add).then_inc(ms_ready, 1)
                    dve.wait_ge(ms_root, 1)
                    link(V.reciprocal(ms[:], ms[:]))
                    for b in range(B):
                        for t in range(b * TB, (b + 1) * TB):
                            last = V.tensor_tensor(o[:, t], o[:, t], ms[:, t].unsqueeze(2).to_broadcast([P, H, DK]),
                                                   ALU.mult)
                        link(last)
                        for t in range(b * TB, (b + 1) * TB):
                            last = V.tensor_tensor(o[:, t], o[:, t],
                                                   core.onorm[:].unsqueeze(1).to_broadcast([P, H, DK]), ALU.mult)
                        last.then_inc(on_ready, 1)
                    dve.wait_ge(y_kept, NT // 2)
                    link(norm.on_dve(dve, link, y, yn))
                    link(V.tensor_tensor(x[:], x[:], yn, ALU.add))


def expert_mixture(core, ins):
    nc, sem, norm, x, ps, ident = core.nc, core.sem, core.norm, core.x, core.ps, core.ident
    E = 8
    SH = core.SH
    HI, LO = 0, 1
    PRODUCTS = ((HI, HI), (HI, LO), (LO, HI))
    HID = SH + E
    with ExitStack() as own:
        def sb(name, shape, dt=F32):
            return own.enter_context(nc.sbuf_tensor(name, shape, dt))

        xm = sb("xm", [P, NT, D])
        gate_r = sb("gate_r", [P, 2, C, HID, P], F32R)
        up_r = sb("up_r", [P, 2, C, HID, P], F32R)
        down_r = sb("down_r", [P, 2, HID, D], F32R)
        xm_r = sb("xm_r", [P, 2, C, N], F32R)
        router_t = sb("router_t", [P, C, E])
        scores = sb("scores", [P, NT, E])
        select = sb("select", [P, NT, E])
        best = sb("best8", [P, NT, 8])
        where = sb("where", [P, NT, 8], U32)
        where_f = sb("where_f", [P, NT, 8])
        first = sb("first", [P, NT, E])
        second = sb("second", [P, NT, E])
        total = sb("score_sum", [P, NT])
        room = [0]

        def over(size):
            room[0] += size
            assert room[0] <= core.stored.shape[1]
            return core.stored[:, room[0] - size:room[0]]

        hidden = over(4 * T).rearrange("p (a t) -> p a t", a=4)
        xm_t = hidden.rearrange("p a t -> p (a t)").rearrange("p (c n) -> p c n", c=C)
        gated = over(2 * T).rearrange("p (a t) -> p a t", a=2)
        share_t = over(N)[0:E, :]
        share = over(E * N).rearrange("p (e n) -> p e n", e=E)
        hidden_r = sb("hidden_r", [P, 2, 2, T], F32R)
        y = xm

        xm_ready, xm_turned, xm_kept = sem("xm_ready"), sem("xm_turned"), sem("xm_kept")
        turned, kept_act, kept_dve = sem("ffn_w_turned"), sem("ffn_w_kept"), sem("ffn_w_kept_dve")
        router_turned, router_kept = sem("router_turned"), sem("router_kept")
        scores_done, scores_kept = sem("scores_done"), sem("scores_kept")
        share_ready, share_turned, share_t_kept = sem("share_ready"), sem("share_turned"), sem("share_t_kept")
        share_out, share_in = sem("share_out"), sem("share_in")
        up_done, silu_ready, prod_ready, hidden_ready = (sem("up_done"), sem("silu_ready"), sem("prod_ready"),
                                                         sem("hidden_ready"))
        xm_hi_kept, xm_lo_kept, hidden_hi, hidden_lo = (sem("xm_hi_kept"), sem("xm_lo_kept"), sem("hidden_hi"),
                                                        sem("hidden_lo"))
        down_done, y_ready = sem("down_done"), sem("y_ready")

        turns = []
        def flat(ap):
            return ap.rearrange("p a b -> p (a b)")

        groups = []
        for m, dst in ((core.sw1, gate_r), (core.sw2, up_r)):
            groups += [([m[:, a, c * P:(c + 1) * P] for a in range(a0, a0 + 4)],
                        [flat(dst[:, part, c, a0:a0 + 4, :]) for part in (HI, LO)])
                       for c in range(C) for a0 in range(0, SH, 4)]
        for half, dst in ((0, gate_r), (1, up_r)):
            groups += [([core.w12[:, 2 * e + half, c * P:(c + 1) * P] for e in range(e0, e0 + 4)],
                        [flat(dst[:, part, c, SH + e0:SH + e0 + 4, :]) for part in (HI, LO)])
                       for c in range(C) for e0 in range(0, E, 4)]
        groups += [([core.sw3[:, c, a * P:(a + 1) * P] for a in (a0, a0 + 1) for c in range(C)],
                    [flat(down_r[:, part, a0:a0 + 2, :]) for part in (HI, LO)]) for a0 in range(0, SH, 2)]
        groups += [([core.w3[:, e, c, :] for e in (e0, e0 + 1) for c in range(C)],
                    [flat(down_r[:, part, SH + e0:SH + e0 + 2, :]) for part in (HI, LO)])
                   for e0 in range(0, E, 2)]

        TURNED, STEPS = len(groups), B * HID
        LAG = 3

        def bank_of(n):
            return n if n < 8 else 4 + n % 4

        with nc.Block() as block:

            @block.tensor
            def _(pe):
                pe.wait_ge(core.f_in, core.f_in_total)
                def turn(n):
                    if n >= 8:
                        pe.wait_ge(kept_dve, n - 3)
                    for i, stored in enumerate(groups[n][0]):
                        last = nc.tensor.transpose(ps[:, bank_of(n), i * P:(i + 1) * P], stored, ident[:])
                    last.then_inc(turned, 1)

                for n in range(8):
                    turn(n)
                pe.wait_ge(kept_dve, 4)
                for c in range(C):
                    last = nc.tensor.transpose(ps[:, 3, c * E:(c + 1) * E], core.router[:, c * P:(c + 1) * P],
                                               ident[0:E, 0:E])
                last.then_inc(router_turned, 1)
                pe.wait_ge(xm_ready, 1)
                pe.wait_ge(router_kept, 1)
                for b in range(B):
                    for c in range(C):
                        for t in range(TB):
                            last = nc.tensor.transpose(ps[:, 2 * b + c, t * P:(t + 1) * P],
                                                       xm[:, b * TB + t, c * P:(c + 1) * P], ident[:])
                        last.then_inc(xm_turned, 1)
                pe.wait_ge(xm_kept, B * C)
                for t in range(NT):
                    for c in range(C):
                        last = nc.tensor.matmul(ps[:, 0, t * E:(t + 1) * E], xm_t[:, c, t * P:(t + 1) * P],
                                                router_t[:, c, :], start=c == 0, stop=c == C - 1)
                last.then_inc(scores_done, 1)
                for n in range(8, TURNED):
                    turn(n)
                pe.wait_ge(share_ready, 1)
                pe.wait_ge(scores_kept, 1)
                for t in range(NT):
                    last = nc.tensor.transpose(ps[0:E, 2 + t // TB, (t % TB) * P:(t % TB + 1) * P],
                                               first[:, t, :], ident[:])
                last.then_inc(share_turned, 1)

                def up(n):
                    b, a = n // HID, n % HID
                    bank = 4 + 2 * (n % 2)
                    if n == 0:
                        pe.wait_ge(kept_dve, TURNED)
                        pe.wait_ge(xm_lo_kept, B * C)
                    if n >= 2:
                        pe.wait_ge(prod_ready, n - 1)
                    for which, w in enumerate((gate_r, up_r)):
                        for i, (c, wp, xp) in enumerate((c, *parts) for c in range(C) for parts in PRODUCTS):
                            last = nc.tensor.matmul(ps[:, bank + which, :], w[:, wp, c, a, :],
                                                    xm_r[:, xp, c, b * T:(b + 1) * T], start=i == 0,
                                                    stop=i == C * len(PRODUCTS) - 1)
                        last.then_inc(up_done, 1)

                def down(n):
                    b, a = n // HID, n % HID
                    pe.wait_ge(hidden_lo, n + 1)
                    if n == 0:
                        pe.wait_ge(share_t_kept, 1)
                    if a == 0 and b:
                        pe.wait_ge(y_ready, b * TB)
                    for t in range(TB):
                        for i, (wp, hp) in enumerate(PRODUCTS):
                            last = nc.tensor.matmul(ps[:, t, 0:D], hidden_r[:, n % 2, hp, t * P:(t + 1) * P],
                                                    down_r[:, wp, a, :], start=a == 0 and i == 0,
                                                    stop=a == HID - 1 and i == len(PRODUCTS) - 1)
                    last.then_inc(down_done, 1)

                for n in range(STEPS + LAG):
                    if n < STEPS:
                        up(n)
                    if n >= LAG:
                        down(n - LAG)

            @block.scalar
            def _(act):
                a = nc.scalar.activation
                norm.on_act(act, core.ln_eps[:])
                def high_weights(n):
                    act.wait_ge(turned, n + 1)
                    nc.scalar.copy(groups[n][1][HI], ps[:, bank_of(n), :]).then_inc(kept_act, 1)

                for n in range(8):
                    high_weights(n)
                act.wait_ge(router_turned, 1)
                nc.scalar.copy(router_t[:].rearrange("p c e -> p (c e)"), ps[:, 3, 0:C * E]).then_inc(router_kept, 1)
                for n in range(B * C):
                    act.wait_ge(xm_turned, n + 1)
                    if n == 0:
                        act.wait_ge(kept_dve, 4)
                    own = (n % C, slice((n // C) * T, (n // C + 1) * T))
                    nc.scalar.copy(xm_t[:, own[0], own[1]], ps[:, n, :]).then_inc(xm_kept, 1)
                for n in range(B * C):
                    own = (n % C, slice((n // C) * T, (n // C + 1) * T))
                    act.wait_ge(xm_kept, n + 1)
                    nc.scalar.copy(xm_r[:, HI, own[0], own[1]], xm_t[:, own[0], own[1]]).then_inc(xm_hi_kept, 1)
                act.wait_ge(scores_done, 1)
                a(scores[:].rearrange("p t e -> p (t e)"), ps[:, 0, 0:NT * E], ACT.Sigmoid).then_inc(scores_kept, 1)
                for n in range(8, TURNED):
                    high_weights(n)

                def silu(n):
                    act.wait_ge(up_done, 2 * n + 1)
                    if n >= 2:
                        act.wait_ge(prod_ready, n - 1)
                    a(gated[:, n % 2, :], ps[:, 4 + 2 * (n % 2), :], ACT.Silu).then_inc(silu_ready, 1)

                def high(n):
                    b, i = n // HID, n % HID
                    if i < SH:
                        act.wait_ge(prod_ready, n + 1)
                    else:
                        act.wait_ge(hidden_ready, b * E + i - SH + 1)
                    if n >= 2:
                        act.wait_ge(down_done, n - 1)
                    nc.scalar.copy(hidden_r[:, n % 2, HI, :], hidden[:, n % 4, :]).then_inc(hidden_hi, 1)

                for n in range(STEPS + 1):
                    if n < STEPS:
                        silu(n)
                    if n >= 1:
                        high(n - 1)
                norm.on_act(act, core.ln_eps[:])

            @block.sync
            def _(sp):
                sp.wait_ge(share_t_kept, 1)
                sp.dma_start(core.share_dram, share_t).then_inc(share_out, 16)
                sp.wait_ge(share_out, 16)
                for e in range(E):
                    sp.dma_start(share[:, e, :], core.share_dram[e].partition_broadcast(P)).then_inc(share_in, 16)

            @block.gpsimd
            def _(pool):
                pool.wait_ge(share_in, 16 * E)
                for n in range(STEPS):
                    b, a = n // HID, n % HID
                    if a >= SH:
                        pool.wait_ge(prod_ready, n + 1)
                        nc.gpsimd.tensor_tensor(hidden[:, n % 4, :], hidden[:, n % 4, :],
                                                share[:, a - SH, b * T:(b + 1) * T], ALU.mult) \
                            .then_inc(hidden_ready, 1)
                    pool.wait_ge(hidden_hi, n + 1)
                    if n >= 2:
                        pool.wait_ge(down_done, n - 1)
                    nc.gpsimd.tensor_tensor(hidden_r[:, n % 2, LO, :], hidden[:, n % 4, :],
                                            hidden_r[:, n % 2, HI, :], ALU.subtract).then_inc(hidden_lo, 1)

            @block.vector
            def _(dve):
                V = nc.vector
                link = chain(dve, sem("dve_order"), core.dve_count)
                norm.on_dve(dve, link, x, xm).then_inc(xm_ready, 1)
                def low_weights(n):
                    dve.wait_ge(kept_act, n + 1)
                    V.tensor_tensor(groups[n][1][LO], ps[:, bank_of(n), :], groups[n][1][HI], ALU.subtract) \
                        .then_inc(kept_dve, 1)

                for n in range(8):
                    low_weights(n)
                for n in range(B * C):
                    own = (n % C, slice((n // C) * T, (n // C + 1) * T))
                    dve.wait_ge(xm_hi_kept, n + 1)
                    V.tensor_tensor(xm_r[:, LO, own[0], own[1]], xm_t[:, own[0], own[1]], xm_r[:, HI, own[0], own[1]],
                                    ALU.subtract).then_inc(xm_lo_kept, 1)
                dve.wait_ge(scores_kept, 1)
                link(V.tensor_tensor(select[:], scores[:], core.expert_bias[:].unsqueeze(1).to_broadcast([P, NT, E]),
                                     ALU.add))
                for t in range(NT):
                    last = V.max(best[:, t, :], select[:, t, :])
                link(last)
                for t in range(NT):
                    last = V.max_index(where[:, t, :], best[:, t, :], select[:, t, :])
                link(last)
                link(V.tensor_copy(where_f[:], where[:]))
                number = core.numbers[:].unsqueeze(1).to_broadcast([P, NT, E])
                V.tensor_tensor(first[:], number, where_f[:, :, 0:1].to_broadcast([P, NT, E]), ALU.is_equal)
                link(V.tensor_tensor(second[:], number, where_f[:, :, 1:2].to_broadcast([P, NT, E]), ALU.is_equal))
                link(V.tensor_tensor(first[:], first[:], second[:], ALU.add))
                link(V.tensor_tensor(first[:], first[:], scores[:], ALU.mult))
                link(V.tensor_reduce(total[:], first[:], AX_X, ALU.add))
                link(V.tensor_scalar(total[:], total[:], 1e-9, None, ALU.add))
                link(V.reciprocal(total[:], total[:]))
                V.tensor_tensor(first[:], first[:], total[:].unsqueeze(2).to_broadcast([P, NT, E]), ALU.mult) \
                    .then_inc(share_ready, 1)
                for n in range(8, TURNED):
                    low_weights(n)
                dve.wait_ge(share_turned, 1)
                V.tensor_copy(share_t, ps[0:E, 2:4, :].rearrange("p a b -> p (a b)")).then_inc(share_t_kept, 1)

                def keep_y(b):
                    dve.wait_ge(down_done, (b + 1) * HID)
                    for t in range(TB):
                        V.tensor_copy(y[:, b * TB + t, :], ps[:, t, 0:D]).then_inc(y_ready, 1)

                for n in range(STEPS):
                    if n >= 4:
                        dve.wait_ge(down_done, n - 3)
                    dve.wait_ge(silu_ready, n + 1)
                    dve.wait_ge(up_done, 2 * n + 2)
                    V.tensor_tensor(hidden[:, n % 4, :], gated[:, n % 2, :], ps[:, 4 + 2 * (n % 2) + 1, :], ALU.mult) \
                        .then_inc(prod_ready, 1)
                    if n == HID + LAG - 2:
                        keep_y(0)
                keep_y(1)
                dve.wait_ge(y_ready, NT)
                link(norm.on_dve(dve, link, y, y))
                link(V.tensor_tensor(x[:], x[:], y[:], ALU.add))


def sandwich(nc, ins, out):
    with ExitStack() as ctx:
        core = Core(nc, ctx)
        core.x = core.sb("x", [P, NT, D])
        core.ident = core.sb("ident", [P, P])
        core.ones = core.sb("ones", [P, P])
        core.ln_eps = core.sb("ln_eps", [P, 1])
        core.l2_eps = core.sb("l2_eps", [P, 1])
        core.ps = ctx.enter_context(nc.psum_tensor("ps", [P, 8, 512], F32))
        core.norm = Norm(core)
        core.dve_count = [0]
        core.weights(ins)
        for layer in (time_mixing, expert_choice, delta_attention, expert_mixture):
            layer(core, ins)
        stored = core.sem("stored")
        with nc.Block() as block:
            @block.sync
            def _(sp):
                sp.dma_start(tiles(out.rearrange("b t d -> (b t) d")), core.x[:]).then_inc(stored, 16)
                sp.wait_ge(stored, 16)


_INS = ["L0_attn_hidden_state", "L0_attn_ln_w", "L0_attn_ln_b", "L0_attn_Wk", "L0_attn_Wv", "L0_attn_Wr",
        "L0_attn_Wo", "L0_attn_mix_k", "L0_attn_mix_v", "L0_attn_mix_r", "L0_attn_time_decay",
        "L0_attn_current_token_weight", "L0_ffn_router_w", "L0_ffn_router_b", "L0_ffn_expert_w",
        "L0_ffn_expert_b", "L1_attn_Wq", "L1_attn_Wk", "L1_attn_Wv", "L1_attn_Wb", "L1_attn_Wo",
        "L1_attn_conv_q", "L1_attn_conv_k", "L1_attn_conv_v", "L1_attn_onorm_w", "L1_ffn_w12", "L1_ffn_w3",
        "L1_ffn_router_w", "L1_ffn_expert_bias", "L1_ffn_sw1", "L1_ffn_sw2", "L1_ffn_sw3"]


def kernel(**inputs):
    import numpy as _np
    import concourse.bacc as _bacc
    from concourse import mybir as _mybir
    from concourse.bass_utils import run_bass_kernel_spmd as _run

    nc = _bacc.Bacc("TRN2", target_bir_lowering=False, num_devices=1)
    arrays, ins = {}, {}
    for name in _INS:
        a = _np.ascontiguousarray(inputs[name])
        arrays[f"in_{name}_dram"] = a
        ins[name] = nc.dram_tensor(f"in_{name}_dram", a.shape, _mybir.dt.from_np(a.dtype),
                                   kind="ExternalInput").ap()
    out = nc.dram_tensor("out_0_dram", (B, T, D), F32, kind="ExternalOutput").ap()
    sandwich(nc, ins, out)
    r = _run(nc, [arrays], core_ids=[0])
    return r.results[0]["out_0_dram"]
```

```python
from contextlib import ExitStack

import concourse.bass as bass
from concourse import mybir

F32 = mybir.dt.float32
F32R = mybir.dt.float32r
U32 = mybir.dt.uint32
ALU = mybir.AluOpType
ACT = mybir.ActivationFunctionType
AX_X = mybir.AxisListType.X

P = 128
B, T, D = 2, 512, 256
N = B * T
NT = N // P
TB = T // P
C = D // P
LN_EPS = 1e-5


class Core:

    def __init__(self, nc, ctx):
        self.nc, self.ctx, self.named = nc, ctx, {}

    def sb(self, name, shape):
        return self.ctx.enter_context(self.nc.sbuf_tensor(name, shape, F32))

    def weights(self, ins):
        sb = self.sb
        self.w_ec = sb("w_ec", [P, C, D + 16])
        self.b_ec = sb("b_ec", [1, D + 16])
        self.w_in = self.sem("w_in")
        self.loads = [
            (self.w_ec[:, :, 0:D], ins["L0_ffn_expert_w"].rearrange("(c p) n -> p c n", p=P)),
            (self.w_ec[:, :, D:], ins["L0_ffn_router_w"].rearrange("(c p) n -> p c n", p=P)),
            (self.b_ec[:, 0:D], ins["L0_ffn_expert_b"].unsqueeze(0)),
            (self.b_ec[:, D:], ins["L0_ffn_router_b"].unsqueeze(0)),
        ]
        self.w_qkv = sb("w_qkv", [P, 3, C, D])
        self.w_beta = sb("w_beta", [P, C, 16])
        self.w_o = sb("w_o", [P, C, D])
        self.conv_w = sb("conv_w", [P, 3, 4])
        self.onorm = sb("onorm", [P, 16])
        for n, name in enumerate("qkv"):
            self.loads += [
                (self.w_qkv[:, n], ins["L1_attn_W" + name].rearrange("(c p) n -> p c n", p=P)),
                (self.conv_w[:, n], ins["L1_attn_conv_" + name].partition_broadcast(P)),
            ]
        self.loads += [
            (self.w_beta[:], ins["L1_attn_Wb"].rearrange("(c p) n -> p c n", p=P)),
            (self.w_o[:], ins["L1_attn_Wo"].rearrange("(c p) n -> p c n", p=P)),
            (self.onorm[:], ins["L1_attn_onorm_w"].partition_broadcast(P)),
        ]
        self.conv = sb("conv", [P, 4, P + 3])
        self.taps = sb("taps", [P, 4, P + 3])
        self.scratch = sb("taps_scaled", [P, 3, P + 3])
        self.above = sb("above", [P, 32])
        self.upto = sb("upto", [P, 32])
        self.same_of_pair = sb("same_of_pair", [P, 32])
        self.numbers = sb("numbers", [P, 8])
        self.w_in_total = 16 * len(self.loads)

    def late_weights(self, ins):
        sb = self.sb
        E, self.SH = 8, 1024 // P
        self.stored = sb("stored", [P, 6 * self.SH * D])
        tile = self.SH * D

        def part(n, size, split, **sizes):
            return self.stored[:, n * tile:(n + size) * tile].rearrange(split, **sizes)

        self.sw1 = part(0, 1, "p (a d) -> p a d", d=D)
        self.sw2 = part(1, 1, "p (a d) -> p a d", d=D)
        self.w12 = part(2, 2, "p (a d) -> p a d", d=D)
        self.sw3 = part(4, 1, "p (c h) -> p c h", c=C)
        self.w3 = part(5, 1, "p (e c h) -> p e c h", e=E, c=C)
        self.router = sb("router", [E, D])
        self.expert_bias = sb("expert_bias", [P, E])
        self.f_in = self.sem("f_in")
        self.share_dram = self.nc.dram_tensor("share_dram", (E, N), F32, kind="Internal").ap()
        self.ffn_loads = [
            (self.sw1, ins["L1_ffn_sw1"].rearrange("(a p) d -> p a d", p=P)),
            (self.sw2, ins["L1_ffn_sw2"].rearrange("(a p) d -> p a d", p=P)),
            (self.w12, ins["L1_ffn_w12"].rearrange("e (a p) d -> p (e a) d", p=P)),
            (self.sw3, ins["L1_ffn_sw3"].rearrange("(c p) h -> p c h", p=P)),
            (self.w3, ins["L1_ffn_w3"].rearrange("e (c p) h -> p e c h", p=P)),
            (self.router[:], ins["L1_ffn_router_w"]),
            (self.expert_bias[:], ins["L1_ffn_expert_bias"].partition_broadcast(P)),
        ]
        self.f_in_total = 16 * len(self.ffn_loads)

    def prefetch_late(self, sp):
        for place, source in self.ffn_loads:
            sp.dma_start(place, source).then_inc(self.f_in, 16)

    def prefetch(self, sp):
        for place, source in self.loads:
            sp.dma_start(place, source).then_inc(self.w_in, 16)

    def masks(self, pool, order):
        g = self.nc.gpsimd
        count = [0]

        def link(ins):
            count[0] += 1
            ins.then_inc(order, 1)
            pool.wait_ge(order, count[0])

        def where(dst, op, fill, base, pattern, step):
            link(g.affine_select(out=dst, in_=dst, compare_op=op, fill=fill, base=base, pattern=pattern,
                                 channel_multiplier=step))

        for e in range(8):
            link(g.memset(self.numbers[:, e:e + 1], float(e)))
        for m in (self.above, self.upto, self.same_of_pair):
            link(g.memset(m[:], 1.0))
        for r in range(4):
            rows = slice(32 * r, 32 * r + 32)
            where(self.above[rows], ALU.is_gt, 0.0, 0, [[1, 32]], -1)
            where(self.upto[rows], ALU.is_ge, 0.0, 0, [[1, 32]], -1)
        for r in range(4):
            by_head = self.same_of_pair[32 * r:32 * r + 32].rearrange("p (h e) -> p h e", h=2)
            where(by_head, ALU.is_ge, 0.0, 0, [[-16, 2], [0, 16]], 1)
            where(by_head, ALU.is_ge, 0.0, 15, [[16, 2], [0, 16]], -1)
        link(g.memset(self.taps[:], 0.0))
        for d in range(4):
            where(self.taps[:, d], ALU.not_equal, 1.0, -d, [[1, P + 3]], -1)
        link(g.tensor_copy(self.conv[:, 0], self.taps[:, 0]))
        pool.wait_ge(self.w_in, self.w_in_total)
        for n in range(3):
            link(g.tensor_scalar(self.conv[:, 1 + n], self.taps[:, 3], self.conv_w[:, n, 0:1], 0.0, ALU.mult,
                                 ALU.add))
        for d in (2, 1, 0):
            for n in range(3):
                link(g.tensor_scalar(self.scratch[:, n], self.taps[:, d], self.conv_w[:, n, 3 - d:4 - d], 0.0,
                                     ALU.mult, ALU.add))
            for n in range(3):
                link(g.tensor_tensor(self.conv[:, 1 + n], self.conv[:, 1 + n], self.scratch[:, n], ALU.add))

    def sem(self, name):
        if name not in self.named:
            self.named[name] = self.ctx.enter_context(self.nc.semaphore(name))
        return self.named[name]


def chain(eng, sem, count):
    def link(ins):
        count[0] += 1
        ins.then_inc(sem, 1)
        eng.wait_ge(sem, count[0])
    return link


def tiles(dram):
    return dram.rearrange("(t p) d -> p t d", p=P)


class Norm:

    def __init__(self, core):
        sb = core.sb
        self.nc, self.done = core.nc, [0, 0]
        self.stats = sb("ln_stats", [P, NT, 6])
        self.mv = sb("ln_mean_var", [P, NT, 2])
        self.std = sb("ln_std_dev", [P, NT])
        self.inv = sb("ln_inverse_std", [P, NT])
        self.var_ready, self.std_ready = core.sem("ln_var"), core.sem("ln_std")

    def on_act(self, act, eps):
        self.done[1] += 1
        act.wait_ge(self.var_ready, self.done[1])
        self.nc.scalar.activation(self.std[:], self.mv[:, :, 1], ACT.Sqrt, bias=eps).then_inc(self.std_ready, 1)

    def on_dve(self, dve, link, src, dst):
        v = self.nc.vector
        self.done[0] += 1
        for t in range(NT):
            last = v.bn_stats(self.stats[:, t, :], src[:, t, :])
        link(last)
        for t in range(NT):
            last = v.bn_aggr(self.mv[:, t, :], self.stats[:, t, :])
        last.then_inc(self.var_ready, 1)
        dve.wait_ge(self.std_ready, self.done[0])
        link(v.reciprocal(self.inv[:], self.std[:]))
        for t in range(NT):
            last = v.tensor_scalar(dst[:, t, :], src[:, t, :], self.mv[:, t, 0:1], self.inv[:, t:t + 1],
                                   ALU.subtract, ALU.mult)
        return last


def time_mixing(core, ins):
    nc, sem, norm, x = core.nc, core.sem, core.norm, core.x
    KEY, VALUE, GATE, OUT = range(4)
    with ExitStack() as own:
        def sb(name, shape):
            return own.enter_context(nc.sbuf_tensor(name, shape, F32))

        w_nat = sb("w_nat", [P, 4, C, D])
        w_t = sb("w_t", [P, 4, C, D])
        vec = sb("vec", [P, 7, C])
        vec_rows = sb("vec_rows", [7 * C, P])
        decay = sb("decay", [P, C])
        xn = sb("xn", [P, NT, D])
        xl = sb("xl", [P, NT, D])
        xs = sb("xs", [P, C, B, T + 1])
        diff = sb("diff", [P, C, B, T])
        mixed = sb("mixed", [P, 3, C, B, T])
        k = sb("k", [P, C, B, T])
        v = sb("v", [P, C, B, T])
        r = sb("r", [P, C, B, T])
        top = sb("top", [P, C, B, T + 1])
        num = sb("num", [P, C, B, T + 1])
        den = sb("den", [P, C, B, T + 1])
        ea = sb("ea", [P, C, B, T])
        eb = sb("eb", [P, C, B, T])
        ec = w_nat[:].rearrange("p i c h -> p (i c h)").rearrange("p (c b t) -> p c b t", c=C, b=B)
        ed = xl[:].rearrange("p t d -> p (t d)").rearrange("p (c b t) -> p c b t", c=C, b=B)
        LN_W, LN_B, MIX_K, MIX_V, MIX_R, DECAY, BONUS = range(7)
        BEFORE = -3.0e38

        x_in, w_in, vec_in = sem("x_in"), sem("wkv_w_in"), sem("wkv_vec_in")
        vec_turned, vec_kept = sem("wkv_vec_turned"), sem("wkv_vec_kept")
        w_turned, w_kept = sem("wkv_w_turned"), sem("wkv_w_kept")
        xl_ready, xl_turned, xs_ready = sem("xl_ready"), sem("xl_turned"), sem("xs_ready")
        mix_ready, proj, kv_kept, r_kept = sem("mix_ready"), sem("wkv_proj"), sem("kv_kept"), sem("r_kept")
        decay_exp = sem("decay_exp")
        d_ready, cur_prev_exp, scaled_ready, scan_exp = (sem("bonus_diff"), sem("bonus_exp"), sem("scan_diff"),
                                                         sem("scan_exp"))
        rw_ready, rw_proj = sem("rw_ready"), sem("rw_proj")
        ps = core.ps
        hidden = ins["L0_attn_hidden_state"].rearrange("b t d -> (b t) d")

        with nc.Block() as block:

            @block.sync
            def _(sp):
                for t in range(0, NT, 2):
                    sp.dma_start(x[:, t:t + 2, :], tiles(hidden)[:, t:t + 2, :]).then_inc(x_in, 16)
                for i, name in enumerate(["ln_w", "ln_b", "mix_k", "mix_v", "mix_r", "time_decay",
                                          "current_token_weight"]):
                    sp.dma_start(vec_rows[C * i:C * i + C, :], ins["L0_attn_" + name].rearrange("(c p) -> c p", p=P)) \
                        .then_inc(vec_in, 16)
                core.prefetch(sp)

            @block.gpsimd
            def _(pool):
                for i, name in enumerate(["Wk", "Wv", "Wr", "Wo"]):
                    pool.dma_start(w_nat[:, i], ins["L0_attn_" + name].rearrange("(c p) h -> p c h", p=P)) \
                        .then_inc(w_in, 16)
                made = sem("pool_made")
                nc.gpsimd.memset(core.ident[:], 0.0).then_inc(made, 1)
                pool.wait_ge(made, 1)
                nc.gpsimd.affine_select(out=core.ident[:], in_=core.ident[:], compare_op=ALU.not_equal, fill=1.0,
                                        base=0, pattern=[[-1, P]], channel_multiplier=1).then_inc(made, 1)
                nc.gpsimd.memset(core.ones[:], 1.0).then_inc(made, 1)
                nc.gpsimd.memset(core.ln_eps[:], LN_EPS).then_inc(made, 1)
                nc.gpsimd.memset(core.l2_eps[:], 1e-6).then_inc(made, 1)
                nc.gpsimd.memset(xs[:, :, :, 0:1], 0.0).then_inc(made, 1)
                nc.gpsimd.memset(top[:, :, :, 0:1], BEFORE).then_inc(made, 1)
                nc.gpsimd.memset(num[:, :, :, 0:1], 0.0).then_inc(made, 1)
                nc.gpsimd.memset(den[:, :, :, 0:1], 0.0).then_inc(made, 1)
                core.masks(pool, sem("masks_order"))

            @block.tensor
            def _(pe):
                pe.wait_ge(sem("pool_made"), 2)
                for i in range(4):
                    pe.wait_ge(w_in, 64)
                    for h in range(C):
                        for o in range(C):
                            last = nc.tensor.transpose(ps[:, i, h * D + o * P:h * D + (o + 1) * P],
                                                       w_nat[:, i, o, h * P:(h + 1) * P], core.ident[:])
                    last.then_inc(w_turned, 1)
                pe.wait_ge(vec_in, 7 * 16)
                nc.tensor.transpose(ps[:, 4, 0:7 * C], vec_rows[:], core.ident[0:7 * C, 0:7 * C]).then_inc(vec_turned, 1)
                pe.wait_ge(vec_kept, 1)
                pe.wait_ge(xl_ready, 1)
                for b in range(B):
                    for c in range(C):
                        for t in range(TB):
                            last = nc.tensor.transpose(ps[:, 4 + 2 * b + c, t * P:(t + 1) * P],
                                                       xl[:, b * TB + t, c * P:(c + 1) * P], core.ident[:])
                    last.then_inc(xl_turned, 1)
                pe.wait_ge(w_kept, 4)
                pe.wait_ge(xs_ready, 4)
                for i in (KEY, VALUE, GATE):
                    pe.wait_ge(mix_ready, i + 1)
                    if i == GATE:
                        pe.wait_ge(kv_kept, 4)
                    for o in range(C):
                        for b in range(B):
                            bank = 4 * (i % 2) + 2 * o + b
                            for c in range(C):
                                last = nc.tensor.matmul(ps[:, bank, :], w_t[:, i, c, o * P:(o + 1) * P],
                                                        mixed[:, i, c, b, :], start=c == 0, stop=c == C - 1)
                            last.then_inc(proj, 1)
                pe.wait_ge(rw_ready, 2)
                for t in range(NT):
                    bank = 4 + t // 2
                    for c in range(C):
                        last = nc.tensor.matmul(ps[:, bank, (t % 2) * D:(t % 2 + 1) * D],
                                                r[:, c, t // TB, (t % TB) * P:(t % TB + 1) * P],
                                                w_t[:, OUT, c, :], start=c == 0, stop=c == C - 1)
                    last.then_inc(rw_proj, 1)

            @block.scalar
            def _(act):
                a = nc.scalar.activation
                act.wait_ge(sem("pool_made"), 4)
                for i in range(4):
                    act.wait_ge(w_turned, i + 1)
                    nc.scalar.copy(w_t[:, i].rearrange("p c o -> p (c o)"), ps[:, i, :]).then_inc(w_kept, 1)
                act.wait_ge(vec_turned, 1)
                nc.scalar.copy(vec[:].rearrange("p i c -> p (i c)"), ps[:, 4, 0:7 * C]).then_inc(vec_kept, 1)
                norm.on_act(act, core.ln_eps[:])
                norm.on_act(act, core.ln_eps[:])
                act.wait_ge(vec_kept, 1)
                for b in range(B):
                    act.wait_ge(xl_turned, b + 1)
                    for c in range(C):
                        a(xs[:, c, b, 1:], ps[:, 4 + 2 * b + c, :], ACT.Identity, scale=vec[:, LN_W, c:c + 1],
                          bias=vec[:, LN_B, c:c + 1]).then_inc(xs_ready, 1)
                a(decay[:], vec[:, DECAY, :], ACT.Exp).then_inc(decay_exp, 1)
                for i in (KEY, VALUE):
                    for o in range(C):
                        for b in range(B):
                            act.wait_ge(proj, 4 * i + 2 * o + b + 1)
                            nc.scalar.copy((k, v)[i][:, o, b, :], ps[:, 4 * i + 2 * o + b, :]).then_inc(kv_kept, 1)
                for c in range(C):
                    act.wait_ge(d_ready, 2 * c + 2)
                    a(ea[:, c], ea[:, c], ACT.Exp, scale=-1.0).then_inc(cur_prev_exp, 1)
                    a(eb[:, c], eb[:, c], ACT.Exp).then_inc(cur_prev_exp, 1)
                    act.wait_ge(scaled_ready, 2 * c + 2)
                    a(ec[:, c], ec[:, c], ACT.Exp).then_inc(scan_exp, 1)
                    a(ed[:, c], ed[:, c], ACT.Exp).then_inc(scan_exp, 1)
                for o in range(C):
                    for b in range(B):
                        act.wait_ge(proj, 8 + 2 * o + b + 1)
                        a(r[:, o, b, :], ps[:, 2 * o + b, :], ACT.Sigmoid).then_inc(r_kept, 1)
                norm.on_act(act, core.ln_eps[:])

            @block.vector
            def _(dve):
                V = nc.vector
                link = chain(dve, sem("dve_order"), core.dve_count)
                dve.wait_ge(x_in, 4 * 16)
                link(norm.on_dve(dve, link, x, xn))
                norm.on_dve(dve, link, xn, xl).then_inc(xl_ready, 1)
                dve.wait_ge(xs_ready, 4)
                dve.wait_ge(sem("pool_made"), 9)
                dve.wait_ge(vec_kept, 1)
                for c in range(C):
                    last = V.tensor_tensor(diff[:, c], xs[:, c, :, 1:], xs[:, c, :, :T], ALU.subtract)
                link(last)
                for i in (KEY, VALUE, GATE):
                    for c in range(C):
                        last = V.scalar_tensor_tensor(mixed[:, i, c], diff[:, c], vec[:, MIX_K + i, c:c + 1],
                                                      xs[:, c, :, :T], ALU.mult, ALU.add)
                    last.then_inc(mix_ready, 1)
                dve.wait_ge(decay_exp, 1)
                link(V.tensor_scalar(decay[:], decay[:], -1.0, None, ALU.mult))
                dve.wait_ge(w_kept, 4)
                for c in range(C):
                    dve.wait_ge(kv_kept, 2 * c + 2)
                    for b in range(B):
                        last = V.tensor_tensor_scan(top[:, c, b, 1:], decay[:, c:c + 1].to_broadcast([P, T]),
                                                    k[:, c, b, :], BEFORE, ALU.add, ALU.max)
                    link(last)
                    link(V.scalar_tensor_tensor(diff[:, c], k[:, c], vec[:, BONUS, c:c + 1], top[:, c, :, :T],
                                                ALU.add, ALU.subtract))
                    V.tensor_scalar(ea[:, c], diff[:, c], 0.0, None, ALU.max).then_inc(d_ready, 1)
                    V.tensor_scalar(eb[:, c], diff[:, c], 0.0, None, ALU.min).then_inc(d_ready, 1)
                    V.scalar_tensor_tensor(ec[:, c], top[:, c, :, :T], decay[:, c:c + 1], top[:, c, :, 1:],
                                           ALU.add, ALU.subtract).then_inc(scaled_ready, 1)
                    V.tensor_tensor(ed[:, c], k[:, c], top[:, c, :, 1:], ALU.subtract).then_inc(scaled_ready, 1)
                for c in range(C):
                    dve.wait_ge(kv_kept, 4 + 2 * c + 2)
                    dve.wait_ge(scan_exp, 2 * c + 2)
                    link(V.tensor_tensor(diff[:, c], ed[:, c], v[:, c], ALU.mult))
                    for b in range(B):
                        V.tensor_tensor_scan(num[:, c, b, 1:], ec[:, c, b, :], diff[:, c, b, :], 0.0,
                                             ALU.mult, ALU.add)
                        last = V.tensor_tensor_scan(den[:, c, b, 1:], ec[:, c, b, :], ed[:, c, b, :], 0.0,
                                                    ALU.mult, ALU.add)
                    link(last)
                    dve.wait_ge(cur_prev_exp, 2 * c + 2)
                    V.tensor_tensor(diff[:, c], ea[:, c], num[:, c, :, :T], ALU.mult)
                    V.tensor_tensor(ec[:, c], eb[:, c], v[:, c], ALU.mult)
                    link(V.tensor_tensor(ed[:, c], ea[:, c], den[:, c, :, :T], ALU.mult))
                    V.tensor_tensor(ea[:, c], ed[:, c], eb[:, c], ALU.add)
                    link(V.tensor_tensor(diff[:, c], diff[:, c], ec[:, c], ALU.add))
                    link(V.reciprocal(ea[:, c], ea[:, c]))
                    link(V.tensor_tensor(diff[:, c], diff[:, c], ea[:, c], ALU.mult))
                    dve.wait_ge(r_kept, 2 * c + 2)
                    V.tensor_tensor(r[:, c], r[:, c], diff[:, c], ALU.mult).then_inc(rw_ready, 1)
                for t in range(0, NT, 2):
                    dve.wait_ge(rw_proj, t + 2)
                    last = V.tensor_tensor(xn[:, t:t + 2, :], xn[:, t:t + 2, :],
                                           ps[:, 4 + t // 2, :].rearrange("p (t d) -> p t d", t=2), ALU.add)
                link(last)
                link(norm.on_dve(dve, link, xn, xl))
                link(V.tensor_tensor(x[:], x[:], xl[:], ALU.add))


def expert_choice(core, ins):
    nc, sem, norm, x, ps = core.nc, core.sem, core.norm, core.x, core.ps
    E = 16
    K = N // E
    W = D + E
    core.late_weights(ins)
    with ExitStack() as own:
        def sb(name, shape):
            return own.enter_context(nc.sbuf_tensor(name, shape, F32))

        xf = sb("xf", [P, NT, D])
        xf_t = sb("xf_t", [P, C, N])
        z = sb("z", [P, NT, D])
        logits = sb("logits", [P, NT, E])
        low = sb("logit_max", [P, NT])
        total = sb("exp_sum", [P, NT])
        probs = sb("probs", [P, NT, E])
        probs_t = sb("probs_t", [E, N])
        left = sb("left", [E, N])
        best = sb("best", [E, 8])
        chosen = sb("chosen", [E, N])
        g = sb("g", [P, NT])
        xf_ready, xf_turned, xf_kept = sem("xf_ready"), sem("xf_turned"), sem("xf_kept")
        z_done, z_kept, logits_kept = sem("z_done"), sem("z_kept"), sem("logits_kept")
        exp_in, exp_out, probs_ready = sem("exp_in"), sem("exp_out"), sem("probs_ready")
        probs_turned, probs_kept, chosen_ready, g_done = (sem("probs_turned"), sem("probs_kept"),
                                                          sem("chosen_ready"), sem("g_done"))
        with nc.Block() as block:

            @block.sync
            def _(sp):
                core.prefetch_late(sp)

            @block.tensor
            def _(pe):
                pe.wait_ge(core.w_in, core.w_in_total)
                pe.wait_ge(xf_ready, 1)
                for b in range(B):
                    for c in range(C):
                        for t in range(TB):
                            last = nc.tensor.transpose(ps[:, 2 * b + c, t * P:(t + 1) * P],
                                                       xf[:, b * TB + t, c * P:(c + 1) * P], core.ident[:])
                        last.then_inc(xf_turned, 1)
                for n in range(NT):
                    t = (n + 4) % NT
                    pe.wait_ge(xf_kept, 4 if n >= 4 or t >= 4 else 2)
                    for c in range(C):
                        nc.tensor.matmul(ps[:, t, 0:W], xf_t[:, c, t * P:(t + 1) * P], core.w_ec[:, c, :],
                                         start=c == 0, stop=False)
                    nc.tensor.matmul(ps[:, t, 0:W], core.ones[0:1, :], core.b_ec[:], start=False, stop=True) \
                        .then_inc(z_done, 1)
                pe.wait_ge(probs_ready, 1)
                pe.wait_ge(z_kept, NT)
                for t in range(NT):
                    last = nc.tensor.transpose(ps[0:E, t // 4, (t % 4) * P:(t % 4 + 1) * P], probs[:, t, :],
                                               core.ident[:])
                last.then_inc(probs_turned, 1)
                pe.wait_ge(chosen_ready, 1)
                for t in range(NT):
                    last = nc.tensor.matmul(ps[:, 2, t:t + 1], chosen[:, t * P:(t + 1) * P], core.ones[0:E, 0:1],
                                            start=True, stop=True)
                last.then_inc(g_done, 1)

            @block.scalar
            def _(act):
                norm.on_act(act, core.ln_eps[:])
                for b in range(B):
                    for c in range(C):
                        act.wait_ge(xf_turned, 2 * b + c + 1)
                        nc.scalar.copy(xf_t[:, c, b * T:(b + 1) * T], ps[:, 2 * b + c, :]).then_inc(xf_kept, 1)
                for n in range(NT):
                    t = (n + 4) % NT
                    act.wait_ge(logits_kept, n + 1)
                    nc.scalar.copy(z[:, t, :], ps[:, t, 0:D]).then_inc(z_kept, 1)
                act.wait_ge(exp_in, 1)
                nc.scalar.activation(probs[:], logits[:], ACT.Exp).then_inc(exp_out, 1)
                norm.on_act(act, core.ln_eps[:])

            @block.vector
            def _(dve):
                V = nc.vector
                link = chain(dve, sem("dve_order"), core.dve_count)
                norm.on_dve(dve, link, x, xf).then_inc(xf_ready, 1)
                for n in range(NT):
                    t = (n + 4) % NT
                    dve.wait_ge(z_done, n + 1)
                    V.tensor_copy(logits[:, t, :], ps[:, t, D:W]).then_inc(logits_kept, 1)
                dve.wait_ge(logits_kept, NT)
                link(V.tensor_reduce(low[:], logits[:], AX_X, ALU.max))
                V.tensor_tensor(logits[:], logits[:], low[:].unsqueeze(2).to_broadcast([P, NT, E]),
                                ALU.subtract).then_inc(exp_in, 1)
                dve.wait_ge(exp_out, 1)
                link(V.tensor_reduce(total[:], probs[:], AX_X, ALU.add))
                link(V.reciprocal(total[:], total[:]))
                V.tensor_tensor(probs[:], probs[:], total[:].unsqueeze(2).to_broadcast([P, NT, E]),
                                ALU.mult).then_inc(probs_ready, 1)
                dve.wait_ge(probs_turned, 1)
                link(V.tensor_copy(probs_t[:], ps[0:E, 0:2, :].rearrange("p a b -> p (a b)")))
                for n in range(0, K, 8):
                    src = probs_t if n == 0 else left
                    link(V.max(best[:], src[:]))
                    link(V.match_replace(left[:], best[:], src[:], 0.0))
                V.tensor_tensor(chosen[:], probs_t[:], left[:], ALU.subtract).then_inc(chosen_ready, 1)
                dve.wait_ge(g_done, 1)
                link(V.tensor_copy(g[:], ps[:, 2, 0:NT]))
                dve.wait_ge(z_kept, NT)
                for t in range(NT):
                    last = V.tensor_scalar(z[:, t, :], z[:, t, :], g[:, t:t + 1], None, ALU.mult)
                link(last)
                link(norm.on_dve(dve, link, z, xf))
                link(V.tensor_tensor(x[:], x[:], xf[:], ALU.add))


def delta_attention(core, ins):
    nc, sem, norm, x, ps, ident = core.nc, core.sem, core.norm, core.x, core.ps, core.ident
    H, DK, CH = 16, 16, 32
    HH = H // C
    G = B * C
    NCH = T // CH
    GROUP = P // CH
    GROUPS = NCH // GROUP
    TAPS = 4
    X_, Q_, K_, V_ = range(4)
    strand = [slice(q * CH, (q + 1) * CH) for q in range(G)]

    outer = ExitStack()

    def place(stack):
        return lambda name, shape: stack.enter_context(nc.sbuf_tensor(name, shape, F32))

    def features(ap):
        return ap.rearrange("p h d -> p (h d)")

    with outer:
        sb = place(outer)
        qkv_rows = sb("qkv", [P, NCH, 3, P])
        qkv = qkv_rows[:].rearrange("p n a (h d) -> p n a h d", h=HH)
        q_t = qkv_rows[:, :, 0].rearrange("p n (q i) -> p n q i", q=G)
        k_t = sb("k_t", [P, NCH, G, CH])
        qk_t = sb("qk_t", [P, NCH, HH, CH])
        beta = sb("beta", [P, NCH, HH])
        n_t = sb("n_t", [P, NCH, HH, CH])
        half = NCH // 2
        stage = ExitStack()
        kbd_first = place(stage)("kbd_first", [P, HH, half, G, CH])

        xa_ready, conv_done, conv_kept = sem("xa_ready"), sem("conv_done"), sem("conv_kept")
        conv_kept_dve = sem("conv_kept_dve")
        qkv_done, silu_done, beta_done = sem("qkv_done"), sem("silu_done"), sem("beta_done")
        ss_ready, ss_root, kq_ready = sem("ss_ready"), sem("ss_root"), sem("kq_ready")
        kq_turned, k_kept, q_kept = sem("kq_turned"), sem("k_kept"), sem("q_kept")
        zeroed, masked_beta = sem("kbd_zeroed"), sem("masked_beta")
        spread = (sem("kbd_first_spread"), sem("kbd_second_spread"))
        with stage:
            sb = place(stage)
            xc = sb("xc", [P, C, 4, N])
            xa = qk_t[:].rearrange("p n h i -> p (n h i)")[:, 0:NT * D].rearrange("p (t d) -> p t d", t=NT)
            sq = qk_t[:].rearrange("p n h i -> p (n h i)")[:, NT * D:].rearrange("p (s n f) -> p s n f", s=2, n=GROUP)
            kbd_second = xc[:].rearrange("p c k t -> p (c k t)").rearrange("p (h n q i) -> p h n q i", h=HH, n=half,
                                                                           q=G)
            kbd = (kbd_first, kbd_second)
            ss = sb("ss", [P, NCH, 2 * HH])
            PROJ_BANKS, BETA_BANK = 7, 7
            with nc.Block() as block:

                @block.gpsimd
                def _(pool):
                    g = nc.gpsimd
                    g.memset(kbd_first[:], 0.0).then_inc(zeroed, 1)
                    pool.wait_ge(qkv_done, NCH)
                    g.memset(kbd_second, 0.0).then_inc(zeroed, 1)
                    pool.wait_ge(beta_done, 1)
                    g.tensor_tensor(n_t[:], core.above[:].unsqueeze(1).unsqueeze(1).to_broadcast([P, NCH, HH, CH]),
                                    beta[:].unsqueeze(3).to_broadcast([P, NCH, HH, CH]), ALU.mult) \
                        .then_inc(masked_beta, 1)

                @block.sync
                def _(sp):
                    for part in range(2):
                        sp.wait_ge(zeroed, part + 1)
                        sp.wait_ge(k_kept, (part + 1) * GROUPS // 2)
                        for h in range(HH):
                            rows = slice(h * DK, (h + 1) * DK)
                            sp.dma_start(kbd[part][rows, h], k_t[rows, part * half:(part + 1) * half]) \
                                .then_inc(spread[part], 16)

                @block.tensor
                def _(pe):
                    pe.wait_ge(xa_ready, 1)
                    for t in range(NT):
                        for c in range(C):
                            n = 2 * t + c
                            if n >= 8:
                                pe.wait_ge((conv_kept, conv_kept_dve)[c], t - 3)
                            lead = t % TB == 0
                            last = nc.tensor.matmul(ps[:, n % 8, :], xa[:, t, c * P:(c + 1) * P],
                                                    core.conv[:, :, 0:P], start=True, stop=lead)
                            if not lead:
                                out = ps[:, n % 8, :].rearrange("p (k t) -> p k t", k=4)[:, 1:4, 0:TAPS - 1]
                                last = nc.tensor.matmul(out, xa[:, t - 1, c * P:(c + 1) * P],
                                                        core.conv[:, 1:4, P:P + TAPS - 1], start=False, stop=True)
                            last.then_inc(conv_done, 1)
                    pe.wait_ge(conv_kept, NT)
                    pe.wait_ge(conv_kept_dve, NT)
                    for n in range(NCH):
                        if n >= PROJ_BANKS:
                            pe.wait_ge(silu_done, n - PROJ_BANKS + 1)
                        bank = n % PROJ_BANKS
                        for which, src in enumerate((Q_, K_, V_)):
                            for ci in range(C):
                                for q in range(G):
                                    b, c = q // C, q % C
                                    last = nc.tensor.matmul(ps[strand[q], bank, which * P:(which + 1) * P],
                                                            xc[:, ci, src, b * T + n * CH:b * T + (n + 1) * CH],
                                                            core.w_qkv[:, which, ci, c * P:(c + 1) * P],
                                                            start=ci == 0, stop=ci == C - 1, skip_group_check=True)
                        for ci in range(C):
                            for q in range(G):
                                b, c = q // C, q % C
                                last = nc.tensor.matmul(ps[strand[q], BETA_BANK, n * HH:(n + 1) * HH],
                                                        xc[:, ci, X_, b * T + n * CH:b * T + (n + 1) * CH],
                                                        core.w_beta[:, ci, c * HH:(c + 1) * HH],
                                                        start=ci == 0, stop=ci == C - 1, skip_group_check=True)
                        last.then_inc(qkv_done, 1)
                    pe.wait_ge(silu_done, NCH)
                    pe.wait_ge(beta_done, 1)
                    for g in range(GROUPS):
                        pe.wait_ge(kq_ready, g + 1)
                        for which in (1, 0):
                            for i in range(GROUP):
                                last = nc.tensor.transpose(ps[:, 2 * g + which, i * P:(i + 1) * P],
                                                           features(qkv[:, g * GROUP + i, which]), ident[:])
                            last.then_inc(kq_turned, 1)

                @block.scalar
                def _(act):
                    a = nc.scalar.activation
                    norm.on_act(act, core.ln_eps[:])
                    for t in range(NT):
                        act.wait_ge(conv_done, 2 * t + 1)
                        nc.scalar.copy(xc[:, 0, :, t * P:(t + 1) * P],
                                       ps[:, 2 * t % 8, :].rearrange("p (k t) -> p k t", k=4)).then_inc(conv_kept, 1)
                    for n in range(NCH):
                        act.wait_ge(qkv_done, n + 1)
                        a(qkv_rows[:, n].rearrange("p a f -> p (a f)"), ps[:, n % PROJ_BANKS, 0:3 * P], ACT.Silu) \
                            .then_inc(silu_done, 1)
                    a(beta[:].rearrange("p n h -> p (n h)"), ps[:, BETA_BANK, 0:NCH * HH], ACT.Sigmoid) \
                        .then_inc(beta_done, 1)
                    act.wait_ge(ss_ready, GROUPS)
                    a(ss[:], ss[:], ACT.Sqrt, bias=core.l2_eps[:]).then_inc(ss_root, 1)
                    for g in range(GROUPS):
                        act.wait_ge(kq_turned, 2 * g + 1)
                        nc.scalar.copy(k_t[:, g * GROUP:(g + 1) * GROUP].rearrange("p n q i -> p (n q i)"),
                                       ps[:, 2 * g + 1, :]).then_inc(k_kept, 1)

                @block.vector
                def _(dve):
                    V = nc.vector
                    link = chain(dve, sem("dve_order"), core.dve_count)
                    norm.on_dve(dve, link, x, xa).then_inc(xa_ready, 1)
                    for t in range(NT):
                        dve.wait_ge(conv_done, 2 * t + 2)
                        V.tensor_copy(xc[:, 1, :, t * P:(t + 1) * P],
                                      ps[:, (2 * t + 1) % 8, :].rearrange("p (k t) -> p k t", k=4)) \
                            .then_inc(conv_kept_dve, 1)
                    for g in range(GROUPS):
                        own = slice(g * GROUP, (g + 1) * GROUP)
                        dve.wait_ge(silu_done, (g + 1) * GROUP)
                        rows = qkv_rows[:, own, 0:2].rearrange("p n a f -> p n (a f)")
                        link(V.tensor_tensor(sq[:, g % 2], rows, rows, ALU.mult))
                        V.tensor_reduce(ss[:, own], sq[:, g % 2].rearrange("p n (a d) -> p n a d", d=DK), AX_X,
                                        ALU.add).then_inc(ss_ready, 1)
                    dve.wait_ge(ss_root, 1)
                    link(V.reciprocal(ss[:], ss[:]))
                    link(V.tensor_scalar(ss[:, :, 0:HH], ss[:, :, 0:HH], float(DK) ** -0.5, None, ALU.mult))
                    for g in range(GROUPS):
                        own = slice(g * GROUP, (g + 1) * GROUP)
                        rows = qkv_rows[:, own, 0:2].rearrange("p n a (h d) -> p n (a h) d", d=DK)
                        V.tensor_tensor(rows, rows, ss[:, own].unsqueeze(3).to_broadcast([P, GROUP, 2 * HH, DK]),
                                        ALU.mult).then_inc(kq_ready, 1)
                    for g in range(GROUPS):
                        dve.wait_ge(kq_turned, 2 * g + 2)
                        V.tensor_copy(qkv_rows[:, g * GROUP:(g + 1) * GROUP, 0],
                                      ps[:, 2 * g, :].rearrange("p (n f) -> p n f", n=GROUP)).then_inc(q_kept, 1)

            pair_done, n_masked, qk_flipped = sem("pair_done"), sem("n_masked"), sem("qk_flipped")
            KK = HH * CH
            with nc.Block() as block:

                @block.gpsimd
                def _(pool):
                    for n in range(0, NCH, 2):
                        pool.wait_ge(qk_flipped, n + 2)
                        nc.gpsimd.tensor_tensor(qk_t[:, n:n + 2], qk_t[:, n:n + 2],
                                                core.upto[:].unsqueeze(1).unsqueeze(1).to_broadcast([P, 2, HH, CH]),
                                                ALU.mult)

                @block.tensor
                def _(pe):
                    for n in range(NCH):
                        pe.wait_ge(spread[n // half], 16 * HH)
                        if n >= 8:
                            pe.wait_ge(qk_flipped, n - 7)
                        for which, src in enumerate((k_t, q_t)):
                            for q in range(G):
                                last = nc.tensor.matmul(
                                    ps[strand[q], n % 8, which * KK:(which + 1) * KK], src[:, n, q, :],
                                    kbd[n // half][:, :, n % half, q, :], start=True, stop=True,
                                    skip_group_check=True)
                        last.then_inc(pair_done, 1)

                @block.vector
                def _(dve):
                    V = nc.vector
                    dve.wait_ge(masked_beta, 1)
                    for n in range(NCH):
                        dve.wait_ge(pair_done, n + 1)
                        V.tensor_tensor(n_t[:, n], n_t[:, n],
                                        ps[:, n % 8, 0:KK].rearrange("p (h i) -> p h i", h=HH),
                                        ALU.mult).then_inc(n_masked, 1)
                        V.transpose(qk_t[:, n].rearrange("p h i -> p (h i)"), ps[:, n % 8, KK:]) \
                            .then_inc(qk_flipped, 1)

        r_t = outer.enter_context(nc.sbuf_tensor("r_t", [P, NCH, HH, CH], F32))
        n_turned, n_kept, n_kept_dve = sem("n_turned"), sem("n_kept"), sem("n_kept_dve")
        eye_ready, inv_done, r_turned, r_kept = sem("eye_ready"), sem("inv_done"), sem("r_turned"), sem("r_kept")
        ROWS = 4
        with ExitStack() as stage:
            sb = place(stage)
            nm = sb("nm", [P, CH, G, CH])
            inv = sb("inv", [P, CH, G, CH])
            terms = sb("terms", [P, G * CH * CH // 4])
            with nc.Block() as block:

                @block.gpsimd
                def _(pool):
                    nc.gpsimd.memset(inv[:], 0.0).then_inc(eye_ready, 1)
                    pool.wait_ge(eye_ready, 1)
                    nc.gpsimd.affine_select(out=inv[:], in_=inv[:], compare_op=ALU.not_equal, fill=1.0, base=0,
                                            pattern=[[1, CH], [0, G], [-1, CH]], channel_multiplier=0) \
                        .then_inc(eye_ready, 1)

                @block.tensor
                def _(pe):
                    cols = n_t[:].rearrange("p n h i -> p (n h) i")
                    for n in range(CH // ROWS):
                        for i in range(n * ROWS, (n + 1) * ROWS):
                            last = nc.tensor.transpose(ps[:, n, (i % ROWS) * P:(i % ROWS + 1) * P], cols[:, :, i],
                                                       ident[:])
                        last.then_inc(n_turned, 1)
                    for n in range(CH // ROWS):
                        pe.wait_ge(inv_done, n + 1)
                        if n == 0:
                            pe.wait_ge(n_kept, CH // ROWS)
                        for i in range(n * ROWS, (n + 1) * ROWS):
                            last = nc.tensor.transpose(ps[:, n, (i % ROWS) * P:(i % ROWS + 1) * P],
                                                       inv[:, i].rearrange("p g c -> p (g c)"), ident[:])
                        last.then_inc(r_turned, 1)

                @block.scalar
                def _(act):
                    for n in range(CH // ROWS):
                        act.wait_ge(n_turned, n + 1)
                        nc.scalar.copy(nm[:, n * ROWS:(n + 1) * ROWS].rearrange("p i g j -> p (i g j)"),
                                       ps[:, n, :]).then_inc(n_kept, 1)
                    for n in range(CH // ROWS):
                        act.wait_ge(r_turned, n + 1)
                        nc.scalar.copy(r_t[:].rearrange("p n h i -> p i (n h)")[:, n * ROWS:(n + 1) * ROWS],
                                       ps[:, n, :].rearrange("p (i h) -> p i h", i=ROWS)).then_inc(r_kept, 1)

                @block.vector
                def _(dve):
                    V = nc.vector
                    link = chain(dve, sem("dve_order"), core.dve_count)
                    dve.wait_ge(eye_ready, 2)
                    dve.wait_ge(n_kept, CH // ROWS)
                    for j in range(CH - 1):
                        below = CH - 1 - j
                        part = terms[:, 0:below * G * (j + 1)].rearrange("p (i g c) -> p i g c", g=G, c=j + 1)
                        link(V.tensor_tensor(part, nm[:, j + 1:, :, j:j + 1].to_broadcast([P, below, G, j + 1]),
                                             inv[:, j, :, 0:j + 1].unsqueeze(1).to_broadcast([P, below, G, j + 1]),
                                             ALU.mult))
                        last = V.tensor_tensor(inv[:, j + 1:, :, 0:j + 1], inv[:, j + 1:, :, 0:j + 1], part,
                                               ALU.subtract)
                        i = j + 1
                        if i % ROWS == ROWS - 1:
                            last.then_inc(inv_done, 1)
                            dve.wait_ge(inv_done, i // ROWS + 1)
                        else:
                            link(last)

        wu_done, wu_kept, wu_ready = sem("wu_done"), sem("wu_kept"), sem("wu_ready")
        wu_ready_dve = sem("wu_ready_dve")
        w_turned, w_kept = sem("delta_w_turned"), sem("delta_w_kept")
        with ExitStack() as stage:
            sb = place(stage)
            wu = n_t[:].rearrange("p n h i -> p (n h i)").rearrange("p (n a h d) -> p n a h d", n=NCH, a=2, h=HH)
            w_t = k_t
            state = sb("state", [P, NCH, G, CH])
            HPAIRS = HH * DK // CH
            heads = [slice(a * CH, (a + 1) * CH) for a in range(HPAIRS)]
            u = sb("u", [P, NCH, P])
            PAIR = 2
            PAIRS = NCH // PAIR
            ON_ACT, ON_DVE = (0, 1), (2, 3)
            with nc.Block() as block:

                def pair_of(rows, m):
                    own = slice(m * PAIR, (m + 1) * PAIR)
                    count = rows.stop - rows.start
                    return (wu[rows, own].rearrange("p n a h d -> p n h a d"),
                            beta[rows, own].unsqueeze(3).to_broadcast([count, PAIR, HH, 2 * DK]))

                @block.tensor
                def _(pe):
                    for m in range(PAIRS):
                        if m >= 2:
                            pe.wait_ge(wu_kept, len(ON_ACT) * (m - 1))
                            pe.wait_ge(wu_ready_dve, len(ON_DVE) * (m - 1))
                        for i in range(PAIR):
                            n = m * PAIR + i
                            for h in range(HH):
                                for q in range(G):
                                    place_ = (i * HH + h) * 2 * DK
                                    last = nc.tensor.matmul(ps[strand[q], G * (m % 2) + q, place_:place_ + 2 * DK],
                                                            r_t[strand[q], n, h, :], qkv[strand[q], n, 1:3, h, :],
                                                            start=True, stop=True, skip_group_check=True)
                        last.then_inc(wu_done, 1)
                    pe.wait_ge(wu_kept, len(ON_ACT) * PAIRS)
                    for g in range(GROUPS):
                        pe.wait_ge(wu_ready, 2 * (g + 1))
                        pe.wait_ge(wu_ready_dve, 2 * len(ON_DVE) * (g + 1))
                        if g == 0:
                            pe.wait_ge(wu_ready_dve, len(ON_DVE) * PAIRS)
                        for i in range(GROUP):
                            last = nc.tensor.transpose(ps[:, g, i * P:(i + 1) * P],
                                                       features(wu[:, g * GROUP + i, 0]), ident[:])
                        last.then_inc(w_turned, 1)

                @block.scalar
                def _(act):
                    for m in range(PAIRS):
                        act.wait_ge(wu_done, m + 1)
                        for q in ON_ACT:
                            own = wu[strand[q], m * PAIR:(m + 1) * PAIR].rearrange("p n a h d -> p n h a d")
                            nc.scalar.copy(own, ps[strand[q], G * (m % 2) + q, :]
                                           .rearrange("p (n h a d) -> p n h a d", n=PAIR, h=HH, a=2)) \
                                .then_inc(wu_kept, 1)
                    for g in range(GROUPS):
                        act.wait_ge(w_turned, g + 1)
                        nc.scalar.copy(w_t[:, g * GROUP:(g + 1) * GROUP].rearrange("p n q i -> p (n q i)"),
                                       ps[:, g, :]).then_inc(w_kept, 1)

                @block.gpsimd
                def _(pool):
                    rows = slice(0, len(ON_ACT) * CH)
                    for m in range(PAIRS):
                        pool.wait_ge(wu_kept, len(ON_ACT) * (m + 1))
                        own = wu[rows, m * PAIR:(m + 1) * PAIR].rearrange("p n a h d -> p n a (h d)")
                        for i in range(PAIR):
                            n = m * PAIR + i
                            last = nc.gpsimd.tensor_tensor(
                                wu[rows, n], wu[rows, n],
                                beta[rows, n].unsqueeze(1).unsqueeze(3).to_broadcast([len(ON_ACT) * CH, 2, HH, DK]),
                                ALU.mult)
                        last.then_inc(wu_ready, 1)

                @block.vector
                def _(dve):
                    V = nc.vector
                    V.memset(state[:, 0], 0.0).then_inc(sem("state_zeroed"), 1)
                    for m in range(PAIRS):
                        dve.wait_ge(wu_done, m + 1)
                        for q in ON_DVE:
                            for i in range(PAIR):
                                n = m * PAIR + i
                                src = ps[strand[q], G * (m % 2) + q, i * HH * 2 * DK:(i + 1) * HH * 2 * DK]
                                last = V.tensor_tensor(
                                    wu[strand[q], n], src.rearrange("p (h a d) -> p a h d", h=HH, a=2),
                                    beta[strand[q], n].unsqueeze(1).unsqueeze(3).to_broadcast([CH, 2, HH, DK]),
                                    ALU.mult)
                            last.then_inc(wu_ready_dve, 1)

            ws_done, u_ready, ku_done, state_ready = (sem("ws_done"), sem("u_ready"), sem("ku_done"),
                                                      sem("state_ready"))
            qs_done = sem("qs_done")
            with nc.Block() as block:
                @block.tensor
                def _(pe):
                    for n in range(NCH):
                        if n:
                            pe.wait_ge(state_ready, n)
                        for a in range(HPAIRS):
                            for q in range(G):
                                last = nc.tensor.matmul(ps[strand[q], a, 0:CH], w_t[heads[a], n, q, :],
                                                        state[heads[a], n, q, :], start=True, stop=True,
                                                        skip_group_check=True)
                        last.then_inc(ws_done, 1)
                        pe.wait_ge(u_ready, n + 1)
                        if n < NCH - 1:
                            for a in range(HPAIRS):
                                for q in range(G):
                                    last = nc.tensor.matmul(ps[heads[a], G + q, 0:CH],
                                                            qkv_rows[strand[q], n, 1, heads[a]],
                                                            u[strand[q], n, heads[a]], start=n == 0,
                                                            stop=n == NCH - 2, skip_group_check=True)
                            last.then_inc(ku_done, 1)
                        if n:
                            for a in range(HPAIRS):
                                for q in range(G):
                                    last = nc.tensor.matmul(ps[strand[q], a, n * CH:(n + 1) * CH],
                                                            q_t[heads[a], n, q, :], state[heads[a], n, q, :],
                                                            start=True, stop=True, skip_group_check=True)
                            last.then_inc(qs_done, 1)

                @block.vector
                def _(dve):
                    V = nc.vector
                    for n in range(NCH):
                        dve.wait_ge(ws_done, n + 1)
                        V.tensor_tensor(u[:, n].rearrange("p (a e) -> p a e", a=HPAIRS),
                                        features(wu[:, n, 1]).rearrange("p (a e) -> p a e", a=HPAIRS),
                                        ps[:, 0:HPAIRS, 0:CH], ALU.subtract).then_inc(u_ready, 1)
                        if n < NCH - 1:
                            dve.wait_ge(ku_done, n + 1)
                            V.tensor_tensor(state[:, n + 1], ps[:, G:2 * G, 0:CH],
                                            core.same_of_pair[:].unsqueeze(1).to_broadcast([P, G, CH]),
                                            ALU.mult).then_inc(state_ready, 1)

            qs_kept, au_done, o_ready = sem("qs_kept"), sem("au_done"), sem("o_ready")

            def half_of(g):
                return G * ((g + 1) % 2)

            squared, ms_ready, ms_root = sem("o_squared"), sem("ms_ready"), sem("ms_root")
            scaled, on_ready = sem("o_scaled"), sem("on_ready")
            o_turned, ot_kept, wo_done, y_kept = sem("o_turned"), sem("ot_kept"), sem("wo_done"), sem("y_kept")
            o = sb("o", [P, NCH, HH, DK])
            ms = sb("ms", [P, NCH, HH])
            done_with = n_t[:].rearrange("p n h i -> p (n h i)")
            osq = done_with[:, 0:NCH * P].rearrange("p (n h e) -> p n h e", n=NCH, h=HH)
            o_t = done_with[:, NCH * P:].rearrange("p (g q j) -> p g q j", g=GROUPS, q=G)
            y = w_t[:].rearrange("p n q i -> p (n q i)").rearrange("p (t d) -> p t d", t=NT)
            with nc.Block() as block:

                @block.tensor
                def _(pe):
                    def read_out(g):
                        if g == 1:
                            pe.wait_ge(qs_kept, GROUPS)
                        if g >= 2:
                            pe.wait_ge(y_kept, g - 1)
                        for i in range(GROUP):
                            n = g * GROUP + i
                            for h in range(HH):
                                for q in range(G):
                                    col = i * P + h * DK
                                    last = nc.tensor.matmul(ps[strand[q], half_of(g) + q, col:col + DK],
                                                            qk_t[strand[q], n, h, :],
                                                            u[strand[q], n, h * DK:(h + 1) * DK], start=True,
                                                            stop=True, skip_group_check=True)
                        last.then_inc(au_done, 1)

                    def project(g):
                        pe.wait_ge(on_ready, g + 1)
                        for i in range(GROUP):
                            last = nc.tensor.transpose(ps[:, half_of(g), i * P:(i + 1) * P],
                                                       features(o[:, g * GROUP + i]), ident[:])
                        last.then_inc(o_turned, 1)
                        pe.wait_ge(ot_kept, g + 1)
                        for b in range(B):
                            for c in range(C):
                                last = nc.tensor.matmul(ps[:, half_of(g) + 1, b * D:(b + 1) * D],
                                                        o_t[:, g, C * b + c, :], core.w_o[:, c, :], start=c == 0,
                                                        stop=c == C - 1)
                        last.then_inc(wo_done, 1)

                    read_out(0)
                    for g in range(GROUPS):
                        if g + 1 < GROUPS:
                            read_out(g + 1)
                        project(g)

                @block.scalar
                def _(act):
                    for g in range(GROUPS):
                        first = 1 if g == 0 else 0
                        own = slice(g * GROUP + first, (g + 1) * GROUP)
                        nc.scalar.copy(o[:, own].rearrange("p n h e -> p n (h e)")
                                       .rearrange("p n (a f) -> p a n f", a=HPAIRS),
                                       ps[:, 0:HPAIRS, own.start * CH:own.stop * CH]
                                       .rearrange("p a (n f) -> p a n f", f=CH)).then_inc(qs_kept, 1)

                    def project(g):
                        own = slice(g * GROUP, (g + 1) * GROUP)
                        act.wait_ge(ms_ready, g + 1)
                        nc.scalar.activation(ms[:, own], ms[:, own], ACT.Sqrt, scale=1.0 / DK, bias=core.ln_eps[:]) \
                            .then_inc(ms_root, 1)
                        act.wait_ge(o_turned, g + 1)
                        nc.scalar.copy(o_t[:, g].rearrange("p q (n i) -> p q n i", n=GROUP),
                                       ps[:, half_of(g), :].rearrange("p (n q i) -> p q n i", n=GROUP, q=G)) \
                            .then_inc(ot_kept, 1)
                        act.wait_ge(wo_done, g + 1)
                        nc.scalar.copy(y.rearrange("p (b t) d -> p b t d", b=B)[:, :, g],
                                       ps[:, half_of(g) + 1, :].rearrange("p (b d) -> p b d", b=B)) \
                            .then_inc(y_kept, 1)

                    for g in range(GROUPS):
                        project(g)
                    norm.on_act(act, core.ln_eps[:])

                @block.gpsimd
                def _(pool):
                    for g in range(GROUPS):
                        own = slice(g * GROUP, (g + 1) * GROUP)
                        pool.wait_ge(o_ready, G * (g + 1))
                        nc.gpsimd.tensor_tensor(osq[:, own], o[:, own], o[:, own], ALU.mult).then_inc(squared, 1)
                        pool.wait_ge(squared, g + 1)
                        nc.gpsimd.tensor_tensor(o[:, own], o[:, own],
                                                core.onorm[:].unsqueeze(1).unsqueeze(1)
                                                .to_broadcast([P, GROUP, HH, DK]), ALU.mult).then_inc(scaled, 1)

                @block.vector
                def _(dve):
                    V = nc.vector
                    link = chain(dve, sem("dve_order"), core.dve_count)
                    link(V.memset(o[:, 0], 0.0))
                    for g in range(GROUPS):
                        own = slice(g * GROUP, (g + 1) * GROUP)
                        dve.wait_ge(au_done, g + 1)
                        dve.wait_ge(qs_kept, g + 1)
                        for q in range(G):
                            V.tensor_tensor(o[strand[q], own], o[strand[q], own],
                                            ps[strand[q], half_of(g) + q, :]
                                            .rearrange("p (n h e) -> p n h e", n=GROUP, h=HH),
                                            ALU.add).then_inc(o_ready, 1)
                        dve.wait_ge(squared, g + 1)
                        V.tensor_reduce(ms[:, own], osq[:, own], AX_X, ALU.add).then_inc(ms_ready, 1)
                        dve.wait_ge(ms_root, g + 1)
                        link(V.reciprocal(ms[:, own], ms[:, own]))
                        dve.wait_ge(scaled, g + 1)
                        V.tensor_tensor(o[:, own], o[:, own],
                                        ms[:, own].unsqueeze(3).to_broadcast([P, GROUP, HH, DK]),
                                        ALU.mult).then_inc(on_ready, 1)
                    dve.wait_ge(y_kept, GROUPS)
                    link(norm.on_dve(dve, link, y, y))
                    link(V.tensor_tensor(x[:], x[:], y, ALU.add))


def expert_mixture(core, ins):
    nc, sem, norm, x, ps, ident = core.nc, core.sem, core.norm, core.x, core.ps, core.ident
    E = 8
    SH = core.SH
    HI, LO = 0, 1
    PRODUCTS = ((HI, HI), (HI, LO), (LO, HI))
    HID = SH + E
    with ExitStack() as own:
        def sb(name, shape, dt=F32):
            return own.enter_context(nc.sbuf_tensor(name, shape, dt))

        xm = sb("xm", [P, NT, D])
        gate_r = sb("gate_r", [P, 2, C, HID, P], F32R)
        up_r = sb("up_r", [P, 2, C, HID, P], F32R)
        down_r = sb("down_r", [P, 2, HID, D], F32R)
        xm_r = sb("xm_r", [P, 2, C, N], F32R)
        router_t = sb("router_t", [P, C, E])
        scores = sb("scores", [P, NT, E])
        select = sb("select", [P, NT, E])
        best = sb("best8", [P, NT, 8])
        where = sb("where", [P, NT, 8], U32)
        where_f = sb("where_f", [P, NT, 8])
        first = sb("first", [P, NT, E])
        second = sb("second", [P, NT, E])
        total = sb("score_sum", [P, NT])
        room = [0]

        def over(size):
            room[0] += size
            assert room[0] <= core.stored.shape[1]
            return core.stored[:, room[0] - size:room[0]]

        hidden = over(4 * T).rearrange("p (a t) -> p a t", a=4)
        xm_t = hidden.rearrange("p a t -> p (a t)").rearrange("p (c n) -> p c n", c=C)
        gated = over(2 * T).rearrange("p (a t) -> p a t", a=2)
        share_t = over(N)[0:E, :]
        share = over(E * N).rearrange("p (e n) -> p e n", e=E)
        hidden_r = sb("hidden_r", [P, 2, 2, T], F32R)
        y = xm

        xm_ready, xm_turned, xm_kept = sem("xm_ready"), sem("xm_turned"), sem("xm_kept")
        turned, kept_act, kept_dve = sem("ffn_w_turned"), sem("ffn_w_kept"), sem("ffn_w_kept_dve")
        router_turned, router_kept = sem("router_turned"), sem("router_kept")
        scores_done, scores_kept = sem("scores_done"), sem("scores_kept")
        share_ready, share_turned, share_t_kept = sem("share_ready"), sem("share_turned"), sem("share_t_kept")
        share_out, share_in = sem("share_out"), sem("share_in")
        up_done, silu_ready, prod_ready, hidden_ready = (sem("up_done"), sem("silu_ready"), sem("prod_ready"),
                                                         sem("hidden_ready"))
        xm_hi_kept, xm_lo_kept, hidden_hi, hidden_lo = (sem("xm_hi_kept"), sem("xm_lo_kept"), sem("hidden_hi"),
                                                        sem("hidden_lo"))
        down_done, y_ready = sem("down_done"), sem("y_ready")

        turns = []
        def flat(ap):
            return ap.rearrange("p a b -> p (a b)")

        groups = []
        for m, dst in ((core.sw1, gate_r), (core.sw2, up_r)):
            groups += [([m[:, a, c * P:(c + 1) * P] for a in range(a0, a0 + 4)],
                        [flat(dst[:, part, c, a0:a0 + 4, :]) for part in (HI, LO)])
                       for c in range(C) for a0 in range(0, SH, 4)]
        for half, dst in ((0, gate_r), (1, up_r)):
            groups += [([core.w12[:, 2 * e + half, c * P:(c + 1) * P] for e in range(e0, e0 + 4)],
                        [flat(dst[:, part, c, SH + e0:SH + e0 + 4, :]) for part in (HI, LO)])
                       for c in range(C) for e0 in range(0, E, 4)]
        groups += [([core.sw3[:, c, a * P:(a + 1) * P] for a in (a0, a0 + 1) for c in range(C)],
                    [flat(down_r[:, part, a0:a0 + 2, :]) for part in (HI, LO)]) for a0 in range(0, SH, 2)]
        groups += [([core.w3[:, e, c, :] for e in (e0, e0 + 1) for c in range(C)],
                    [flat(down_r[:, part, SH + e0:SH + e0 + 2, :]) for part in (HI, LO)])
                   for e0 in range(0, E, 2)]

        TURNED, STEPS = len(groups), B * HID
        LAG = 3

        def bank_of(n):
            return n if n < 8 else 4 + n % 4

        with nc.Block() as block:

            @block.tensor
            def _(pe):
                pe.wait_ge(core.f_in, core.f_in_total)
                def turn(n):
                    if n >= 8:
                        pe.wait_ge(kept_dve, n - 3)
                    for i, stored in enumerate(groups[n][0]):
                        last = nc.tensor.transpose(ps[:, bank_of(n), i * P:(i + 1) * P], stored, ident[:])
                    last.then_inc(turned, 1)

                for n in range(8):
                    turn(n)
                pe.wait_ge(kept_dve, 4)
                for c in range(C):
                    last = nc.tensor.transpose(ps[:, 3, c * E:(c + 1) * E], core.router[:, c * P:(c + 1) * P],
                                               ident[0:E, 0:E])
                last.then_inc(router_turned, 1)
                pe.wait_ge(xm_ready, 1)
                pe.wait_ge(router_kept, 1)
                for b in range(B):
                    for c in range(C):
                        for t in range(TB):
                            last = nc.tensor.transpose(ps[:, 2 * b + c, t * P:(t + 1) * P],
                                                       xm[:, b * TB + t, c * P:(c + 1) * P], ident[:])
                        last.then_inc(xm_turned, 1)
                pe.wait_ge(xm_kept, B * C)
                for t in range(NT):
                    for c in range(C):
                        last = nc.tensor.matmul(ps[:, 0, t * E:(t + 1) * E], xm_t[:, c, t * P:(t + 1) * P],
                                                router_t[:, c, :], start=c == 0, stop=c == C - 1)
                last.then_inc(scores_done, 1)
                for n in range(8, TURNED):
                    turn(n)
                pe.wait_ge(share_ready, 1)
                pe.wait_ge(scores_kept, 1)
                for t in range(NT):
                    last = nc.tensor.transpose(ps[0:E, 2 + t // TB, (t % TB) * P:(t % TB + 1) * P],
                                               first[:, t, :], ident[:])
                last.then_inc(share_turned, 1)

                def up(n):
                    b, a = n // HID, n % HID
                    bank = 4 + 2 * (n % 2)
                    if n == 0:
                        pe.wait_ge(kept_dve, TURNED)
                        pe.wait_ge(xm_lo_kept, B * C)
                    if n >= 2:
                        pe.wait_ge(prod_ready, n - 1)
                    for which, w in enumerate((gate_r, up_r)):
                        for i, (c, wp, xp) in enumerate((c, *parts) for c in range(C) for parts in PRODUCTS):
                            last = nc.tensor.matmul(ps[:, bank + which, :], w[:, wp, c, a, :],
                                                    xm_r[:, xp, c, b * T:(b + 1) * T], start=i == 0,
                                                    stop=i == C * len(PRODUCTS) - 1)
                        last.then_inc(up_done, 1)

                def down(n):
                    b, a = n // HID, n % HID
                    pe.wait_ge(hidden_lo, n + 1)
                    if n == 0:
                        pe.wait_ge(share_t_kept, 1)
                    if a == 0 and b:
                        pe.wait_ge(y_ready, b * TB)
                    for t in range(TB):
                        for i, (wp, hp) in enumerate(PRODUCTS):
                            last = nc.tensor.matmul(ps[:, t, 0:D], hidden_r[:, n % 2, hp, t * P:(t + 1) * P],
                                                    down_r[:, wp, a, :], start=a == 0 and i == 0,
                                                    stop=a == HID - 1 and i == len(PRODUCTS) - 1)
                    last.then_inc(down_done, 1)

                for n in range(STEPS + LAG):
                    if n < STEPS:
                        up(n)
                    if n >= LAG:
                        down(n - LAG)

            @block.scalar
            def _(act):
                a = nc.scalar.activation
                norm.on_act(act, core.ln_eps[:])
                def high_weights(n):
                    act.wait_ge(turned, n + 1)
                    nc.scalar.copy(groups[n][1][HI], ps[:, bank_of(n), :]).then_inc(kept_act, 1)

                for n in range(8):
                    high_weights(n)
                act.wait_ge(router_turned, 1)
                nc.scalar.copy(router_t[:].rearrange("p c e -> p (c e)"), ps[:, 3, 0:C * E]).then_inc(router_kept, 1)
                for n in range(B * C):
                    act.wait_ge(xm_turned, n + 1)
                    if n == 0:
                        act.wait_ge(kept_dve, 4)
                    own = (n % C, slice((n // C) * T, (n // C + 1) * T))
                    nc.scalar.copy(xm_t[:, own[0], own[1]], ps[:, n, :]).then_inc(xm_kept, 1)
                for n in range(B * C):
                    own = (n % C, slice((n // C) * T, (n // C + 1) * T))
                    act.wait_ge(xm_kept, n + 1)
                    nc.scalar.copy(xm_r[:, HI, own[0], own[1]], xm_t[:, own[0], own[1]]).then_inc(xm_hi_kept, 1)
                act.wait_ge(scores_done, 1)
                a(scores[:].rearrange("p t e -> p (t e)"), ps[:, 0, 0:NT * E], ACT.Sigmoid).then_inc(scores_kept, 1)
                for n in range(8, TURNED):
                    high_weights(n)

                def silu(n):
                    act.wait_ge(up_done, 2 * n + 1)
                    if n >= 2:
                        act.wait_ge(prod_ready, n - 1)
                    a(gated[:, n % 2, :], ps[:, 4 + 2 * (n % 2), :], ACT.Silu).then_inc(silu_ready, 1)

                def high(n):
                    b, i = n // HID, n % HID
                    if i < SH:
                        act.wait_ge(prod_ready, n + 1)
                    else:
                        act.wait_ge(hidden_ready, b * E + i - SH + 1)
                    if n >= 2:
                        act.wait_ge(down_done, n - 1)
                    nc.scalar.copy(hidden_r[:, n % 2, HI, :], hidden[:, n % 4, :]).then_inc(hidden_hi, 1)

                for n in range(STEPS + 1):
                    if n < STEPS:
                        silu(n)
                    if n >= 1:
                        high(n - 1)
                norm.on_act(act, core.ln_eps[:])

            @block.sync
            def _(sp):
                sp.wait_ge(share_t_kept, 1)
                sp.dma_start(core.share_dram, share_t).then_inc(share_out, 16)
                sp.wait_ge(share_out, 16)
                for e in range(E):
                    sp.dma_start(share[:, e, :], core.share_dram[e].partition_broadcast(P)).then_inc(share_in, 16)

            @block.gpsimd
            def _(pool):
                pool.wait_ge(share_in, 16 * E)
                for n in range(STEPS):
                    b, a = n // HID, n % HID
                    if a >= SH:
                        pool.wait_ge(prod_ready, n + 1)
                        nc.gpsimd.tensor_tensor(hidden[:, n % 4, :], hidden[:, n % 4, :],
                                                share[:, a - SH, b * T:(b + 1) * T], ALU.mult) \
                            .then_inc(hidden_ready, 1)
                    pool.wait_ge(hidden_hi, n + 1)
                    if n >= 2:
                        pool.wait_ge(down_done, n - 1)
                    nc.gpsimd.tensor_tensor(hidden_r[:, n % 2, LO, :], hidden[:, n % 4, :],
                                            hidden_r[:, n % 2, HI, :], ALU.subtract).then_inc(hidden_lo, 1)

            @block.vector
            def _(dve):
                V = nc.vector
                link = chain(dve, sem("dve_order"), core.dve_count)
                norm.on_dve(dve, link, x, xm).then_inc(xm_ready, 1)
                def low_weights(n):
                    dve.wait_ge(kept_act, n + 1)
                    V.tensor_tensor(groups[n][1][LO], ps[:, bank_of(n), :], groups[n][1][HI], ALU.subtract) \
                        .then_inc(kept_dve, 1)

                for n in range(8):
                    low_weights(n)
                for n in range(B * C):
                    own = (n % C, slice((n // C) * T, (n // C + 1) * T))
                    dve.wait_ge(xm_hi_kept, n + 1)
                    V.tensor_tensor(xm_r[:, LO, own[0], own[1]], xm_t[:, own[0], own[1]], xm_r[:, HI, own[0], own[1]],
                                    ALU.subtract).then_inc(xm_lo_kept, 1)
                dve.wait_ge(scores_kept, 1)
                link(V.tensor_tensor(select[:], scores[:], core.expert_bias[:].unsqueeze(1).to_broadcast([P, NT, E]),
                                     ALU.add))
                for t in range(NT):
                    last = V.max(best[:, t, :], select[:, t, :])
                link(last)
                for t in range(NT):
                    last = V.max_index(where[:, t, :], best[:, t, :], select[:, t, :])
                link(last)
                link(V.tensor_copy(where_f[:], where[:]))
                number = core.numbers[:].unsqueeze(1).to_broadcast([P, NT, E])
                V.tensor_tensor(first[:], number, where_f[:, :, 0:1].to_broadcast([P, NT, E]), ALU.is_equal)
                link(V.tensor_tensor(second[:], number, where_f[:, :, 1:2].to_broadcast([P, NT, E]), ALU.is_equal))
                link(V.tensor_tensor(first[:], first[:], second[:], ALU.add))
                link(V.tensor_tensor(first[:], first[:], scores[:], ALU.mult))
                link(V.tensor_reduce(total[:], first[:], AX_X, ALU.add))
                link(V.tensor_scalar(total[:], total[:], 1e-9, None, ALU.add))
                link(V.reciprocal(total[:], total[:]))
                V.tensor_tensor(first[:], first[:], total[:].unsqueeze(2).to_broadcast([P, NT, E]), ALU.mult) \
                    .then_inc(share_ready, 1)
                for n in range(8, TURNED):
                    low_weights(n)
                dve.wait_ge(share_turned, 1)
                V.tensor_copy(share_t, ps[0:E, 2:4, :].rearrange("p a b -> p (a b)")).then_inc(share_t_kept, 1)

                def keep_y(b):
                    dve.wait_ge(down_done, (b + 1) * HID)
                    for t in range(TB):
                        V.tensor_copy(y[:, b * TB + t, :], ps[:, t, 0:D]).then_inc(y_ready, 1)

                for n in range(STEPS):
                    if n >= 4:
                        dve.wait_ge(down_done, n - 3)
                    dve.wait_ge(silu_ready, n + 1)
                    dve.wait_ge(up_done, 2 * n + 2)
                    V.tensor_tensor(hidden[:, n % 4, :], gated[:, n % 2, :], ps[:, 4 + 2 * (n % 2) + 1, :], ALU.mult) \
                        .then_inc(prod_ready, 1)
                    if n == HID + LAG - 2:
                        keep_y(0)
                keep_y(1)
                dve.wait_ge(y_ready, NT)
                link(norm.on_dve(dve, link, y, y))
                link(V.tensor_tensor(x[:], x[:], y[:], ALU.add))


def sandwich(nc, ins, out):
    with ExitStack() as ctx:
        core = Core(nc, ctx)
        core.x = core.sb("x", [P, NT, D])
        core.ident = core.sb("ident", [P, P])
        core.ones = core.sb("ones", [P, P])
        core.ln_eps = core.sb("ln_eps", [P, 1])
        core.l2_eps = core.sb("l2_eps", [P, 1])
        core.ps = ctx.enter_context(nc.psum_tensor("ps", [P, 8, 512], F32))
        core.norm = Norm(core)
        core.dve_count = [0]
        core.weights(ins)
        for layer in (time_mixing, expert_choice, delta_attention, expert_mixture):
            layer(core, ins)
        stored = core.sem("stored")
        with nc.Block() as block:
            @block.sync
            def _(sp):
                sp.dma_start(tiles(out.rearrange("b t d -> (b t) d")), core.x[:]).then_inc(stored, 16)
                sp.wait_ge(stored, 16)


_INS = ["L0_attn_hidden_state", "L0_attn_ln_w", "L0_attn_ln_b", "L0_attn_Wk", "L0_attn_Wv", "L0_attn_Wr",
        "L0_attn_Wo", "L0_attn_mix_k", "L0_attn_mix_v", "L0_attn_mix_r", "L0_attn_time_decay",
        "L0_attn_current_token_weight", "L0_ffn_router_w", "L0_ffn_router_b", "L0_ffn_expert_w",
        "L0_ffn_expert_b", "L1_attn_Wq", "L1_attn_Wk", "L1_attn_Wv", "L1_attn_Wb", "L1_attn_Wo",
        "L1_attn_conv_q", "L1_attn_conv_k", "L1_attn_conv_v", "L1_attn_onorm_w", "L1_ffn_w12", "L1_ffn_w3",
        "L1_ffn_router_w", "L1_ffn_expert_bias", "L1_ffn_sw1", "L1_ffn_sw2", "L1_ffn_sw3"]


def kernel(**inputs):
    import numpy as _np
    import concourse.bacc as _bacc
    from concourse import mybir as _mybir
    from concourse.bass_utils import run_bass_kernel_spmd as _run

    nc = _bacc.Bacc("TRN2", target_bir_lowering=False, num_devices=1)
    arrays, ins = {}, {}
    for name in _INS:
        a = _np.ascontiguousarray(inputs[name])
        arrays[f"in_{name}_dram"] = a
        ins[name] = nc.dram_tensor(f"in_{name}_dram", a.shape, _mybir.dt.from_np(a.dtype),
                                   kind="ExternalInput").ap()
    out = nc.dram_tensor("out_0_dram", (B, T, D), F32, kind="ExternalOutput").ap()
    sandwich(nc, ins, out)
    r = _run(nc, [arrays], core_ids=[0])
    return r.results[0]["out_0_dram"]
```

```python
from contextlib import ExitStack

import concourse.bass as bass
from concourse import mybir

F32 = mybir.dt.float32
F32R = mybir.dt.float32r
U32 = mybir.dt.uint32
ALU = mybir.AluOpType
ACT = mybir.ActivationFunctionType
AX_X = mybir.AxisListType.X

P = 128
B, T, D = 2, 512, 256
N = B * T
NT = N // P
TB = T // P
C = D // P
LN_EPS = 1e-5


class Core:

    def __init__(self, nc, ctx):
        self.nc, self.ctx, self.named = nc, ctx, {}

    def sb(self, name, shape):
        return self.ctx.enter_context(self.nc.sbuf_tensor(name, shape, F32))

    def weights(self, ins):
        sb = self.sb
        self.w_ec = sb("w_ec", [P, C, D + 16])
        self.b_ec = sb("b_ec", [P, D + 16])
        self.w_in = self.sem("w_in")
        self.loads = [
            (self.w_ec[:, :, 0:D], ins["L0_ffn_expert_w"].rearrange("(c p) n -> p c n", p=P)),
            (self.w_ec[:, :, D:], ins["L0_ffn_router_w"].rearrange("(c p) n -> p c n", p=P)),
            (self.b_ec[:, 0:D], ins["L0_ffn_expert_b"].partition_broadcast(P)),
            (self.b_ec[:, D:], ins["L0_ffn_router_b"].partition_broadcast(P)),
        ]
        taps = 4 * (P + 3)
        sizes = (3 * C * D, C * 16, C * D, taps, taps, 3 * (P + 3))
        self.third = sb("third", [P, sum(sizes)])
        w_qkv, w_beta, w_o, conv, taps, scratch = (self.third[:, sum(sizes[:n]):sum(sizes[:n + 1])]
                                                   for n in range(len(sizes)))
        self.w_qkv = w_qkv.rearrange("p (n c d) -> p n c d", n=3, c=C)
        self.w_beta = w_beta.rearrange("p (c h) -> p c h", c=C)
        self.w_o = w_o.rearrange("p (c d) -> p c d", c=C)
        self.conv_w = sb("conv_w", [P, 3, 4])
        self.onorm = sb("onorm", [P, 16])
        for n, name in enumerate("qkv"):
            self.loads += [
                (self.w_qkv[:, n], ins["L1_attn_W" + name].rearrange("(c p) n -> p c n", p=P)),
                (self.conv_w[:, n], ins["L1_attn_conv_" + name].partition_broadcast(P)),
            ]
        self.loads += [
            (self.w_beta, ins["L1_attn_Wb"].rearrange("(c p) n -> p c n", p=P)),
            (self.w_o, ins["L1_attn_Wo"].rearrange("(c p) n -> p c n", p=P)),
            (self.onorm[:], ins["L1_attn_onorm_w"].partition_broadcast(P)),
        ]
        self.conv = conv.rearrange("p (k t) -> p k t", k=4)
        self.taps = taps.rearrange("p (k t) -> p k t", k=4)
        self.scratch = scratch.rearrange("p (k t) -> p k t", k=3)
        self.above = sb("above", [P, 32])
        self.upto = sb("upto", [P, 32])
        self.same_of_pair = sb("same_of_pair", [P, 32])
        self.numbers = sb("numbers", [P, 8])
        self.own_head = sb("own_head", [P, 8])
        self.w_in_total = 16 * len(self.loads)

    def late_weights(self, ins):
        sb = self.sb
        E, self.SH = 8, 1024 // P
        self.stored = sb("stored", [P, 6 * self.SH * D])
        tile = self.SH * D

        def part(n, size, split, **sizes):
            return self.stored[:, n * tile:(n + size) * tile].rearrange(split, **sizes)

        self.sw1 = part(0, 1, "p (a d) -> p a d", d=D)
        self.sw2 = part(1, 1, "p (a d) -> p a d", d=D)
        self.w12 = part(2, 2, "p (a d) -> p a d", d=D)
        self.sw3 = part(4, 1, "p (c h) -> p c h", c=C)
        self.w3 = part(5, 1, "p (e c h) -> p e c h", e=E, c=C)
        self.router = sb("router", [E, D])
        self.expert_bias = sb("expert_bias", [P, E])
        self.f_in = self.sem("f_in")
        self.share_dram = self.nc.dram_tensor("share_dram", (E, N), F32, kind="Internal").ap()
        self.ffn_loads = [
            (self.sw1, ins["L1_ffn_sw1"].rearrange("(a p) d -> p a d", p=P)),
            (self.sw2, ins["L1_ffn_sw2"].rearrange("(a p) d -> p a d", p=P)),
            (self.w12, ins["L1_ffn_w12"].rearrange("e (a p) d -> p (e a) d", p=P)),
            (self.sw3, ins["L1_ffn_sw3"].rearrange("(c p) h -> p c h", p=P)),
            (self.w3, ins["L1_ffn_w3"].rearrange("e (c p) h -> p e c h", p=P)),
            (self.router[:], ins["L1_ffn_router_w"]),
            (self.expert_bias[:], ins["L1_ffn_expert_bias"].partition_broadcast(P)),
        ]
        self.f_in_total = 16 * len(self.ffn_loads)

    def prefetch_late(self, sp):
        for place, source in self.ffn_loads:
            sp.dma_start(place, source).then_inc(self.f_in, 16)

    def prefetch(self, sp):
        for place, source in self.loads:
            sp.dma_start(place, source).then_inc(self.w_in, 16)

    def masks(self, pool, order):
        g = self.nc.gpsimd
        count = [0]

        def link(ins):
            count[0] += 1
            ins.then_inc(order, 1)
            pool.wait_ge(order, count[0])

        def where(dst, op, fill, base, pattern, step):
            link(g.affine_select(out=dst, in_=dst, compare_op=op, fill=fill, base=base, pattern=pattern,
                                 channel_multiplier=step))

        for e in range(8):
            link(g.memset(self.numbers[:, e:e + 1], float(e)))
        for m in (self.above, self.upto, self.same_of_pair):
            link(g.memset(m[:], 1.0))
        for r in range(4):
            rows = slice(32 * r, 32 * r + 32)
            where(self.above[rows], ALU.is_gt, 0.0, 0, [[1, 32]], -1)
            where(self.upto[rows], ALU.is_ge, 0.0, 0, [[1, 32]], -1)
        for r in range(4):
            by_head = self.same_of_pair[32 * r:32 * r + 32].rearrange("p (h e) -> p h e", h=2)
            where(by_head, ALU.is_ge, 0.0, 0, [[-16, 2], [0, 16]], 1)
            where(by_head, ALU.is_ge, 0.0, 15, [[16, 2], [0, 16]], -1)
        link(g.memset(self.own_head[:], 1.0))
        where(self.own_head[:], ALU.is_ge, 0.0, 0, [[-16, 8]], 1)
        where(self.own_head[:], ALU.is_ge, 0.0, 15, [[16, 8]], -1)
        link(g.memset(self.taps, 0.0))
        for d in range(4):
            where(self.taps[:, d], ALU.not_equal, 1.0, -d, [[1, P + 3]], -1)
        link(g.tensor_copy(self.conv[:, 0], self.taps[:, 0]))
        pool.wait_ge(self.w_in, self.w_in_total)
        for n in range(3):
            link(g.tensor_scalar(self.conv[:, 1 + n], self.taps[:, 3], self.conv_w[:, n, 0:1], 0.0, ALU.mult,
                                 ALU.add))
        for d in (2, 1, 0):
            for n in range(3):
                link(g.tensor_scalar(self.scratch[:, n], self.taps[:, d], self.conv_w[:, n, 3 - d:4 - d], 0.0,
                                     ALU.mult, ALU.add))
            for n in range(3):
                link(g.tensor_tensor(self.conv[:, 1 + n], self.conv[:, 1 + n], self.scratch[:, n], ALU.add))

    def sem(self, name):
        if name not in self.named:
            self.named[name] = self.ctx.enter_context(self.nc.semaphore(name))
        return self.named[name]


def chain(eng, sem, count):
    def link(ins):
        count[0] += 1
        ins.then_inc(sem, 1)
        eng.wait_ge(sem, count[0])
    return link


def tiles(dram):
    return dram.rearrange("(t p) d -> p t d", p=P)


class Norm:

    def __init__(self, core):
        sb = core.sb
        self.nc, self.done = core.nc, [0, 0]
        self.stats = sb("ln_stats", [P, NT, 6])
        self.mv = sb("ln_mean_var", [P, NT, 2])
        self.std = sb("ln_std_dev", [P, NT])
        self.inv = sb("ln_inverse_std", [P, NT])
        self.var_ready, self.std_ready = core.sem("ln_var"), core.sem("ln_std")

    def on_act(self, act, eps):
        self.done[1] += 1
        act.wait_ge(self.var_ready, self.done[1])
        self.nc.scalar.activation(self.std[:], self.mv[:, :, 1], ACT.Sqrt, bias=eps).then_inc(self.std_ready, 1)

    def on_dve(self, dve, link, src, dst, ready=None, order=range(NT), arrived=lambda t: None):
        for t in order:
            arrived(t)
            last = self.tile_stats(src, t)
        link(last)
        self.gather_stats().then_inc(self.var_ready, 1)
        self.inverse_std(dve, link)
        return self.normalize(src, dst, ready)

    def tile_stats(self, src, t):
        return self.nc.vector.bn_stats(self.stats[:, t, :], src[:, t, :])

    def gather_stats(self):
        for t in range(NT):
            last = self.nc.vector.bn_aggr(self.mv[:, t, :], self.stats[:, t, :])
        return last

    def inverse_std(self, dve, link):
        self.done[0] += 1
        dve.wait_ge(self.std_ready, self.done[0])
        link(self.nc.vector.reciprocal(self.inv[:], self.std[:]))

    def normalize(self, src, dst, ready=None):
        v = self.nc.vector
        for t in range(NT):
            last = v.tensor_scalar(dst[:, t, :], src[:, t, :], self.mv[:, t, 0:1], self.inv[:, t:t + 1],
                                   ALU.subtract, ALU.mult)
            if ready is not None:
                last.then_inc(ready, 1)
        return last


def time_mixing(core, ins):
    nc, sem, norm, x = core.nc, core.sem, core.norm, core.x
    KEY, VALUE, GATE, OUT = range(4)
    with ExitStack() as own:
        def sb(name, shape):
            return own.enter_context(nc.sbuf_tensor(name, shape, F32))

        w_nat = sb("w_nat", [P, 4, C, D])
        w_t = sb("w_t", [P, 4, C, D])
        vec = sb("vec", [P, 7, C])
        vec_rows = sb("vec_rows", [7 * C, P])
        decay = sb("decay", [P, C])
        xn = sb("xn", [P, NT, D])
        xl = sb("xl", [P, NT, D])
        xs = sb("xs", [P, C, B, T + 1])
        diff = sb("diff", [P, C, B, T])
        mixed = sb("mixed", [P, 3, C, B, T])
        k = sb("k", [P, C, B, T])
        v = sb("v", [P, C, B, T])
        r = sb("r", [P, C, B, T])
        top = sb("top", [P, C, B, T + 1])
        num = sb("num", [P, C, B, T + 1])
        den = sb("den", [P, C, B, T + 1])
        ea = sb("ea", [P, C, B, T])
        eb = sb("eb", [P, C, B, T])
        ec = w_nat[:].rearrange("p i c h -> p (i c h)").rearrange("p (c b t) -> p c b t", c=C, b=B)
        ed = xl[:].rearrange("p t d -> p (t d)").rearrange("p (c b t) -> p c b t", c=C, b=B)
        LN_W, LN_B, MIX_K, MIX_V, MIX_R, DECAY, BONUS = range(7)
        BEFORE = -3.0e38

        w_in, vec_in = sem("wkv_w_in"), sem("wkv_vec_in")
        x_in = [sem(f"x_in_{n}") for n in range(NT // 2)]
        vec_turned, vec_kept = sem("wkv_vec_turned"), sem("wkv_vec_kept")
        w_turned, w_kept = sem("wkv_w_turned"), sem("wkv_w_kept")
        xl_ready, xl_turned, xs_ready = sem("xl_ready"), sem("xl_turned"), sem("xs_ready")
        mix_ready, proj, kv_kept, r_kept = sem("mix_ready"), sem("wkv_proj"), sem("kv_kept"), sem("r_kept")
        decay_exp = sem("decay_exp")
        d_ready, cur_prev_exp, scaled_ready, scan_exp = (sem("bonus_diff"), sem("bonus_exp"), sem("scan_diff"),
                                                         sem("scan_exp"))
        clipped = sem("bonus_clipped")
        rw_ready, rw_proj = sem("rw_ready"), sem("rw_proj")
        ps = core.ps
        hidden = ins["L0_attn_hidden_state"].rearrange("b t d -> (b t) d")

        with nc.Block() as block:

            @block.sync
            def _(sp):
                for t in range(0, NT, 2):
                    sp.dma_start(x[:, t:t + 2, :], tiles(hidden)[:, t:t + 2, :]).then_inc(x_in[t // 2], 16)
                for i, name in enumerate(["ln_w", "ln_b", "mix_k", "mix_v", "mix_r", "time_decay",
                                          "current_token_weight"]):
                    sp.dma_start(vec_rows[C * i:C * i + C, :], ins["L0_attn_" + name].rearrange("(c p) -> c p", p=P)) \
                        .then_inc(vec_in, 16)
                core.prefetch(sp)

            @block.gpsimd
            def _(pool):
                for i, name in enumerate(["Wk", "Wv", "Wr", "Wo"]):
                    pool.dma_start(w_nat[:, i], ins["L0_attn_" + name].rearrange("(c p) h -> p c h", p=P)) \
                        .then_inc(w_in, 16)
                made = sem("pool_made")
                nc.gpsimd.memset(core.ident[:], 0.0).then_inc(made, 1)
                pool.wait_ge(made, 1)
                nc.gpsimd.affine_select(out=core.ident[:], in_=core.ident[:], compare_op=ALU.not_equal, fill=1.0,
                                        base=0, pattern=[[-1, P]], channel_multiplier=1).then_inc(made, 1)
                nc.gpsimd.memset(core.ones[:], 1.0).then_inc(made, 1)
                nc.gpsimd.memset(core.ln_eps[:], LN_EPS).then_inc(made, 1)
                nc.gpsimd.memset(core.l2_eps[:], 1e-6).then_inc(made, 1)
                nc.gpsimd.memset(xs[:, :, :, 0:1], 0.0).then_inc(made, 1)
                nc.gpsimd.memset(top[:, :, :, 0:1], BEFORE).then_inc(made, 1)
                nc.gpsimd.memset(num[:, :, :, 0:1], 0.0).then_inc(made, 1)
                nc.gpsimd.memset(den[:, :, :, 0:1], 0.0).then_inc(made, 1)
                core.masks(pool, sem("masks_order"))

            @block.tensor
            def _(pe):
                pe.wait_ge(sem("pool_made"), 2)
                for i in range(4):
                    pe.wait_ge(w_in, 64)
                    for h in range(C):
                        for o in range(C):
                            last = nc.tensor.transpose(ps[:, i, h * D + o * P:h * D + (o + 1) * P],
                                                       w_nat[:, i, o, h * P:(h + 1) * P], core.ident[:])
                    last.then_inc(w_turned, 1)
                pe.wait_ge(vec_in, 7 * 16)
                nc.tensor.transpose(ps[:, 4, 0:7 * C], vec_rows[:], core.ident[0:7 * C, 0:7 * C]).then_inc(vec_turned, 1)
                pe.wait_ge(vec_kept, 1)
                for b in range(B):
                    for c in range(C):
                        for t in range(TB):
                            pe.wait_ge(xl_ready, b * TB + t + 1)
                            last = nc.tensor.transpose(ps[:, 4 + 2 * b + c, t * P:(t + 1) * P],
                                                       xl[:, b * TB + t, c * P:(c + 1) * P], core.ident[:])
                    last.then_inc(xl_turned, 1)
                pe.wait_ge(w_kept, 4)
                pe.wait_ge(xs_ready, 4)
                for i in (KEY, VALUE, GATE):
                    pe.wait_ge(mix_ready, i + 1)
                    if i == GATE:
                        pe.wait_ge(kv_kept, 4)
                    for o in range(C):
                        for b in range(B):
                            bank = 4 * (i % 2) + 2 * o + b
                            for c in range(C):
                                last = nc.tensor.matmul(ps[:, bank, :], w_t[:, i, c, o * P:(o + 1) * P],
                                                        mixed[:, i, c, b, :], start=c == 0, stop=c == C - 1)
                            last.then_inc(proj, 1)
                for c in range(C):
                    pe.wait_ge(rw_ready, c + 1)
                    for t in range(NT):
                        last = nc.tensor.matmul(ps[:, 4 + t // 2, (t % 2) * D:(t % 2 + 1) * D],
                                                r[:, c, t // TB, (t % TB) * P:(t % TB + 1) * P],
                                                w_t[:, OUT, c, :], start=c == 0 and t % 2 == 0, stop=c == C - 1,
                                                skip_group_check=True)
                        if c == C - 1:
                            last.then_inc(rw_proj, 1)

            @block.scalar
            def _(act):
                a = nc.scalar.activation
                act.wait_ge(sem("pool_made"), 4)
                norm.on_act(act, core.ln_eps[:])
                for i in range(4):
                    act.wait_ge(w_turned, i + 1)
                    nc.scalar.copy(w_t[:, i].rearrange("p c o -> p (c o)"), ps[:, i, :]).then_inc(w_kept, 1)
                act.wait_ge(vec_turned, 1)
                nc.scalar.copy(vec[:].rearrange("p i c -> p (i c)"), ps[:, 4, 0:7 * C]).then_inc(vec_kept, 1)
                norm.on_act(act, core.ln_eps[:])
                act.wait_ge(vec_kept, 1)
                for b in range(B):
                    act.wait_ge(xl_turned, b + 1)
                    for c in range(C):
                        a(xs[:, c, b, 1:], ps[:, 4 + 2 * b + c, :], ACT.Identity, scale=vec[:, LN_W, c:c + 1],
                          bias=vec[:, LN_B, c:c + 1]).then_inc(xs_ready, 1)
                a(decay[:], vec[:, DECAY, :], ACT.Exp).then_inc(decay_exp, 1)

                def keep(i, o):
                    for b in range(B):
                        act.wait_ge(proj, 4 * i + 2 * o + b + 1)
                        nc.scalar.copy((k, v)[i][:, o, b, :], ps[:, 4 * i + 2 * o + b, :]).then_inc(kv_kept, 1)

                for o in range(C):
                    keep(KEY, o)
                for c in range(C):
                    act.wait_ge(d_ready, c + 1)
                    a(ea[:, c], diff[:, c], ACT.Relu).then_inc(clipped, 1)
                    a(eb[:, c], diff[:, c], ACT.Relu, scale=-1.0).then_inc(clipped, 1)
                    act.wait_ge(scaled_ready, 2 * c + 2)
                    a(ec[:, c], ec[:, c], ACT.Exp).then_inc(scan_exp, 1)
                    a(ed[:, c], ed[:, c], ACT.Exp).then_inc(scan_exp, 1)
                    act.wait_ge(clipped, 2 * c + 2)
                    a(ea[:, c], ea[:, c], ACT.Exp, scale=-1.0).then_inc(cur_prev_exp, 1)
                    a(eb[:, c], eb[:, c], ACT.Exp, scale=-1.0).then_inc(cur_prev_exp, 1)
                    keep(VALUE, c)
                for o in range(C):
                    for b in range(B):
                        act.wait_ge(proj, 8 + 2 * o + b + 1)
                        a(r[:, o, b, :], ps[:, 2 * o + b, :], ACT.Sigmoid).then_inc(r_kept, 1)
                norm.on_act(act, core.ln_eps[:])

            @block.vector
            def _(dve):
                V = nc.vector
                link = chain(dve, sem("dve_order"), core.dve_count)
                for t in range(NT):
                    dve.wait_ge(x_in[t // 2], 16)
                    last = norm.tile_stats(x, t)
                link(last)
                norm.gather_stats().then_inc(norm.var_ready, 1)
                norm.inverse_std(dve, link)
                variance = norm.mv[:, :, 1]
                link(V.tensor_tensor(variance, variance, norm.inv[:], ALU.mult))
                V.tensor_tensor(variance, variance, norm.inv[:], ALU.mult).then_inc(norm.var_ready, 1)
                link(norm.normalize(x, xn))
                norm.inverse_std(dve, link)
                for t in range(NT):
                    V.tensor_scalar(xl[:, t, :], xn[:, t, :], norm.inv[:, t:t + 1], None, ALU.mult) \
                        .then_inc(xl_ready, 1)
                dve.wait_ge(xs_ready, 4)
                dve.wait_ge(sem("pool_made"), 9)
                dve.wait_ge(vec_kept, 1)
                for c in range(C):
                    last = V.tensor_tensor(diff[:, c], xs[:, c, :, 1:], xs[:, c, :, :T], ALU.subtract)
                link(last)
                for i in (KEY, VALUE, GATE):
                    for c in range(C):
                        last = V.scalar_tensor_tensor(mixed[:, i, c], diff[:, c], vec[:, MIX_K + i, c:c + 1],
                                                      xs[:, c, :, :T], ALU.mult, ALU.add)
                    last.then_inc(mix_ready, 1)
                dve.wait_ge(decay_exp, 1)
                link(V.tensor_scalar(decay[:], decay[:], -1.0, None, ALU.mult))
                dve.wait_ge(w_kept, 4)
                for c in range(C):
                    dve.wait_ge(kv_kept, 2 * c + 2)
                    for b in range(B):
                        last = V.tensor_tensor_scan(top[:, c, b, 1:], decay[:, c:c + 1].to_broadcast([P, T]),
                                                    k[:, c, b, :], BEFORE, ALU.add, ALU.max)
                    link(last)
                    V.scalar_tensor_tensor(diff[:, c], k[:, c], vec[:, BONUS, c:c + 1], top[:, c, :, :T],
                                           ALU.add, ALU.subtract).then_inc(d_ready, 1)
                    V.scalar_tensor_tensor(ec[:, c], top[:, c, :, :T], decay[:, c:c + 1], top[:, c, :, 1:],
                                           ALU.add, ALU.subtract).then_inc(scaled_ready, 1)
                    V.tensor_tensor(ed[:, c], k[:, c], top[:, c, :, 1:], ALU.subtract).then_inc(scaled_ready, 1)
                for c in range(C):
                    dve.wait_ge(kv_kept, 4 + 2 * c + 2)
                    dve.wait_ge(scan_exp, 2 * c + 2)
                    dve.wait_ge(clipped, 2 * c + 2)
                    link(V.tensor_tensor(diff[:, c], ed[:, c], v[:, c], ALU.mult))
                    for b in range(B):
                        V.tensor_tensor_scan(num[:, c, b, 1:], ec[:, c, b, :], diff[:, c, b, :], 0.0,
                                             ALU.mult, ALU.add)
                        last = V.tensor_tensor_scan(den[:, c, b, 1:], ec[:, c, b, :], ed[:, c, b, :], 0.0,
                                                    ALU.mult, ALU.add)
                    link(last)
                    dve.wait_ge(cur_prev_exp, 2 * c + 2)
                    V.tensor_tensor(diff[:, c], ea[:, c], num[:, c, :, :T], ALU.mult)
                    V.tensor_tensor(ec[:, c], eb[:, c], v[:, c], ALU.mult)
                    link(V.tensor_tensor(ed[:, c], ea[:, c], den[:, c, :, :T], ALU.mult))
                    V.tensor_tensor(ea[:, c], ed[:, c], eb[:, c], ALU.add)
                    link(V.tensor_tensor(diff[:, c], diff[:, c], ec[:, c], ALU.add))
                    link(V.reciprocal(ea[:, c], ea[:, c]))
                    link(V.tensor_tensor(diff[:, c], diff[:, c], ea[:, c], ALU.mult))
                    dve.wait_ge(r_kept, 2 * c + 2)
                    V.tensor_tensor(r[:, c], r[:, c], diff[:, c], ALU.mult).then_inc(rw_ready, 1)

                def mixed_in(t):
                    if t % 2 == 0:
                        dve.wait_ge(rw_proj, t + 2)
                        link(V.tensor_tensor(xn[:, t:t + 2, :], xn[:, t:t + 2, :],
                                             ps[:, 4 + t // 2, :].rearrange("p (t d) -> p t d", t=2), ALU.add))

                link(norm.on_dve(dve, link, xn, xl, arrived=mixed_in))
                link(V.tensor_tensor(x[:], x[:], xl[:], ALU.add))


def expert_choice(core, ins):
    nc, sem, norm, x, ps = core.nc, core.sem, core.norm, core.x, core.ps
    E = 16
    K = N // E
    W = D + E
    WARM_UP = 30
    core.late_weights(ins)
    with ExitStack() as own:
        def sb(name, shape):
            return own.enter_context(nc.sbuf_tensor(name, shape, F32))

        xf = sb("xf", [P, NT, D])
        xf_t = sb("xf_t", [P, C, N])
        both = sb("z_logits", [P, NT, W])
        z, logits = both[:, :, 0:D], both[:, :, D:]
        low = sb("logit_max", [P, NT])
        total = sb("exp_sum", [P, NT])
        probs = sb("probs", [P, NT, E])
        probs_t = sb("probs_t", [E, N])
        left = sb("left", [E, N])
        best = sb("best", [E, 8])
        chosen = sb("chosen", [E, N])
        g = sb("g", [P, NT])
        xf_ready, xf_turned, xf_kept = sem("xf_ready"), sem("xf_turned"), sem("xf_kept")
        z_done, z_kept = sem("z_done"), sem("z_kept")
        exp_in, exp_out, probs_ready = sem("exp_in"), sem("exp_out"), sem("probs_ready")
        probs_turned, probs_kept, chosen_ready, g_done = (sem("probs_turned"), sem("probs_kept"),
                                                          sem("chosen_ready"), sem("g_done"))
        with nc.Block() as block:

            @block.sync
            def _(sp):
                core.prefetch_late(sp)

            @block.tensor
            def _(pe):
                pe.wait_ge(core.w_in, core.w_in_total)
                for n in range(WARM_UP):
                    nc.tensor.transpose(ps[:, 7, 0:P], core.ident[:], core.ident[:])
                pe.wait_ge(xf_ready, NT)
                for b in range(B):
                    for c in range(C):
                        for t in range(TB):
                            last = nc.tensor.transpose(ps[:, 2 * b + c, t * P:(t + 1) * P],
                                                       xf[:, b * TB + t, c * P:(c + 1) * P], core.ident[:])
                        last.then_inc(xf_turned, 1)
                for n in range(NT):
                    t = (n + 4) % NT
                    pe.wait_ge(xf_kept, 4 if n >= 4 or t >= 4 else 2)
                    for c in range(C):
                        last = nc.tensor.matmul(ps[:, t, 0:W], xf_t[:, c, t * P:(t + 1) * P], core.w_ec[:, c, :],
                                                start=c == 0, stop=c == C - 1)
                    last.then_inc(z_done, 1)
                pe.wait_ge(probs_ready, 1)
                pe.wait_ge(z_kept, NT)
                for t in range(NT):
                    last = nc.tensor.transpose(ps[0:E, t // 4, (t % 4) * P:(t % 4 + 1) * P], probs[:, t, :],
                                               core.ident[:])
                last.then_inc(probs_turned, 1)
                pe.wait_ge(chosen_ready, 1)
                for t in range(NT):
                    last = nc.tensor.matmul(ps[:, 2, t:t + 1], chosen[:, t * P:(t + 1) * P], core.ones[0:E, 0:1],
                                            start=True, stop=True)
                last.then_inc(g_done, 1)

            @block.scalar
            def _(act):
                norm.on_act(act, core.ln_eps[:])
                for b in range(B):
                    for c in range(C):
                        act.wait_ge(xf_turned, 2 * b + c + 1)
                        nc.scalar.copy(xf_t[:, c, b * T:(b + 1) * T], ps[:, 2 * b + c, :]).then_inc(xf_kept, 1)
                act.wait_ge(exp_in, 1)
                nc.scalar.activation(probs[:], logits, ACT.Exp).then_inc(exp_out, 1)
                norm.on_act(act, core.ln_eps[:])

            @block.vector
            def _(dve):
                V = nc.vector
                link = chain(dve, sem("dve_order"), core.dve_count)
                norm.on_dve(dve, link, x, xf, ready=xf_ready)
                for n in range(NT):
                    t = (n + 4) % NT
                    dve.wait_ge(z_done, n + 1)
                    V.tensor_tensor(both[:, t, :], ps[:, t, 0:W], core.b_ec[:], ALU.add).then_inc(z_kept, 1)
                    if n:
                        dve.wait_ge(z_kept, n)
                        norm.tile_stats(z, (n + 3) % NT)
                dve.wait_ge(z_kept, NT)
                link(norm.tile_stats(z, (NT + 3) % NT))
                link(norm.gather_stats())
                link(V.tensor_reduce(low[:], logits, AX_X, ALU.max))
                V.tensor_tensor(logits, logits, low[:].unsqueeze(2).to_broadcast([P, NT, E]),
                                ALU.subtract).then_inc(exp_in, 1)
                dve.wait_ge(exp_out, 1)
                link(V.tensor_reduce(total[:], probs[:], AX_X, ALU.add))
                link(V.reciprocal(total[:], total[:]))
                V.tensor_tensor(probs[:], probs[:], total[:].unsqueeze(2).to_broadcast([P, NT, E]),
                                ALU.mult).then_inc(probs_ready, 1)
                dve.wait_ge(probs_turned, 1)
                link(V.tensor_copy(probs_t[:], ps[0:E, 0:2, :].rearrange("p a b -> p (a b)")))
                for n in range(0, K, 8):
                    src = probs_t if n == 0 else left
                    link(V.max(best[:], src[:]))
                    link(V.match_replace(left[:], best[:], src[:], 0.0))
                V.tensor_tensor(chosen[:], probs_t[:], left[:], ALU.subtract).then_inc(chosen_ready, 1)
                dve.wait_ge(g_done, 1)
                link(V.tensor_copy(g[:], ps[:, 2, 0:NT]))
                link(V.tensor_tensor(norm.mv[:, :, 1], norm.mv[:, :, 1], g[:], ALU.mult))
                V.tensor_tensor(norm.mv[:, :, 1], norm.mv[:, :, 1], g[:], ALU.mult).then_inc(norm.var_ready, 1)
                norm.inverse_std(dve, link)
                link(V.tensor_tensor(norm.inv[:], norm.inv[:], g[:], ALU.mult))
                link(norm.normalize(z, xf))
                link(V.tensor_tensor(x[:], x[:], xf[:], ALU.add))


def delta_attention(core, ins):
    nc, sem, norm, x, ps, ident = core.nc, core.sem, core.norm, core.x, core.ps, core.ident
    H, DK, CH = 16, 16, 32
    HH = H // C
    G = B * C
    NCH = T // CH
    GROUP = P // CH
    GROUPS = NCH // GROUP
    TAPS = 4
    WARM_UP = 22
    X_, Q_, K_, V_ = range(4)
    strand = [slice(q * CH, (q + 1) * CH) for q in range(G)]

    outer = ExitStack()

    def place(stack):
        return lambda name, shape: stack.enter_context(nc.sbuf_tensor(name, shape, F32))

    def features(ap):
        return ap.rearrange("p h d -> p (h d)")

    with outer:
        sb = place(outer)
        qkv_rows = sb("qkv", [P, NCH, 3, P])
        qkv = qkv_rows[:].rearrange("p n a (h d) -> p n a h d", h=HH)
        q_t = qkv_rows[:, :, 0].rearrange("p n (q i) -> p n q i", q=G)
        k_t = sb("k_t", [P, NCH, G, CH])
        qk_t = sb("qk_t", [P, NCH, HH, CH])
        beta = sb("beta", [P, NCH, HH])
        n_t = sb("n_t", [P, NCH, HH, CH])
        half = NCH // 2
        stage = ExitStack()
        kbd_first = place(stage)("kbd_first", [P, HH, half, G, CH])

        xa_ready, conv_done, conv_kept = sem("xa_ready"), sem("conv_done"), sem("conv_kept")
        conv_kept_dve = sem("conv_kept_dve")
        qkv_done, silu_done, beta_done = sem("qkv_done"), sem("silu_done"), sem("beta_done")
        ss_ready, ss_root, kq_ready = sem("ss_ready"), sem("ss_root"), sem("kq_ready")
        kq_turned, k_kept, q_kept = sem("kq_turned"), sem("k_kept"), sem("q_kept")
        masked_beta = sem("masked_beta")
        spread_act, spread_dve, spread_pool = sem("kbd_on_act"), sem("kbd_on_dve"), sem("kbd_on_pool")
        with stage:
            sb = place(stage)
            xc = sb("xc", [P, C, 4, N])
            xa = qk_t[:].rearrange("p n h i -> p (n h i)")[:, 0:NT * D].rearrange("p (t d) -> p t d", t=NT)
            sq = qk_t[:].rearrange("p n h i -> p (n h i)")[:, NT * D:].rearrange("p (s n f) -> p s n f", s=2, n=GROUP)
            kbd_second = xc[:].rearrange("p c k t -> p (c k t)").rearrange("p (h n q i) -> p h n q i", h=HH, n=half,
                                                                           q=G)
            kbd = (kbd_first, kbd_second)
            ss = sb("ss", [P, NCH, 2 * HH])
            PROJ_BANKS, K_BANK, Q_BANK, BETA_BANK = 5, 5, 6, 7
            TURN_LAG = 3
            WHICH_BANK = (Q_BANK, K_BANK)
            pair_done, n_masked, qk_flipped = sem("pair_done"), sem("n_masked"), sem("qk_flipped")
            KK = HH * CH
            PAIR_BANKS = 5
            ACT_HEADS, DVE_HEADS, POOL_HEADS = range(0, 4), range(4, 7), range(7, 8)

            def spread_out(eng, scale, heads, g):
                eng.wait_ge(k_kept, g + 1)
                if g >= GROUPS // 2:
                    eng.wait_ge(qkv_done, NCH)
                for h in heads:
                    place_ = kbd[g // 2][:, h, g % 2 * GROUP:(g % 2 + 1) * GROUP].rearrange("p n q i -> p (n q i)")
                    keys = k_t[:, g * GROUP:(g + 1) * GROUP].rearrange("p n q i -> p (n q i)")
                    last = scale(place_, keys, core.own_head[:, h:h + 1])
                return last

            with nc.Block() as block:

                @block.gpsimd
                def _(pool):
                    def scale(out, keys, own):
                        return nc.gpsimd.tensor_scalar(out, keys, own, 0.0, ALU.mult, ALU.add)

                    for g in range(GROUPS // 2):
                        spread_out(pool, scale, POOL_HEADS, g).then_inc(spread_pool, 1)
                    pool.wait_ge(beta_done, 1)
                    nc.gpsimd.tensor_tensor(n_t[:],
                                            core.above[:].unsqueeze(1).unsqueeze(1).to_broadcast([P, NCH, HH, CH]),
                                            beta[:].unsqueeze(3).to_broadcast([P, NCH, HH, CH]), ALU.mult)                         .then_inc(masked_beta, 1)
                    for g in range(GROUPS // 2, GROUPS):
                        spread_out(pool, scale, POOL_HEADS, g).then_inc(spread_pool, 1)
                    for n in range(0, NCH, 2):
                        pool.wait_ge(qk_flipped, n + 2)
                        nc.gpsimd.tensor_tensor(qk_t[:, n:n + 2], qk_t[:, n:n + 2],
                                                core.upto[:].unsqueeze(1).unsqueeze(1).to_broadcast([P, 2, HH, CH]),
                                                ALU.mult)

                @block.tensor
                def _(pe):
                    for n in range(WARM_UP):
                        nc.tensor.transpose(ps[:, 0, 0:P], ident[:], ident[:])
                    for t in range(NT):
                        pe.wait_ge(xa_ready, t + 1)
                        for c in range(C):
                            n = 2 * t + c
                            if n >= 8:
                                pe.wait_ge((conv_kept, conv_kept_dve)[c], t - 3)
                            lead = t % TB == 0
                            last = nc.tensor.matmul(ps[:, n % 8, :], xa[:, t, c * P:(c + 1) * P],
                                                    core.conv[:, :, 0:P], start=True, stop=lead)
                            if not lead:
                                out = ps[:, n % 8, :].rearrange("p (k t) -> p k t", k=4)[:, 1:4, 0:TAPS - 1]
                                last = nc.tensor.matmul(out, xa[:, t - 1, c * P:(c + 1) * P],
                                                        core.conv[:, 1:4, P:P + TAPS - 1], start=False, stop=True)
                            last.then_inc(conv_done, 1)
                    pe.wait_ge(conv_kept, NT)
                    pe.wait_ge(conv_kept_dve, NT)

                    def turn(g):
                        pe.wait_ge(kq_ready, g + 1)
                        if g:
                            pe.wait_ge(k_kept, g)
                            pe.wait_ge(q_kept, g)
                        for which in (1, 0):
                            for i in range(GROUP):
                                last = nc.tensor.transpose(ps[:, WHICH_BANK[which], i * P:(i + 1) * P],
                                                           features(qkv[:, g * GROUP + i, which]), ident[:])
                            last.then_inc(kq_turned, 1)

                    for n in range(NCH):
                        if n >= PROJ_BANKS:
                            pe.wait_ge(silu_done, n - PROJ_BANKS + 1)
                        bank = n % PROJ_BANKS
                        for which, src in enumerate((Q_, K_, V_)):
                            for ci in range(C):
                                for q in range(G):
                                    b, c = q // C, q % C
                                    last = nc.tensor.matmul(ps[strand[q], bank, which * P:(which + 1) * P],
                                                            xc[:, ci, src, b * T + n * CH:b * T + (n + 1) * CH],
                                                            core.w_qkv[:, which, ci, c * P:(c + 1) * P],
                                                            start=ci == 0, stop=ci == C - 1, skip_group_check=True)
                        for ci in range(C):
                            for q in range(G):
                                b, c = q // C, q % C
                                last = nc.tensor.matmul(ps[strand[q], BETA_BANK, n * HH:(n + 1) * HH],
                                                        xc[:, ci, X_, b * T + n * CH:b * T + (n + 1) * CH],
                                                        core.w_beta[:, ci, c * HH:(c + 1) * HH],
                                                        start=ci == 0, stop=ci == C - 1, skip_group_check=True)
                        last.then_inc(qkv_done, 1)
                        if n % GROUP == TURN_LAG - 1 and n >= GROUP:
                            turn(n // GROUP - 1)

                    def inside_chunks(g):
                        for spread in (spread_act, spread_dve, spread_pool):
                            pe.wait_ge(spread, g + 1)
                        pe.wait_ge(q_kept, g + 1)
                        for n in range(g * GROUP, (g + 1) * GROUP):
                            if n >= PAIR_BANKS:
                                pe.wait_ge(qk_flipped, n - PAIR_BANKS + 1)
                            for which, src in enumerate((k_t, q_t)):
                                for q in range(G):
                                    last = nc.tensor.matmul(
                                        ps[strand[q], n % PAIR_BANKS, which * KK:(which + 1) * KK], src[:, n, q, :],
                                        kbd[n // half][:, :, n % half, q, :], start=True, stop=True,
                                        skip_group_check=True)
                            last.then_inc(pair_done, 1)

                    pe.wait_ge(silu_done, NCH)
                    inside_chunks(0)
                    turn(GROUPS - 1)
                    for g in range(1, GROUPS):
                        inside_chunks(g)

                @block.scalar
                def _(act):
                    a = nc.scalar.activation
                    norm.on_act(act, core.ln_eps[:])
                    for t in range(NT):
                        act.wait_ge(conv_done, 2 * t + 1)
                        nc.scalar.copy(xc[:, 0, :, t * P:(t + 1) * P],
                                       ps[:, 2 * t % 8, :].rearrange("p (k t) -> p k t", k=4)).then_inc(conv_kept, 1)

                    def keep_keys(g):
                        act.wait_ge(kq_turned, 2 * g + 1)
                        nc.scalar.copy(k_t[:, g * GROUP:(g + 1) * GROUP].rearrange("p n q i -> p (n q i)"),
                                       ps[:, K_BANK, :]).then_inc(k_kept, 1)

                    def scale(out, keys, own):
                        return a(out, keys, ACT.Copy, scale=own)

                    for n in range(NCH):
                        g = n // GROUP
                        act.wait_ge(qkv_done, n + 1)
                        a(qkv_rows[:, n].rearrange("p a f -> p (a f)"), ps[:, n % PROJ_BANKS, 0:3 * P], ACT.Silu)                             .then_inc(silu_done, 1)
                        if n % GROUP == TURN_LAG - 1 and g:
                            keep_keys(g - 1)
                        if n % GROUP == GROUP - 1 and 0 < g < GROUPS - 1:
                            spread_out(act, scale, ACT_HEADS, g - 1).then_inc(spread_act, 1)
                        if n == NCH - 1:
                            a(beta[:].rearrange("p n h -> p (n h)"), ps[:, BETA_BANK, 0:NCH * HH], ACT.Sigmoid)                                 .then_inc(beta_done, 1)
                        if n % GROUP == GROUP - 1:
                            own = slice(g * GROUP, (g + 1) * GROUP)
                            act.wait_ge(ss_ready, g + 1)
                            a(ss[:, own], ss[:, own], ACT.Sqrt, bias=core.l2_eps[:]).then_inc(ss_root, 1)
                    spread_out(act, scale, ACT_HEADS, GROUPS - 2).then_inc(spread_act, 1)
                    keep_keys(GROUPS - 1)
                    spread_out(act, scale, ACT_HEADS, GROUPS - 1).then_inc(spread_act, 1)

                @block.vector
                def _(dve):
                    V = nc.vector
                    link = chain(dve, sem("dve_order"), core.dve_count)
                    norm.on_dve(dve, link, x, xa, ready=xa_ready)
                    for t in range(NT):
                        dve.wait_ge(conv_done, 2 * t + 2)
                        V.tensor_copy(xc[:, 1, :, t * P:(t + 1) * P],
                                      ps[:, (2 * t + 1) % 8, :].rearrange("p (k t) -> p k t", k=4)) \
                            .then_inc(conv_kept_dve, 1)

                    def scale(out, keys, own):
                        return V.tensor_scalar(out, keys, own, None, ALU.mult)

                    def keep_queries(g):
                        dve.wait_ge(kq_turned, 2 * g + 2)
                        V.tensor_copy(qkv_rows[:, g * GROUP:(g + 1) * GROUP, 0],
                                      ps[:, Q_BANK, :].rearrange("p (n f) -> p n f", n=GROUP)).then_inc(q_kept, 1)

                    for g in range(GROUPS):
                        own = slice(g * GROUP, (g + 1) * GROUP)
                        if g:
                            keep_queries(g - 1)
                        dve.wait_ge(silu_done, (g + 1) * GROUP)
                        rows = qkv_rows[:, own, 0:2].rearrange("p n a f -> p n (a f)")
                        link(V.tensor_tensor(sq[:, g % 2], rows, rows, ALU.mult))
                        V.tensor_reduce(ss[:, own], sq[:, g % 2].rearrange("p n (a d) -> p n a d", d=DK), AX_X,
                                        ALU.add).then_inc(ss_ready, 1)
                        dve.wait_ge(ss_root, g + 1)
                        link(V.reciprocal(ss[:, own], ss[:, own]))
                        link(V.tensor_scalar(ss[:, own, 0:HH], ss[:, own, 0:HH], float(DK) ** -0.5, None, ALU.mult))
                        rows = qkv_rows[:, own, 0:2].rearrange("p n a (h d) -> p n (a h) d", d=DK)
                        V.tensor_tensor(rows, rows, ss[:, own].unsqueeze(3).to_broadcast([P, GROUP, 2 * HH, DK]),
                                        ALU.mult).then_inc(kq_ready, 1)
                        if 0 < g < GROUPS - 1:
                            spread_out(dve, scale, DVE_HEADS, g - 1).then_inc(spread_dve, 1)

                    def take_out(n):
                        dve.wait_ge(pair_done, n + 1)
                        V.tensor_tensor(n_t[:, n], n_t[:, n],
                                        ps[:, n % PAIR_BANKS, 0:KK].rearrange("p (h i) -> p h i", h=HH),
                                        ALU.mult).then_inc(n_masked, 1)
                        V.transpose(qk_t[:, n].rearrange("p h i -> p (h i)"), ps[:, n % PAIR_BANKS, KK:])                             .then_inc(qk_flipped, 1)

                    spread_out(dve, scale, DVE_HEADS, GROUPS - 2).then_inc(spread_dve, 1)
                    dve.wait_ge(masked_beta, 1)
                    dve.wait_ge(ss_ready, GROUPS)
                    for n in range(2):
                        take_out(n)
                    keep_queries(GROUPS - 1)
                    spread_out(dve, scale, DVE_HEADS, GROUPS - 1).then_inc(spread_dve, 1)
                    for n in range(2, NCH):
                        take_out(n)

        r_t = outer.enter_context(nc.sbuf_tensor("r_t", [P, NCH, HH, CH], F32))
        n_turned, n_kept, n_kept_dve = sem("n_turned"), sem("n_kept"), sem("n_kept_dve")
        inv_done, r_turned, r_kept = sem("inv_done"), sem("r_turned"), sem("r_kept")
        ROWS = 4
        with ExitStack() as stage:
            sb = place(stage)
            nm = sb("nm", [P, CH, G, CH])
            inv = sb("inv", [P, CH, G, CH])
            terms = sb("terms", [P, G * CH * CH // 4])
            with nc.Block() as block:

                @block.tensor
                def _(pe):
                    cols = n_t[:].rearrange("p n h i -> p (n h) i")
                    for n in range(CH // ROWS):
                        for i in range(n * ROWS, (n + 1) * ROWS):
                            last = nc.tensor.transpose(ps[:, n, (i % ROWS) * P:(i % ROWS + 1) * P], cols[:, :, i],
                                                       ident[:])
                        last.then_inc(n_turned, 1)
                    for n in range(CH // ROWS):
                        pe.wait_ge(inv_done, n + 1)
                        if n == 0:
                            pe.wait_ge(n_kept, CH // ROWS)
                        for i in range(n * ROWS, (n + 1) * ROWS):
                            last = nc.tensor.transpose(ps[:, n, (i % ROWS) * P:(i % ROWS + 1) * P],
                                                       inv[:, i].rearrange("p g c -> p (g c)"), ident[:])
                        last.then_inc(r_turned, 1)

                @block.scalar
                def _(act):
                    for n in range(CH // ROWS):
                        act.wait_ge(n_turned, n + 1)
                        nc.scalar.copy(nm[:, n * ROWS:(n + 1) * ROWS].rearrange("p i g j -> p (i g j)"),
                                       ps[:, n, :]).then_inc(n_kept, 1)
                    for n in range(CH // ROWS):
                        act.wait_ge(r_turned, n + 1)
                        nc.scalar.copy(r_t[:].rearrange("p n h i -> p i (n h)")[:, n * ROWS:(n + 1) * ROWS],
                                       ps[:, n, :].rearrange("p (i h) -> p i h", i=ROWS)).then_inc(r_kept, 1)

                @block.vector
                def _(dve):
                    V = nc.vector
                    link = chain(dve, sem("dve_order"), core.dve_count)
                    link(V.memset(inv[:], 0.0))
                    flat = inv[:].rearrange("p i g j -> p (i g j)")
                    for g in range(G):
                        last = V.memset(flat[:, g * CH::G * CH + 1], 1.0)
                    link(last)
                    dve.wait_ge(n_kept, CH // ROWS)
                    for j in range(CH - 1):
                        below = CH - 1 - j
                        part = terms[:, 0:below * G * (j + 1)].rearrange("p (i g c) -> p i g c", g=G, c=j + 1)
                        link(V.tensor_tensor(part, nm[:, j + 1:, :, j:j + 1].to_broadcast([P, below, G, j + 1]),
                                             inv[:, j, :, 0:j + 1].unsqueeze(1).to_broadcast([P, below, G, j + 1]),
                                             ALU.mult))
                        last = V.tensor_tensor(inv[:, j + 1:, :, 0:j + 1], inv[:, j + 1:, :, 0:j + 1], part,
                                               ALU.subtract)
                        i = j + 1
                        if i % ROWS == ROWS - 1:
                            last.then_inc(inv_done, 1)
                            dve.wait_ge(inv_done, i // ROWS + 1)
                        else:
                            link(last)

        wu_done, wu_kept, wu_ready = sem("wu_done"), sem("wu_kept"), sem("wu_ready")
        wu_ready_dve = sem("wu_ready_dve")
        w_turned, w_kept = sem("delta_w_turned"), sem("delta_w_kept")
        with ExitStack() as stage:
            sb = place(stage)
            wu = n_t[:].rearrange("p n h i -> p (n h i)").rearrange("p (n a h d) -> p n a h d", n=NCH, a=2, h=HH)
            w_t = k_t
            state = sb("state", [P, NCH, G, CH])
            HPAIRS = HH * DK // CH
            heads = [slice(a * CH, (a + 1) * CH) for a in range(HPAIRS)]
            u = sb("u", [P, NCH, P])
            u_bd = (sb("u_bd", [P, NCH // 2, HH, G, DK]),
                    r_t[:].rearrange("p n h i -> p (n h i)").rearrange("p (n h q e) -> p n h q e", n=NCH // 2,
                                                                       h=HH, q=G))

            def u_diagonal(n):
                return u_bd[n // half][:, n % half]

            PAIR = 2
            PAIRS = NCH // PAIR
            ON_ACT, ON_DVE = (0, 1), (2, 3)
            ws_done, u_ready, ku_done, state_ready = (sem("ws_done"), sem("u_ready"), sem("ku_done"),
                                                      sem("state_ready"))
            qs_done = sem("qs_done")
            WS_COLS = slice(GROUPS * P - CH, GROUPS * P)

            def strands_of(b):
                return range(b * C, (b + 1) * C)

            with nc.Block() as block:

                def pair_of(rows, m):
                    own = slice(m * PAIR, (m + 1) * PAIR)
                    count = rows.stop - rows.start
                    return (wu[rows, own].rearrange("p n a h d -> p n h a d"),
                            beta[rows, own].unsqueeze(3).to_broadcast([count, PAIR, HH, 2 * DK]))

                @block.tensor
                def _(pe):
                    for m in range(PAIRS):
                        if m >= 2:
                            pe.wait_ge(wu_kept, len(ON_ACT) * (m - 1))
                            pe.wait_ge(wu_ready_dve, len(ON_DVE) * (m - 1))
                        for i in range(PAIR):
                            n = m * PAIR + i
                            for h in range(HH):
                                for q in range(G):
                                    place_ = (i * HH + h) * 2 * DK
                                    last = nc.tensor.matmul(ps[strand[q], G * (m % 2) + q, place_:place_ + 2 * DK],
                                                            r_t[strand[q], n, h, :], qkv[strand[q], n, 1:3, h, :],
                                                            start=True, stop=True, skip_group_check=True)
                        last.then_inc(wu_done, 1)

                    def turn_w(g):
                        pe.wait_ge(wu_ready, 2 * (g + 1))
                        pe.wait_ge(wu_ready_dve, 2 * len(ON_DVE) * (g + 1))
                        for i in range(GROUP):
                            last = nc.tensor.transpose(ps[:, g, i * P:(i + 1) * P],
                                                       features(wu[:, g * GROUP + i, 0]), ident[:])
                        last.then_inc(w_turned, 1)

                    pe.wait_ge(wu_kept, len(ON_ACT) * (PAIRS - 1))
                    pe.wait_ge(wu_ready_dve, len(ON_DVE) * (PAIRS - 1))
                    for g in range(GROUPS - 1):
                        turn_w(g)
                    pe.wait_ge(wu_kept, len(ON_ACT) * PAIRS)
                    pe.wait_ge(wu_ready_dve, len(ON_DVE) * PAIRS)
                    for n in range(NCH):
                        for b in range(B if n else 0):
                            pe.wait_ge(state_ready, B * (n - 1) + b + 1)
                            for a in range(HPAIRS):
                                for q in strands_of(b):
                                    last = nc.tensor.matmul(ps[strand[q], a, WS_COLS], w_t[heads[a], n, q, :],
                                                            state[heads[a], n, q, :], start=True, stop=True,
                                                            skip_group_check=True)
                            last.then_inc(ws_done, 1)
                        for b in range(B):
                            pe.wait_ge(u_ready, B * n + b + 1)
                            if n == NCH - 1:
                                continue
                            for a in range(HPAIRS):
                                for q in strands_of(b):
                                    last = nc.tensor.matmul(ps[heads[a], G + q, 0:CH],
                                                            qkv_rows[strand[q], n, 1, heads[a]],
                                                            u[strand[q], n, heads[a]], start=n == 0,
                                                            stop=n == NCH - 2, skip_group_check=True)
                            last.then_inc(ku_done, 1)
                        if n == 0:
                            turn_w(GROUPS - 1)
                            pe.wait_ge(w_kept, GROUPS)
                        held_back = [(m, G - 1) for m in range(NCH - GROUP, NCH)]
                        now = [(n, q) for q in range(G) if (n, q) not in held_back]
                        for m, q in now + (held_back if n == NCH - 1 else []):
                            rows = slice(m % GROUP * CH, (m % GROUP + 1) * CH)
                            cols = slice(m // GROUP * P + q * CH, m // GROUP * P + (q + 1) * CH)
                            for a in range(HPAIRS):
                                last = nc.tensor.matmul(ps[rows, a, cols], q_t[heads[a], m, q, :],
                                                        state[heads[a], m, q, :], start=True, stop=True,
                                                        skip_group_check=True)
                        last.then_inc(qs_done, 1)

                @block.scalar
                def _(act):
                    for m in range(PAIRS):
                        act.wait_ge(wu_done, m + 1)
                        for q in ON_ACT:
                            own = wu[strand[q], m * PAIR:(m + 1) * PAIR].rearrange("p n a h d -> p n h a d")
                            nc.scalar.copy(own, ps[strand[q], G * (m % 2) + q, :]
                                           .rearrange("p (n h a d) -> p n h a d", n=PAIR, h=HH, a=2)) \
                                .then_inc(wu_kept, 1)
                    for g in range(GROUPS):
                        act.wait_ge(w_turned, g + 1)
                        nc.scalar.copy(w_t[:, g * GROUP:(g + 1) * GROUP].rearrange("p n q i -> p (n q i)"),
                                       ps[:, g, :]).then_inc(w_kept, 1)
                    for n in range(NCH):
                        act.wait_ge(u_ready, B * (n + 1))
                        if n == half:
                            act.wait_ge(sem("u_bd_zeroed_late"), 1)
                        for q in range(G):
                            nc.scalar.copy(u_diagonal(n)[strand[q], :, q, :],
                                           u[strand[q], n].rearrange("p (h e) -> p h e", h=HH))

                @block.gpsimd
                def _(pool):
                    rows = slice(0, len(ON_ACT) * CH)
                    for m in range(PAIRS):
                        pool.wait_ge(wu_kept, len(ON_ACT) * (m + 1))
                        own = wu[rows, m * PAIR:(m + 1) * PAIR].rearrange("p n a h d -> p n a (h d)")
                        for i in range(PAIR):
                            n = m * PAIR + i
                            last = nc.gpsimd.tensor_tensor(
                                wu[rows, n], wu[rows, n],
                                beta[rows, n].unsqueeze(1).unsqueeze(3).to_broadcast([len(ON_ACT) * CH, 2, HH, DK]),
                                ALU.mult)
                        last.then_inc(wu_ready, 1)
                    pool.wait_ge(wu_done, PAIRS)
                    nc.gpsimd.memset(u_bd[1], 0.0).then_inc(sem("u_bd_zeroed_late"), 1)

                @block.vector
                def _(dve):
                    V = nc.vector
                    V.memset(state[:, 0], 0.0).then_inc(sem("state_zeroed"), 1)
                    V.memset(u_bd[0][:], 0.0).then_inc(sem("u_bd_zeroed"), 1)
                    for m in range(PAIRS):
                        dve.wait_ge(wu_done, m + 1)
                        for q in ON_DVE:
                            for i in range(PAIR):
                                n = m * PAIR + i
                                src = ps[strand[q], G * (m % 2) + q, i * HH * 2 * DK:(i + 1) * HH * 2 * DK]
                                last = V.tensor_tensor(
                                    wu[strand[q], n], src.rearrange("p (h a d) -> p a h d", h=HH, a=2),
                                    beta[strand[q], n].unsqueeze(1).unsqueeze(3).to_broadcast([CH, 2, HH, DK]),
                                    ALU.mult)
                            last.then_inc(wu_ready_dve, 1)
                    for n in range(NCH):
                        for b in range(B):
                            rows = slice(b * C * CH, (b + 1) * C * CH)
                            if n == 0:
                                dve.wait_ge(wu_ready, 1)
                                dve.wait_ge(wu_ready_dve, len(ON_DVE))
                                V.tensor_copy(u[rows, 0], features(wu[rows, 0, 1])).then_inc(u_ready, 1)
                                continue
                            dve.wait_ge(ws_done, B * (n - 1) + b + 1)
                            V.tensor_tensor(u[rows, n].rearrange("p (a e) -> p a e", a=HPAIRS),
                                            features(wu[rows, n, 1]).rearrange("p (a e) -> p a e", a=HPAIRS),
                                            ps[rows, 0:HPAIRS, WS_COLS], ALU.subtract).then_inc(u_ready, 1)
                        for b in range(B if n < NCH - 1 else 0):
                            dve.wait_ge(ku_done, B * n + b + 1)
                            V.tensor_tensor(state[:, n + 1, b * C:(b + 1) * C],
                                            ps[:, G + b * C:G + (b + 1) * C, 0:CH],
                                            core.same_of_pair[:].unsqueeze(1).to_broadcast([P, C, CH]),
                                            ALU.mult).then_inc(state_ready, 1)

            qs_kept, au_done, o_ready = sem("qs_kept"), sem("au_done"), sem("o_ready")
            squared, ms_ready, ms_root = sem("o_squared"), sem("ms_ready"), sem("ms_root")
            scaled, on_ready = sem("o_scaled"), sem("on_ready")
            o_turned, ot_kept, wo_done, y_kept = sem("o_turned"), sem("ot_kept"), sem("wo_done"), sem("y_kept")
            o = sb("o", [P, GROUPS, G, P])
            ms = sb("ms", [P, GROUPS, G * HH])
            done_with = n_t[:].rearrange("p n h i -> p (n h i)")
            osq = done_with[:, 0:NCH * P].rearrange("p (g f) -> p g f", g=GROUPS)
            o_t = done_with[:, NCH * P:].rearrange("p (g f) -> p g f", g=GROUPS)
            y = w_t[:].rearrange("p n q i -> p (n q i)").rearrange("p (t d) -> p t d", t=NT)

            def whole(g):
                return o[:, g].rearrange("p q f -> p (q f)")

            def by_head(ap):
                return ap.rearrange("p (h e) -> p h e", e=DK)

            with nc.Block() as block:

                @block.tensor
                def _(pe):
                    def read_out(g):
                        for h in range(HH):
                            for i in range(GROUP):
                                n = g * GROUP + i
                                out = ps[i * CH:(i + 1) * CH, GROUPS + g, :].rearrange("p (q f) -> p q f", q=G)
                                last = nc.tensor.matmul(out[:, :, h * DK:(h + 1) * DK], qk_t[:, n, h, :],
                                                        u_diagonal(n)[:, h], start=True, stop=True,
                                                        skip_group_check=True)
                        last.then_inc(au_done, 1)

                    def turn(g):
                        pe.wait_ge(on_ready, g + 1)
                        for q in range(G):
                            last = nc.tensor.transpose(ps[:, g, q * P:(q + 1) * P], o[:, g, q], ident[:])
                        last.then_inc(o_turned, 1)

                    def project(g):
                        pe.wait_ge(ot_kept, g + 1)
                        for b in range(B):
                            for c in range(C):
                                q = C * b + c
                                last = nc.tensor.matmul(ps[:, GROUPS + g, b * D:(b + 1) * D],
                                                        o_t[:, g, q * P:(q + 1) * P], core.w_o[:, c, :],
                                                        start=c == 0, stop=c == C - 1)
                        last.then_inc(wo_done, 1)

                    for g in range(GROUPS):
                        read_out(g)
                    pe.wait_ge(qs_kept, GROUPS)
                    turn(0)
                    for g in range(GROUPS):
                        if g + 1 < GROUPS:
                            turn(g + 1)
                        project(g)

                @block.scalar
                def _(act):
                    for g in range(GROUPS):
                        nc.scalar.copy(o[:, g].rearrange("p q (a f) -> p q a f", a=HPAIRS),
                                       ps[:, 0:HPAIRS, g * P:(g + 1) * P]
                                       .rearrange("p a (q f) -> p q a f", q=G)).then_inc(qs_kept, 1)

                    def root(g):
                        act.wait_ge(ms_ready, g + 1)
                        nc.scalar.activation(ms[:, g], ms[:, g], ACT.Sqrt, scale=1.0 / DK, bias=core.ln_eps[:]) \
                            .then_inc(ms_root, 1)

                    def keep_turned(g):
                        act.wait_ge(o_turned, g + 1)
                        nc.scalar.copy(o_t[:, g], ps[:, g, :]).then_inc(ot_kept, 1)

                    def keep_y(g):
                        act.wait_ge(wo_done, g + 1)
                        nc.scalar.copy(y.rearrange("p (b t) d -> p b t d", b=B)[:, :, g],
                                       ps[:, GROUPS + g, :].rearrange("p (b d) -> p b d", b=B)).then_inc(y_kept, 1)

                    for g in range(GROUPS + 2):
                        if g < GROUPS:
                            root(g)
                        if 1 <= g <= GROUPS:
                            keep_turned(g - 1)
                        if g >= 2:
                            keep_y(g - 2)
                    norm.on_act(act, core.ln_eps[:])

                @block.gpsimd
                def _(pool):
                    for g in range(GROUPS):
                        pool.wait_ge(o_ready, g + 1)
                        nc.gpsimd.tensor_tensor(osq[:, g], whole(g), whole(g), ALU.mult).then_inc(squared, 1)
                        pool.wait_ge(squared, g + 1)
                        nc.gpsimd.tensor_tensor(by_head(whole(g)), by_head(whole(g)),
                                                core.onorm[:].unsqueeze(1).to_broadcast([P, G * HH, DK]),
                                                ALU.mult).then_inc(scaled, 1)

                @block.vector
                def _(dve):
                    V = nc.vector
                    link = chain(dve, sem("dve_order"), core.dve_count)

                    def scale(g):
                        dve.wait_ge(ms_root, g + 1)
                        link(V.reciprocal(ms[:, g], ms[:, g]))
                        dve.wait_ge(scaled, g + 1)
                        V.tensor_tensor(by_head(whole(g)), by_head(whole(g)),
                                        ms[:, g].unsqueeze(2).to_broadcast([P, G * HH, DK]),
                                        ALU.mult).then_inc(on_ready, 1)

                    def add(g):
                        dve.wait_ge(au_done, g + 1)
                        dve.wait_ge(qs_kept, g + 1)
                        V.tensor_tensor(whole(g), whole(g), ps[:, GROUPS + g, :], ALU.add).then_inc(o_ready, 1)

                    add(0)
                    for g in range(GROUPS):
                        if g + 1 < GROUPS:
                            add(g + 1)
                        dve.wait_ge(squared, g + 1)
                        V.tensor_reduce(ms[:, g], by_head(osq[:, g]), AX_X, ALU.add).then_inc(ms_ready, 1)
                        scale(g)
                    link(norm.on_dve(dve, link, y, y, order=[b * TB + g for g in range(GROUPS) for b in range(B)],
                                     arrived=lambda t: dve.wait_ge(y_kept, t % TB + 1)))
                    link(V.tensor_tensor(x[:], x[:], y, ALU.add))


def expert_mixture(core, ins, out):
    nc, sem, norm, x, ps, ident = core.nc, core.sem, core.norm, core.x, core.ps, core.ident
    E = 8
    SH = core.SH
    HI, LO = 0, 1
    PRODUCTS = ((HI, HI), (HI, LO), (LO, HI))
    HID = SH + E
    with ExitStack() as own:
        def sb(name, shape, dt=F32):
            return own.enter_context(nc.sbuf_tensor(name, shape, dt))

        xm = sb("xm", [P, NT, D])
        gate_r = sb("gate_r", [P, 2, C, HID, P], F32R)
        up_r = sb("up_r", [P, 2, C, HID, P], F32R)
        down_r = sb("down_r", [P, 2, HID, D], F32R)
        xm_r = sb("xm_r", [P, 2, C, N], F32R)
        router_t = sb("router_t", [P, C, E])
        scores = sb("scores", [P, NT, E])
        select = sb("select", [P, NT, E])
        best = sb("best8", [P, NT, 8])
        where = sb("where", [P, NT, 8], U32)
        where_f = sb("where_f", [P, NT, 8])
        first = sb("first", [P, NT, E])
        second = sb("second", [P, NT, E])
        total = sb("score_sum", [P, NT])
        hidden = core.third[:, 0:4 * T].rearrange("p (a t) -> p a t", a=4)
        xm_t = core.third[:, 0:4 * T].rearrange("p (c n) -> p c n", c=C)
        gated = core.third[:, 4 * T:6 * T].rearrange("p (a t) -> p a t", a=2)
        share = core.stored[:, 0:E * N].rearrange("p (e n) -> p e n", e=E)
        share_t = xm[:].rearrange("p t d -> p (t d)")[0:E, 0:N]
        hidden_r = sb("hidden_r", [P, 2, 2, T], F32R)
        y = xm

        xm_ready, xm_turned, xm_kept = sem("xm_ready"), sem("xm_turned"), sem("xm_kept")
        turned, kept_act, kept_dve = sem("ffn_w_turned"), sem("ffn_w_kept"), sem("ffn_w_kept_dve")
        router_turned, router_kept = sem("router_turned"), sem("router_kept")
        scores_done, scores_kept = sem("scores_done"), sem("scores_kept")
        share_ready, share_turned, share_t_kept = sem("share_ready"), sem("share_turned"), sem("share_t_kept")
        share_out = sem("share_out")
        share_in = (sem("share_in_first"), sem("share_in_second"))
        up_done, silu_ready, prod_ready, hidden_ready = (sem("up_done"), sem("silu_ready"), sem("prod_ready"),
                                                         sem("hidden_ready"))
        xm_hi_kept, xm_lo_kept, hidden_hi, hidden_lo = (sem("xm_hi_kept"), sem("xm_lo_kept"), sem("hidden_hi"),
                                                        sem("hidden_lo"))
        down_done, y_ready = sem("down_done"), sem("y_ready")
        normed, x_ready, stored = sem("y_normed"), sem("x_ready"), sem("x_stored")

        def flat(ap):
            return ap.rearrange("p a b -> p (a b)")

        def quad(k):
            a0, groups = 4 * k, []
            for which, dst in enumerate((gate_r, up_r)):
                for c in range(C):
                    cols = slice(c * P, (c + 1) * P)
                    if a0 < SH:
                        tiles_ = [(core.sw1, core.sw2)[which][:, a, cols] for a in range(a0, a0 + 4)]
                    else:
                        tiles_ = [core.w12[:, 2 * (a - SH) + which, cols] for a in range(a0, a0 + 4)]
                    groups.append((tiles_, [flat(dst[:, part, c, a0:a0 + 4, :]) for part in (HI, LO)]))
            return groups

        def pair(j):
            a0 = 2 * j
            if a0 < SH:
                tiles_ = [core.sw3[:, c, a * P:(a + 1) * P] for a in (a0, a0 + 1) for c in range(C)]
            else:
                tiles_ = [core.w3[:, a - SH, c, :] for a in (a0, a0 + 1) for c in range(C)]
            return [(tiles_, [flat(down_r[:, part, a0:a0 + 2, :]) for part in (HI, LO)])]

        FIRST, PER_STEP = 4, 2
        quads = [quad(k) for k in range(HID // 4)]
        pairs = [pair(j) for j in range(HID // 2)]
        groups = list(quads[0])
        for k in range(1, HID // 4):
            groups += pairs[2 * k - 2] + quads[k] + pairs[2 * k - 1]
        groups += pairs[6] + pairs[7]
        TURN_STEPS = (len(groups) - FIRST) // PER_STEP
        STEPS = B * HID
        LAG = 3

        def kept_with(group):
            return [g is group for g in groups].index(True) + 1

        quad_kept = [kept_with(q[-1]) for q in quads]
        pair_kept = [kept_with(p[0]) for p in pairs]
        SCORE_STEP, CHOOSE_STEP, WEIGH_STEP, SHARE_STEP = 0, 1, 2, 4
        BEFORE_SHARES = FIRST + SHARE_STEP * PER_STEP

        def bank_of(n):
            return 4 + n if n < FIRST else 2 + n % 2

        def groups_of(step):
            first = FIRST + step * PER_STEP
            return range(first, first + PER_STEP) if step < TURN_STEPS else ()

        with nc.Block() as block:

            @block.tensor
            def _(pe):
                pe.wait_ge(core.f_in, core.f_in_total)
                def turn(n):
                    if n >= FIRST + 2:
                        pe.wait_ge(kept_dve, n - 1)
                    if n == BEFORE_SHARES:
                        pe.wait_ge(share_t_kept, 1)
                    for i, stored in enumerate(groups[n][0]):
                        last = nc.tensor.transpose(ps[:, bank_of(n), i * P:(i + 1) * P], stored, ident[:])
                    last.then_inc(turned, 1)

                for n in range(FIRST):
                    turn(n)
                for c in range(C):
                    last = nc.tensor.transpose(ps[:, 3, c * E:(c + 1) * E], core.router[:, c * P:(c + 1) * P],
                                               ident[0:E, 0:E])
                last.then_inc(router_turned, 1)
                pe.wait_ge(xm_ready, 1)
                pe.wait_ge(router_kept, 1)
                for b in range(B):
                    for c in range(C):
                        for t in range(TB):
                            last = nc.tensor.transpose(ps[:, 2 * b + c, t * P:(t + 1) * P],
                                                       xm[:, b * TB + t, c * P:(c + 1) * P], ident[:])
                        last.then_inc(xm_turned, 1)

                def score():
                    pe.wait_ge(xm_kept, B * C)
                    for t in range(NT):
                        for c in range(C):
                            last = nc.tensor.matmul(ps[:, 0, t * E:(t + 1) * E], xm_t[:, c, t * P:(t + 1) * P],
                                                    router_t[:, c, :], start=c == 0, stop=c == C - 1)
                    last.then_inc(scores_done, 1)

                def turn_shares():
                    pe.wait_ge(share_ready, 1)
                    pe.wait_ge(kept_dve, BEFORE_SHARES)
                    for t in range(NT):
                        last = nc.tensor.transpose(ps[0:E, 2 + t // TB, (t % TB) * P:(t % TB + 1) * P],
                                                   first[:, t, :], ident[:])
                    last.then_inc(share_turned, 1)

                def up(n):
                    b, a = n // HID, n % HID
                    bank = 4 + 2 * (n % 2)
                    pe.wait_ge(kept_dve, quad_kept[a // 4])
                    pe.wait_ge(xm_lo_kept, C * (b + 1))
                    if n >= 2:
                        pe.wait_ge(prod_ready, n - 1)
                    for which, w in enumerate((gate_r, up_r)):
                        for i, (c, wp, xp) in enumerate((c, *parts) for c in range(C) for parts in PRODUCTS):
                            last = nc.tensor.matmul(ps[:, bank + which, :], w[:, wp, c, a, :],
                                                    xm_r[:, xp, c, b * T:(b + 1) * T], start=i == 0,
                                                    stop=i == C * len(PRODUCTS) - 1)
                        last.then_inc(up_done, 1)

                def down(n):
                    b, a = n // HID, n % HID
                    pe.wait_ge(hidden_lo, n + 1)
                    pe.wait_ge(kept_dve, pair_kept[a // 2])
                    if n == 0:
                        pe.wait_ge(scores_kept, 1)
                    if a == 0 and b:
                        pe.wait_ge(y_ready, b * TB)
                    for t in range(TB):
                        for i, (wp, hp) in enumerate(PRODUCTS):
                            last = nc.tensor.matmul(ps[:, t // 2, t % 2 * D:(t % 2 + 1) * D],
                                                    hidden_r[:, n % 2, hp, t * P:(t + 1) * P],
                                                    down_r[:, wp, a, :], start=a == 0 and i == 0 and t % 2 == 0,
                                                    stop=a == HID - 1 and i == len(PRODUCTS) - 1,
                                                    skip_group_check=True)
                    last.then_inc(down_done, 1)

                for n in range(STEPS + LAG):
                    if n < STEPS:
                        up(n)
                    if n == SCORE_STEP:
                        score()
                    if n == SHARE_STEP:
                        turn_shares()
                    for k in groups_of(n):
                        turn(k)
                    if n >= LAG:
                        down(n - LAG)

            @block.scalar
            def _(act):
                a = nc.scalar.activation

                def high_weights(n):
                    act.wait_ge(turned, n + 1)
                    nc.scalar.copy(groups[n][1][HI], ps[:, bank_of(n), :]).then_inc(kept_act, 1)

                high_weights(0)
                high_weights(1)
                norm.on_act(act, core.ln_eps[:])
                for n in range(2, FIRST):
                    high_weights(n)
                act.wait_ge(router_turned, 1)
                nc.scalar.copy(router_t[:].rearrange("p c e -> p (c e)"), ps[:, 3, 0:C * E]).then_inc(router_kept, 1)
                for n in range(B * C):
                    act.wait_ge(xm_turned, n + 1)
                    own = (n % C, slice((n // C) * T, (n // C + 1) * T))
                    nc.scalar.copy(xm_r[:, HI, own[0], own[1]], ps[:, n, :]).then_inc(xm_hi_kept, 1)
                for n in range(B * C):
                    own = (n % C, slice((n // C) * T, (n // C + 1) * T))
                    act.wait_ge(xm_lo_kept, n + 1)
                    nc.scalar.copy(xm_t[:, own[0], own[1]], ps[:, n, :]).then_inc(xm_kept, 1)

                def silu(n):
                    act.wait_ge(up_done, 2 * n + 1)
                    if n >= 2:
                        act.wait_ge(prod_ready, n - 1)
                    a(gated[:, n % 2, :], ps[:, 4 + 2 * (n % 2), :], ACT.Silu).then_inc(silu_ready, 1)

                def high(n):
                    b, i = n // HID, n % HID
                    if i < SH:
                        act.wait_ge(prod_ready, n + 1)
                    else:
                        act.wait_ge(hidden_ready, b * E + i - SH + 1)
                    if n >= 2:
                        act.wait_ge(down_done, n - 1)
                    nc.scalar.copy(hidden_r[:, n % 2, HI, :], hidden[:, n % 4, :]).then_inc(hidden_hi, 1)

                for n in range(STEPS + 1):
                    if n < STEPS:
                        silu(n)
                    if n == SCORE_STEP:
                        act.wait_ge(scores_done, 1)
                        a(scores[:].rearrange("p t e -> p (t e)"), ps[:, 0, 0:NT * E], ACT.Sigmoid) \
                            .then_inc(scores_kept, 1)
                    for k in groups_of(n):
                        high_weights(k)
                    if n >= 1:
                        high(n - 1)
                norm.on_act(act, core.ln_eps[:])

            @block.sync
            def _(sp):
                sp.wait_ge(share_t_kept, 1)
                sp.dma_start(core.share_dram, share_t).then_inc(share_out, 16)
                sp.wait_ge(share_out, 16)
                for part in range(2):
                    sp.wait_ge(kept_dve, quad_kept[2 * part + 1])
                    for e in range(4 * part, 4 * part + 4):
                        sp.dma_start(share[:, e, :], core.share_dram[e].partition_broadcast(P)) \
                            .then_inc(share_in[part], 16)
                for t in range(0, NT, 2):
                    sp.wait_ge(x_ready, t // 2 + 1)
                    sp.dma_start(tiles(out.rearrange("b t d -> (b t) d"))[:, t:t + 2, :], x[:, t:t + 2]) \
                        .then_inc(stored, 16)
                sp.wait_ge(stored, 16 * (NT // 2))

            @block.gpsimd
            def _(pool):
                for n in range(STEPS - 1):
                    b, a = n // HID, n % HID
                    if a >= SH:
                        pool.wait_ge(share_in[(a - SH) // 4], 16 * 4)
                        pool.wait_ge(prod_ready, n + 1)
                        nc.gpsimd.tensor_tensor(hidden[:, n % 4, :], hidden[:, n % 4, :],
                                                share[:, a - SH, b * T:(b + 1) * T], ALU.mult) \
                            .then_inc(hidden_ready, 1)
                    pool.wait_ge(hidden_hi, n + 1)
                    if n >= 2:
                        pool.wait_ge(down_done, n - 1)
                    nc.gpsimd.tensor_tensor(hidden_r[:, n % 2, LO, :], hidden[:, n % 4, :],
                                            hidden_r[:, n % 2, HI, :], ALU.subtract).then_inc(hidden_lo, 1)

            @block.vector
            def _(dve):
                V = nc.vector
                link = chain(dve, sem("dve_order"), core.dve_count)
                norm.on_dve(dve, link, x, xm).then_inc(xm_ready, 1)
                def low_weights(n):
                    dve.wait_ge(kept_act, n + 1)
                    V.tensor_tensor(groups[n][1][LO], ps[:, bank_of(n), :], groups[n][1][HI], ALU.subtract) \
                        .then_inc(kept_dve, 1)

                for n in range(FIRST):
                    low_weights(n)
                for n in range(B * C):
                    own = (n % C, slice((n // C) * T, (n // C + 1) * T))
                    dve.wait_ge(xm_hi_kept, n + 1)
                    V.tensor_tensor(xm_r[:, LO, own[0], own[1]], ps[:, n, :], xm_r[:, HI, own[0], own[1]],
                                    ALU.subtract).then_inc(xm_lo_kept, 1)

                def choose():
                    dve.wait_ge(scores_kept, 1)
                    link(V.tensor_tensor(select[:], scores[:], core.expert_bias[:].unsqueeze(1).to_broadcast([P, NT, E]),
                                         ALU.add))
                    for t in range(NT):
                        last = V.max(best[:, t, :], select[:, t, :])
                    link(last)
                    for t in range(NT):
                        last = V.max_index(where[:, t, :], best[:, t, :], select[:, t, :])
                    link(last)

                def weigh():
                    link(V.tensor_copy(where_f[:], where[:]))
                    number = core.numbers[:].unsqueeze(1).to_broadcast([P, NT, E])
                    V.tensor_tensor(first[:], number, where_f[:, :, 0:1].to_broadcast([P, NT, E]), ALU.is_equal)
                    link(V.tensor_tensor(second[:], number, where_f[:, :, 1:2].to_broadcast([P, NT, E]), ALU.is_equal))
                    link(V.tensor_tensor(first[:], first[:], second[:], ALU.add))
                    link(V.tensor_tensor(first[:], first[:], scores[:], ALU.mult))
                    link(V.tensor_reduce(total[:], first[:], AX_X, ALU.add))
                    link(V.tensor_scalar(total[:], total[:], 1e-9, None, ALU.add))
                    link(V.reciprocal(total[:], total[:]))
                    V.tensor_tensor(first[:], first[:], total[:].unsqueeze(2).to_broadcast([P, NT, E]), ALU.mult) \
                        .then_inc(share_ready, 1)

                def keep_y(b):
                    dve.wait_ge(down_done, (b + 1) * HID)
                    dve.wait_ge(share_out, 16)
                    for t in range(TB):
                        V.tensor_copy(y[:, b * TB + t, :], ps[:, t // 2, t % 2 * D:(t % 2 + 1) * D]) \
                            .then_inc(y_ready, 1)

                dve.wait_ge(scores_done, 1)
                dve.wait_ge(xm_lo_kept, B * C)
                for n in range(STEPS):
                    if n >= 4:
                        dve.wait_ge(down_done, n - 3)
                    dve.wait_ge(silu_ready, n + 1)
                    dve.wait_ge(up_done, 2 * n + 2)
                    V.tensor_tensor(hidden[:, n % 4, :], gated[:, n % 2, :], ps[:, 4 + 2 * (n % 2) + 1, :], ALU.mult) \
                        .then_inc(prod_ready, 1)
                    if n == SHARE_STEP:
                        dve.wait_ge(share_turned, 1)
                        V.tensor_copy(share_t, ps[0:E, 2:4, :].rearrange("p a b -> p (a b)")) \
                            .then_inc(share_t_kept, 1)
                    for k in groups_of(n):
                        low_weights(k)
                    if n == CHOOSE_STEP:
                        choose()
                    if n == WEIGH_STEP:
                        weigh()
                    if n == HID + LAG - 2:
                        keep_y(0)
                    if n == HID + LAG:
                        dve.wait_ge(y_ready, TB)
                        for t in range(TB):
                            norm.tile_stats(y, t)
                last = STEPS - 1
                dve.wait_ge(share_in[1], 16 * 4)
                dve.wait_ge(prod_ready, last + 1)
                dve.wait_ge(hidden_ready, B * E - 1)
                V.tensor_tensor(hidden[:, last % 4, :], hidden[:, last % 4, :], share[:, E - 1, T:], ALU.mult) \
                    .then_inc(hidden_ready, 1)
                dve.wait_ge(hidden_hi, last + 1)
                dve.wait_ge(hidden_lo, last)
                dve.wait_ge(down_done, last - 1)
                V.tensor_tensor(hidden_r[:, last % 2, LO, :], hidden[:, last % 4, :], hidden_r[:, last % 2, HI, :],
                                ALU.subtract).then_inc(hidden_lo, 1)
                keep_y(1)
                dve.wait_ge(y_ready, NT)
                norm.on_dve(dve, link, y, y, ready=normed, order=range(TB, NT))
                for t in range(0, NT, 2):
                    dve.wait_ge(normed, t + 2)
                    V.tensor_tensor(x[:, t:t + 2], x[:, t:t + 2], y[:, t:t + 2], ALU.add).then_inc(x_ready, 1)


def sandwich(nc, ins, out):
    with ExitStack() as ctx:
        core = Core(nc, ctx)
        core.x = core.sb("x", [P, NT, D])
        core.ident = core.sb("ident", [P, P])
        core.ones = core.sb("ones", [P, P])
        core.ln_eps = core.sb("ln_eps", [P, 1])
        core.l2_eps = core.sb("l2_eps", [P, 1])
        core.ps = ctx.enter_context(nc.psum_tensor("ps", [P, 8, 512], F32))
        core.norm = Norm(core)
        core.dve_count = [0]
        core.weights(ins)
        time_mixing(core, ins)
        expert_choice(core, ins)
        delta_attention(core, ins)
        expert_mixture(core, ins, out)


_INS = ["L0_attn_hidden_state", "L0_attn_ln_w", "L0_attn_ln_b", "L0_attn_Wk", "L0_attn_Wv", "L0_attn_Wr",
        "L0_attn_Wo", "L0_attn_mix_k", "L0_attn_mix_v", "L0_attn_mix_r", "L0_attn_time_decay",
        "L0_attn_current_token_weight", "L0_ffn_router_w", "L0_ffn_router_b", "L0_ffn_expert_w",
        "L0_ffn_expert_b", "L1_attn_Wq", "L1_attn_Wk", "L1_attn_Wv", "L1_attn_Wb", "L1_attn_Wo",
        "L1_attn_conv_q", "L1_attn_conv_k", "L1_attn_conv_v", "L1_attn_onorm_w", "L1_ffn_w12", "L1_ffn_w3",
        "L1_ffn_router_w", "L1_ffn_expert_bias", "L1_ffn_sw1", "L1_ffn_sw2", "L1_ffn_sw3"]


def kernel(**inputs):
    import numpy as _np
    import concourse.bacc as _bacc
    from concourse import mybir as _mybir
    from concourse.bass_utils import run_bass_kernel_spmd as _run

    nc = _bacc.Bacc("TRN2", target_bir_lowering=False, num_devices=1)
    arrays, ins = {}, {}
    for name in _INS:
        a = _np.ascontiguousarray(inputs[name])
        arrays[f"in_{name}_dram"] = a
        ins[name] = nc.dram_tensor(f"in_{name}_dram", a.shape, _mybir.dt.from_np(a.dtype),
                                   kind="ExternalInput").ap()
    out = nc.dram_tensor("out_0_dram", (B, T, D), F32, kind="ExternalOutput").ap()
    sandwich(nc, ins, out)
    r = _run(nc, [arrays], core_ids=[0])
    return r.results[0]["out_0_dram"]
```
